# Optimizing a Trainium2 kernel written in Bass

```python
import numpy as np
import jax
import jax.numpy as jnp

def _softmax(x, axis=-1):
    return jax.nn.softmax(x, axis=axis)

def _gelu(x):
    return jax.nn.gelu(x, approximate=True)

def _silu(x):
    return jax.nn.silu(x)

def _sigmoid(x):
    return jax.nn.sigmoid(x)

def _layernorm(x, axis=-1, eps=1e-05):
    m = jnp.mean(x, axis=axis, keepdims=True)
    v = jnp.var(x, axis=axis, keepdims=True)
    return (x - m) / jnp.sqrt(v + eps)

def _scatter_add(tgt, idx, src, axis=0):
    return tgt.at[idx].add(src)

def _segment_sum(src, seg, n):
    return jax.ops.segment_sum(src, seg, n)
kernel_name = 'mk_prb_d1_jaxref_r4_6372e9'

def setup_inputs(seed: int=0):
    np.random.seed(seed)
    _w = jnp.asarray

    def _L0_attn_setup():
        import jax, jax.numpy as jnp
        import numpy as np
        EMBED_DIM = 256
        NUM_HEADS = 16
        HEAD_DIM = EMBED_DIM // NUM_HEADS
        NUM_FEATS = 64
        YAT_EPS = 0.1
        BATCH = 4
        SEQ = 1024

        def _spherical_features(x, projection):
            x_norm = x / (jnp.linalg.norm(x, axis=-1, keepdims=True) + 1e-08)
            proj = jnp.einsum('bhsd,hfd->bhsf', x_norm, projection)
            return jax.nn.relu(proj) + YAT_EPS
        key = jax.random.key(seed)
        ks = jax.random.split(key, 6)
        s = 1.0 / np.sqrt(EMBED_DIM)
        return {'x': jax.random.normal(ks[0], (BATCH, SEQ, EMBED_DIM), jnp.float32), 'Wq': jax.random.normal(ks[1], (EMBED_DIM, EMBED_DIM), jnp.float32) * s, 'bq': jnp.zeros((EMBED_DIM,), jnp.float32), 'Wk': jax.random.normal(ks[2], (EMBED_DIM, EMBED_DIM), jnp.float32) * s, 'bk': jnp.zeros((EMBED_DIM,), jnp.float32), 'Wv': jax.random.normal(ks[3], (EMBED_DIM, EMBED_DIM), jnp.float32) * s, 'bv': jnp.zeros((EMBED_DIM,), jnp.float32), 'Wo': jax.random.normal(ks[4], (EMBED_DIM, EMBED_DIM), jnp.float32) * s, 'bo': jnp.zeros((EMBED_DIM,), jnp.float32), 'projection': jax.random.normal(ks[5], (NUM_HEADS, NUM_FEATS, HEAD_DIM), jnp.float32)}
    _L0_attn_in = _L0_attn_setup()

    def _L0_ffn_setup():
        import jax, jax.numpy as jnp
        import numpy as np
        NUM_EXPERTS = 8
        TOP_K = 2
        CAP_RATIO = 1.25
        INIT_STD = 0.02
        key = jax.random.key(seed)
        k1, k2, k3, k4 = jax.random.split(key, 4)
        B, T, H, F = (4, 512, 256, 1024)
        x = jax.random.normal(k1, (B, T, H), jnp.float32)
        router_w = jax.random.normal(k2, (NUM_EXPERTS, H), jnp.float32) * INIT_STD
        w1 = jax.random.normal(k3, (NUM_EXPERTS, H, F), jnp.float32) * INIT_STD
        w2 = jax.random.normal(k4, (NUM_EXPERTS, F, H), jnp.float32) * INIT_STD
        return {'x': x, 'router_w': router_w, 'w1': w1, 'w2': w2}
    _L0_ffn_in = _L0_ffn_setup()
    _d = {'L0_attn_x': _L0_attn_in['x'], 'L0_attn_Wq': _L0_attn_in['Wq'], 'L0_attn_bq': _L0_attn_in['bq'], 'L0_attn_Wk': _L0_attn_in['Wk'], 'L0_attn_bk': _L0_attn_in['bk'], 'L0_attn_Wv': _L0_attn_in['Wv'], 'L0_attn_bv': _L0_attn_in['bv'], 'L0_attn_Wo': _L0_attn_in['Wo'], 'L0_attn_bo': _L0_attn_in['bo'], 'L0_attn_projection': _L0_attn_in['projection'], 'L0_ffn_router_w': _L0_ffn_in['router_w'], 'L0_ffn_w1': _L0_ffn_in['w1'], 'L0_ffn_w2': _L0_ffn_in['w2']}
    _x0 = _d['L0_attn_x']
    _d['L0_attn_x'] = jax.random.normal(jax.random.fold_in(jax.random.key(seed), 1), (8, 1024, 256), dtype=_x0.dtype)
    del _x0
    return _d

def reference(L0_attn_x, L0_attn_Wq, L0_attn_bq, L0_attn_Wk, L0_attn_bk, L0_attn_Wv, L0_attn_bv, L0_attn_Wo, L0_attn_bo, L0_attn_projection, L0_ffn_router_w, L0_ffn_w1, L0_ffn_w2):

    def _L0_attn_ref(x, Wq, bq, Wk, bk, Wv, bv, Wo, bo, projection):
        import jax, jax.numpy as jnp
        import numpy as np
        EMBED_DIM = 256
        NUM_HEADS = 16
        HEAD_DIM = EMBED_DIM // NUM_HEADS
        NUM_FEATS = 64
        YAT_EPS = 0.1
        BATCH = 4
        SEQ = 1024

        def _spherical_features(x, projection):
            x_norm = x / (jnp.linalg.norm(x, axis=-1, keepdims=True) + 1e-08)
            proj = jnp.einsum('bhsd,hfd->bhsf', x_norm, projection)
            return jax.nn.relu(proj) + YAT_EPS
        b, s, _ = x.shape

        def heads(t):
            return jnp.transpose(t.reshape(b, s, NUM_HEADS, HEAD_DIM), (0, 2, 1, 3))
        Q = heads(x @ Wq + bq)
        K = heads(x @ Wk + bk)
        V = heads(x @ Wv + bv)
        Qp = _spherical_features(Q, projection)
        Kp = _spherical_features(K, projection)
        KV = jnp.einsum('bhsf,bhsd->bhfd', Kp, V)
        QKV = jnp.einsum('bhsf,bhfd->bhsd', Qp, KV)
        K_sum = jnp.sum(Kp, axis=2)
        normalizer = jnp.einsum('bhsf,bhf->bhs', Qp, K_sum)[..., None]
        normalizer = jnp.maximum(normalizer, 1e-06)
        out = QKV / normalizer
        out = jnp.transpose(out, (0, 2, 1, 3)).reshape(b, s, EMBED_DIM)
        return out @ Wo + bo

    def _L0_ffn_ref(x, router_w, w1, w2):
        import jax, jax.numpy as jnp
        import numpy as np
        NUM_EXPERTS = 8
        TOP_K = 2
        CAP_RATIO = 1.25
        INIT_STD = 0.02
        B, T, H = x.shape
        E, K = (NUM_EXPERTS, TOP_K)
        xf = x.reshape(-1, H)
        N = xf.shape[0]
        P = N * K
        capacity = int(CAP_RATio * N * K / E) + 1 if False else int(CAP_RATIO * N * K / E) + 1
        logits = xf @ router_w.T
        probs = jax.nn.softmax(logits, axis=-1)
        k_probs, k_idx = jax.lax.top_k(probs, K)
        k_probs = k_probs / jnp.sum(k_probs, axis=-1, keepdims=True)
        flat_e = k_idx.reshape(-1)
        onehot = jax.nn.one_hot(flat_e, E, dtype=jnp.int32)
        rank = jnp.take_along_axis(jnp.cumsum(onehot, axis=0) - 1, flat_e[:, None], axis=1)[:, 0]
        keep = rank < capacity
        slot = jnp.minimum(rank, capacity - 1)
        token_id = jnp.arange(P) // K
        dispatched = jnp.where(keep[:, None], xf[token_id], 0.0)
        buf = jnp.zeros((E, capacity, H), x.dtype).at[flat_e, slot].add(dispatched)
        h = jax.nn.silu(jnp.einsum('ech,ehf->ecf', buf, w1))
        out_buf = jnp.einsum('ecf,efh->ech', h, w2)
        pair_out = out_buf[flat_e, slot] * keep[:, None].astype(x.dtype)
        combined = jnp.sum(pair_out.reshape(N, K, H) * k_probs[..., None], axis=1)
        return combined.reshape(B, T, H) + x
    x = L0_attn_x
    xn = _layernorm(x, axis=-1)
    x = x + _L0_attn_ref(xn, L0_attn_Wq, L0_attn_bq, L0_attn_Wk, L0_attn_bk, L0_attn_Wv, L0_attn_bv, L0_attn_Wo, L0_attn_bo, L0_attn_projection) + _L0_ffn_ref(xn, L0_ffn_router_w, L0_ffn_w1, L0_ffn_w2)
    return x

_drawn_inputs = setup_inputs


def setup_inputs(seed=0):
    import zlib

    import numpy as np

    out = dict(_drawn_inputs(seed))
    spreads = {'L0_attn_bq': (0.0, 0.8),
     'L0_attn_bk': (0.0, 0.8),
     'L0_attn_bv': (0.0, 0.1),
     'L0_attn_bo': (0.0, 0.1)}
    factors = {'L0_attn_Wq': 5.889, 'L0_attn_Wk': 5.289, 'L0_attn_Wv': 2.89, 'L0_attn_projection': 8.0}
    for name, (base, spread) in spreads.items():
        noise = np.random.default_rng([zlib.crc32(name.encode()), seed]).standard_normal(out[name].shape)
        drawn = base * np.exp(spread * noise) if base else spread * noise
        out[name] = jnp.asarray(drawn.astype(out[name].dtype))
    for name, factor in factors.items():
        out[name] = (out[name] * factor).astype(out[name].dtype)
    return out
```

```python
from contextlib import ExitStack

import concourse.bass as bass
from concourse import mybir

P = 128
B, S, D = 8, 1024, 256
H, HD, F = 16, 16, 64
E, TOPK, FF = 8, 2, 1024
N = B * S
CAP = int(1.25 * N * TOPK / E) + 1
NT = S // P
HT = NT // 2
HS = HT * P
KC = D // P
PAIRS = H // 2
KVW = 2 * (HD + 1)
WCOLS = 3 * D + E

TS = 256
MT = (N * TOPK) // TS + E
RROWS = -(-CAP // TS) * TS
TRASH = E * RROWS
DUMP = TRASH + TS
META_ROWS = DUMP + N * TOPK
GRP = 4
NG = MT // GRP
assert MT % GRP == 0 and NG > 2

W_SCALE = 16.0
R_SCALE = 256.0
H_SCALE = 64.0
P_SCALE = 1.0 / 16.0
EPSF = 0.1 * P_SCALE
MAGIC = 1597463007.0

F32, F16, I32, U32 = mybir.dt.float32, mybir.dt.float16, mybir.dt.int32, mybir.dt.uint32
ALU = mybir.AluOpType
ACT = mybir.ActivationFunctionType
AX = mybir.AxisListType
PASSES = ((0, 0), (0, 1), (1, 0))

def prep(*names):
    return [("prep", n) for n in names]


def attn(*names):
    return [("attn", n) for n in names]


PREP = prep("xT0", "xT1", "v0", "v1", "nrm0", "v2", "nrmT0", "v3", "xT2", "xT3", "v4", "v5", "nrm1", "v6", "nrmT1", "v7")
TAIL = attn("rank", "vsum", "kvT", "cn", "ab0", "ab1", "ab2", "ab3", "oT0", "oT1", "ab4", "ab5", "ab6", "ab7",
            "out0", "out1", "oT2", "oT3", "out2", "out3")
BODY = TAIL[:8] + PREP[:2] + TAIL[8:16] + PREP[2:5] + TAIL[16:18] + PREP[5:8] + TAIL[18:] + PREP[8:]
PLAN = {"first": PREP, "body": BODY, "tail": TAIL}
PER = {"prep": len(PREP), "attn": len(TAIL)}
NTH = {use: n + 1 for part in (PREP, TAIL) for n, use in enumerate(part)}
SMALL_BANKS = 3
BIG_BANKS = 4
assert len(BODY) % SMALL_BANKS == 0 and BODY[-3:] == PREP[-3:]
QK_USES, FEAT_USES, QF_USES = 2 * 4, 2 * NT + 2 * PAIRS, 2 * PAIRS


def small_use(phase, use, b):
    plan = PLAN[phase]
    n = plan.index(use)
    nth = n if phase == "first" else n + len(PREP)
    if n >= SMALL_BANKS:
        before = plan[n - SMALL_BANKS]
        gap = (before[0] == "prep") - (use[0] == "prep")
        return nth % SMALL_BANKS, before, b + gap
    if phase == "first":
        return nth % SMALL_BANKS, None, None
    return nth % SMALL_BANKS, PREP[n - SMALL_BANKS], b


class Chain:

    def __init__(self, sem, per):
        self.sem, self.per = sem, per

    def start(self, eng, b):
        self.eng, self.base, self.n = eng, b * self.per, 0

    def step(self, ins):
        self.n += 1
        ins.then_inc(self.sem, 1)

    def wait(self):
        self.eng.wait_ge(self.sem, self.base + self.n)

    def link(self, ins):
        self.step(ins)
        self.wait()

    def end(self):
        assert self.n == self.per, (self.n, self.per)


def moe_attention(nc, x, Wq, bq, Wk, bk, Wv, bv, Wo, bo, proj_t, router_t, w1, w2, out):
    xrows = x.rearrange("b s d -> (b s) d")
    orows = out.rearrange("b s d -> (b s) d")
    xs = nc.dram_tensor("xn_split", [N + P, 2 * D], F16, kind="Internal").ap()
    meta = nc.dram_tensor("slot_table", [META_ROWS, 2], I32, kind="Internal").ap()
    wsplit = nc.dram_tensor("experts_split", [E, P, 4, 2, 1024], F16, kind="Internal").ap()

    with ExitStack() as ctx:
        def sb(name, shape, dt):
            return ctx.enter_context(nc.sbuf_tensor(name, shape, dt))

        def sem(name):
            return ctx.enter_context(nc.semaphore(name))

        bank = [ctx.enter_context(nc.psum_tensor(f"bank{i}", [P, 512], F32)) for i in range(8)]
        small = [bank[0], bank[1], bank[6]]
        big = bank[2:6]
        kvbank = bank[7]

        w_hl = sb("w_hl", [P, 2, KC, WCOLS], F16)
        wo_hl = sb("wo_hl", [P, 2, KC, D], F16)
        p_hl = sb("p_hl", [P, 2, KC, 512], F16)
        ident16 = sb("ident16", [P, P], F16)
        ident32 = sb("ident32", [P, P], F32)
        tri = sb("tri", [P, P], F16)
        ones16 = sb("ones16", [P, P], F16)
        cfeat = sb("cfeat", [P, P], F32)
        hsel = sb("hsel", [P, 32], F32)
        iota_e = sb("iota_e", [P, E], F32)
        iota_i = sb("iota_i", [P, 256], I32)
        tok_f = sb("tok_f", [P, NT], F32)
        dump_f = sb("dump_f", [P, 2, NT], F32)
        bqk = sb("bqk", [P, 2, KC], F32)
        bv_b = sb("bv_b", [P, D], F32)
        bo_b = sb("bo_b", [P, D], F32)
        carry = sb("carry", [P, E], F32)
        mt = sb("mt", [P, GRP, 2, 2], I32)
        tab = sb("tab", [1, 2, MT], I32)
        xg = sb("xg", [P, GRP, 2, 2 * D], F16)
        AREA = 16384 + 166336
        EXPERT = 4 * 2 * 1024
        area = sb("area", [P, AREA // 4], F32)
        cursor = [EXPERT // 2]

        def view(shape, dt):
            n = 1
            for k in shape:
                n *= k
            words = n * (2 if dt == F16 else 4) // 4
            a = area[:, cursor[0]:cursor[0] + words]
            cursor[0] += words
            assert cursor[0] * 4 <= AREA, cursor[0] * 4
            if dt != F32:
                a = a.bitcast(dt)
            names = "abcd"[:len(shape)]
            if len(shape) > 1:
                a = a.rearrange(f"p ({' '.join(names)}) -> p {' '.join(names)}", **dict(zip(names, shape)))
            return a

        x_in = [view([HT, D], F32) for _ in range(2)]
        xn = view([HT, D], F32)
        xhl = [view([HT, 2, D], F16) for _ in range(2)]
        xT = [view([2 * KC, HS], F16) for _ in range(2)]
        q32 = [view([HS], F32) for _ in range(2)]
        q_hl = [view([KC, 2, HS], F16) for _ in range(2)]
        k_hl = [view([KC, 2, HS], F16) for _ in range(2)]
        sq = view([2, KC, HS], F32)
        v32 = view([NT, D], F32)
        vp = view([NT, H, 32], F32)
        vsum = view([H, HD + 1], F32)
        resid = view([NT, D], F32)
        rk = [view([KC, 512], F32) for _ in range(2)]
        rq = view([PAIRS, 2, HS], F16)
        kvt = view([256], F32)
        cs_b = view([H, HD + 1], F32)
        kvf = view([PAIRS, KVW], F32)
        kv_hl = view([2, PAIRS, KVW], F16)
        cn_b = view([H, HD + 1], F32)
        nT = view([HS], F32)
        nsq = view([HT, 4, 8], F32)
        ny = view([HT, 4, 8], F32)
        nu = view([HT, 4, 8], F32)
        norm = view([2, HT, 4, 8], F32)
        rn = view([HT, 2, 8], F32)
        nd = view([HT, H, HD + 1], F32)
        dn = view([HT, H], F32)
        o_hl = view([HT, 2, D], F16)
        oT = view([HT, 2 * KC, P], F16)
        osb = [view([2, D], F32) for _ in range(2)]
        w_raw = [view([1024], F32) for _ in range(2)]
        w_st = [view([2, 1024], F16) for _ in range(2)]
        bn = view([HT, 6], F32)
        mv = view([HT, 2], F32)
        va = view([HT], F32)
        vy = view([HT], F32)
        vu = view([HT], F32)
        lg = view([NT, E], F32)
        mx = view([NT, 8], F32)
        mi = view([NT, 8], U32)
        ix = view([2, NT], F32)
        oh = view([2, NT, E], F32)
        m16 = view([NT + 1, E], F16)
        rank = view([NT, E], F32)
        rsel = view([2, NT, E], F32)
        rpos = view([2, NT], F32)
        keep = view([2, NT], F32)
        slot = view([2, NT], F32)
        dl = view([NT], F32)
        eg = view([NT], F32)
        gate = view([2, NT], F32)
        slot_i = view([2, NT], I32)
        rec = view([2, NT, 2], I32)
        tb = v32.rearrange("p a b -> p (a b)")
        vtmp = view([4, D], F32)
        stage = rq.rearrange("p a b c -> p (a b c)").bitcast(F32)
        raw_w = stage[:, 0:KC * WCOLS].rearrange("p (k n) -> p k n", k=KC)
        raw_o = stage[:, KC * WCOLS:KC * (WCOLS + D)].rearrange("p (k n) -> p k n", k=KC)
        raw_p = stage[:, KC * (WCOLS + D):KC * (WCOLS + D + 512)].rearrange("p (m n) -> p m n", m=KC)
        clear = rk[0].rearrange("p a b -> p (a b)").bitcast(I32)[:, 0:2 * DUMP // P]
        zero_rows = rk[1].rearrange("p a b -> p (a b)").bitcast(F16)[:, 0:2 * D]
        tok_i = lg.bitcast(I32)[:, 0, 0:NT]
        dump_i = oh.bitcast(I32)[:, :, 0, :]

        we = area[:, 0:E * EXPERT // 2].bitcast(F16)
        cursor[0] = E * EXPERT // 2
        moe_xT = [view([2 * KC, TS], F16) for _ in range(2)]
        h32 = [view([2, TS], F32) for _ in range(4)]
        hT = [view([FF // P, 2, TS], F16) for _ in range(2)]
        y_sb = [view([2, D], F32) for _ in range(2)]

        weights_loaded = sem("weights_loaded")
        proj_zeroed = sem("proj_zeroed")
        proj_loaded = sem("proj_loaded")
        masks_made = sem("masks_made")
        consts_ready = sem("consts_ready")
        x_plus_xn = sem("x_plus_xn")
        zero_stored = sem("zero_stored")
        pool_prep = sem("pool_prep")
        pool_first = sem("pool_first")
        dve_first = sem("dve_first")
        slots_cleared = sem("slots_cleared")
        x_loaded = [sem(f"x_loaded{i}") for i in range(2)]
        xn_split = sem("xn_split")
        xl_split = sem("xl_split")
        x_summed = sem("x_summed")
        resid_ready = sem("resid_ready")
        xs_stored = [sem(f"xs_stored{i}") for i in range(2)]
        prep_filled, prep_read = sem("prep_filled"), sem("prep_read")
        attn_filled, attn_read = sem("attn_filled"), sem("attn_read")
        filled = {"prep": prep_filled, "attn": attn_filled}
        read = {"prep": prep_read, "attn": attn_read}
        qk_filled = sem("qk_filled")
        qk_read = sem("qk_read")
        qk_squared = sem("qk_squared")
        qk_split = sem("qk_split")
        vp_ready = sem("vp_ready")
        vsum_ready = sem("vsum_ready")
        feat_filled = sem("feat_filled")
        feat_relu = sem("feat_relu")
        qf_split = sem("qf_split")
        kv_tile_done = sem("kv_tile_done")
        kvt_copied = sem("kvt_copied")
        kvf_ready = sem("kvf_ready")
        kv_split = sem("kv_split")
        masks_ready = sem("masks_ready")
        gate_in, gate_exp = sem("gate_in"), sem("gate_exp")
        slots_ready = sem("slots_ready")
        table_cleared = sem("table_cleared")
        meta_stored = sem("meta_stored")
        o_split = sem("o_split")
        out_stored = [sem(f"out_stored{i}") for i in range(2)]
        w_in = [sem(f"w_in{i}") for i in range(2)]
        w_scaled, w_hi, w_lo = sem("w_scaled"), sem("w_hi"), sem("w_lo")
        w_out = [sem(f"w_out{i}") for i in range(2)]
        dve_prep, dve_attn, dve_table = sem("dve_prep"), sem("dve_attn"), sem("dve_table")
        tab_ready = sem("tab_ready")
        experts_in = sem("experts_in")
        meta_in = sem("meta_in")
        rows_in = [sem(f"rows_in{i}") for i in range(2)]
        mx_filled, mx_read = sem("mx_filled"), sem("mx_read")
        mh_filled, mh_silu = sem("mh_filled"), sem("mh_silu")
        mh_split = sem("mh_split")
        mh_step = sem("mh_step")
        my_filled, my_read = sem("my_filled"), sem("my_read")
        added = sem("added")

        block = ctx.enter_context(nc.Block())

        def small_ap(phase, part, name, b, eng=None):
            i, before, bb = small_use(phase, (part, name), b)
            if eng is not None and before is not None:
                eng.wait_ge(read[before[0]], bb * PER[before[0]] + NTH[before])
            return small[i]

        def nth(part, name, b):
            return b * PER[part] + NTH[(part, name)]

        def f16(a):
            return a[:, :].bitcast(F16)

        def rows(ap, first, count):
            return ap[bass.ds(first, count), :]

        def hold(eng, s, value):
            if not isinstance(value, int):
                value = eng.to_reg(value)
            eng.wait_ge(consts_ready, 1)
            eng.wait_ge(s, value)

        w1_rows = w1.rearrange("e k f -> (e k) f")
        w2_rows = w2.rearrange("e f d -> (e f) d")
        ws_rows = wsplit.rearrange("e p c h n -> (e p) c (h n)")

        def w_load(sp, e, c):
            if c < 2:
                src = w1_rows[bass.ds(e * D + c * P, P), :]
                dst = w_raw[c % 2]
            else:
                src = w2_rows[bass.ds(e * FF + (c - 2) * 4 * P, 4 * P), :].rearrange("(c p) d -> p c d", p=P)
                dst = w_raw[c % 2].rearrange("p (c d) -> p c d", c=4)
            if c >= 2:
                hold(sp, w_lo, e * 4 + c - 1)
            sp.dma_start(dst, src).then_inc(w_in[c % 2], 16)

        def w_store(sp, e, c):
            dst = ws_rows[bass.ds(e * P, P), c, :]
            hold(sp, w_lo, e * 4 + c + 1)
            sp.dma_start(dst, w_st[c % 2].rearrange("p h n -> p (h n)")).then_inc(w_out[c % 2], 16)

        def x_load(sp, b, half):
            src = xrows[bass.ds(b * S + half * HS, HS), :].rearrange("(t p) d -> p t d", p=P)
            hold(sp, resid_ready, (b - 1) * 2 + half + 1)
            sp.dma_start(x_in[half], src).then_inc(x_loaded[half], 16)

        def xs_store(sp, b, half):
            dst = xs[bass.ds(b * S + half * HS, HS), :].rearrange("(t p) n -> p t n", p=P)
            hold(sp, xl_split, b * 2 + half + 1)
            sp.dma_start(dst, xhl[half].rearrange("p t h n -> p t (h n)")).then_inc(xs_stored[half], 16)

        def out_store(sp, b, k):
            dst = orows[bass.ds(b * S + k * 2 * P, 2 * P), :].rearrange("(t p) d -> p t d", p=P)
            hold(sp, attn_read, nth("attn", f"out{k}", b))
            sp.dma_start(dst, osb[k % 2]).then_inc(out_stored[k % 2], 16)

        def sp_turn(sp, b, phase, x_next=True):
            w_load(sp, b, 0)
            w_load(sp, b, 1)
            if phase == "body":
                xs_store(sp, b + 1, 0)
            w_store(sp, b, 0)
            w_load(sp, b, 2)
            w_store(sp, b, 1)
            w_load(sp, b, 3)
            out_store(sp, b, 0)
            out_store(sp, b, 1)
            if phase == "body" and x_next:
                x_load(sp, b + 2, 0)
            w_store(sp, b, 2)
            if phase == "body":
                xs_store(sp, b + 1, 1)
            out_store(sp, b, 2)
            out_store(sp, b, 3)
            if phase == "body" and x_next:
                x_load(sp, b + 2, 1)
            w_store(sp, b, 3)

        @block.sync
        def _(sp):
            for half in range(2):
                sp.dma_start(x_in[half], xrows[half * HS:(half + 1) * HS, :].rearrange("(t p) d -> p t d", p=P)) \
                    .then_inc(x_loaded[half], 16)
            for n, w in enumerate((Wq, Wk, Wv)):
                sp.dma_start(raw_w[:, :, n * D:(n + 1) * D], w.rearrange("(k p) n -> p k n", p=P)).then_inc(weights_loaded, 16)
            sp.dma_start(raw_w[:, :, 3 * D:], router_t.rearrange("(k p) n -> p k n", p=P)).then_inc(weights_loaded, 16)
            sp.dma_start(raw_o, Wo.rearrange("(k p) n -> p k n", p=P)).then_inc(weights_loaded, 16)
            for dst, v_ in ((bv_b, bv), (bo_b, bo)):
                sp.dma_start(dst[:, :], v_.rearrange("(a n) -> a n", a=1).broadcast_to([P, D])).then_inc(weights_loaded, 16)
            for n, v_ in enumerate((bq, bk)):
                sp.dma_start(bqk[:, n, :], v_.rearrange("(k p) -> p k", p=P),
                             allow_slow_non_contiguous=True).then_inc(weights_loaded, 16)
            sp.wait_ge(proj_zeroed, 1)
            for h in range(H):
                m, l = h // 8, h % 8
                sp.dma_start(raw_p[l * HD:(l + 1) * HD, m, l * F:(l + 1) * F], proj_t[h]).then_inc(proj_loaded, 16)
            sp.wait_ge(slots_cleared, 1)
            sp.dma_start(meta[0:DUMP, :].rearrange("(p a) c -> p (a c)", p=P), clear[:, 0:2 * DUMP // P]).then_inc(table_cleared, 16)
            sp.dma_start(xs[N:N + P, :], zero_rows).then_inc(zero_stored, 16)
            sp.wait_ge(consts_ready, 1)
            for half in range(2):
                xs_store(sp, 0, half)
                x_load(sp, 1, half)
            sp_turn(sp, 0, "body")
            with sp.Fori(1, B - 2) as b:
                sp_turn(sp, b, "body")
            sp_turn(sp, B - 2, "body", x_next=False)
            sp_turn(sp, B - 1, "tail")
            for n in range(2):
                sp.wait_ge(w_out[n], 16 * 2 * E)
            for e in range(E):
                if e == 1:
                    sp.wait_ge(attn_read, nth("attn", "out3", B - 1))
                    for n in range(2):
                        sp.wait_ge(out_stored[n], 16 * 2 * B)
                    sp.wait_ge(meta_stored, 16 * TOPK * NT * B)
                    sp.wait_ge(tab_ready, 1)
                if e > 0:
                    sp.wait_ge(experts_in, 16 * e)
                sp.dma_start(we[:, e * EXPERT:(e + 1) * EXPERT],
                             wsplit[e].rearrange("p c h n -> p (c h n)")).then_inc(experts_in, 16)
            sp.wait_ge(experts_in, 16 * E)

        def w_high(act, e, c, first=False):
            hold(act, w_in[c % 2], (e * 2 + c // 2 + 1) * 16)
            if not (first and c < 2):
                hold(act, w_out[c % 2], (e * 2 + c // 2) * 16)
            nc.scalar.activation(w_raw[c % 2], w_raw[c % 2], ACT.Copy, scale=R_SCALE).then_inc(w_scaled, 1)
            hold(act, w_scaled, e * 4 + c + 1)
            nc.scalar.activation(w_st[c % 2][:, 0, :], w_raw[c % 2], ACT.Copy).then_inc(w_hi, 1)

        def qk_read_half(act, b, half):
            for n in range(4):
                t = half * 4 + n
                side, m = n // 2, n % 2
                act.wait_ge(qk_filled, b * QK_USES + t + 1)
                if t >= 2:
                    act.wait_ge(qk_split, b * QK_USES + t - 1)
                elif not isinstance(b, int) or b > 0:
                    act.wait_ge(qk_split, (b - 1) * QK_USES + t + 7)
                nc.scalar.activation(q32[n % 2], big[n % BIG_BANKS][:, :], ACT.Identity, bias=bqk[:, side, m:m + 1],
                                     scale=1.0 / W_SCALE).then_inc(qk_read, 1)
                act.wait_ge(qk_read, b * QK_USES + t + 1)
                nc.scalar.activation(sq[:, side, m, :], q32[n % 2], ACT.Square).then_inc(qk_squared, 1)

        def k_relu(act, b, t):
            for m in range(KC):
                n = t * KC + m
                act.wait_ge(feat_filled, b * FEAT_USES + n + 1)
                if m == 0 and t >= 2:
                    act.wait_ge(kv_tile_done, b * NT + t - 1)
                nc.scalar.activation(rk[t % 2][:, m, :], big[n % BIG_BANKS][:, :], ACT.Relu).then_inc(feat_relu, 1)

        def q_relu(act, b, half):
            for p_ in range(PAIRS):
                n = 2 * NT + half * PAIRS + p_
                act.wait_ge(feat_filled, b * FEAT_USES + n + 1)
                nc.scalar.activation(rq[:, p_, 0, :], big[n % BIG_BANKS][:, :], ACT.Relu).then_inc(feat_relu, 1)

        def act_turn(act, b, phase, first=False):
            w_high(act, b, 0, first)
            for t in range(4):
                k_relu(act, b, t)
            act.wait_ge(gate_in, b + 1)
            nc.scalar.activation(eg, dl, ACT.Exp, scale=1.0 / R_SCALE).then_inc(gate_exp, 1)
            w_high(act, b, 1, first)
            for t in range(4, NT):
                k_relu(act, b, t)
            q_relu(act, b, 0)
            w_high(act, b, 2)
            q_relu(act, b, 1)
            if phase == "body":
                qk_read_half(act, b + 1, 0)
            w_high(act, b, 3)
            if phase == "body":
                qk_read_half(act, b + 1, 1)

        def silu(act, t, u, first):
            for j in range(4):
                act.wait_ge(mh_filled, t * 4 + j + 1)
                if not first:
                    act.wait_ge(mh_split, t * 4 + j - 3)
                nc.scalar.activation(h32[j].rearrange("p a b -> p (a b)"), big[j][:, :], ACT.Silu,
                                     scale=1.0 / R_SCALE).then_inc(mh_silu, 1)

        def y_scale(act, t, u, first):
            act.wait_ge(my_filled, t + 1)
            if not first:
                act.wait_ge(added, (t - 1) * 32)
            yb = bank[6 + u % 2]
            for a in range(2):
                nc.scalar.activation(y_sb[u % 2][:, a, :], yb[:, a * D:(a + 1) * D], ACT.Copy,
                                     scale=mt[:, u % GRP, a, 1:2].bitcast(F32)).then_inc(my_read, 1)

        @block.scalar
        def _(act):
            act.wait_ge(consts_ready, 1)
            for half in range(2):
                qk_read_half(act, 0, half)
            act_turn(act, 0, "body", first=True)
            with act.Fori(1, B - 1) as b:
                act_turn(act, b, "body")
            act_turn(act, B - 1, "tail")
            act.wait_ge(attn_read, nth("attn", "out3", B - 1))
            for n in range(2):
                act.wait_ge(out_stored[n], 16 * 2 * B)
                act.wait_ge(w_out[n], 16 * 2 * E)

            def group(g, first=False):
                for u in range(GRP):
                    silu(act, g * GRP + u, u, first and u == 0)
                    if not (first and u == 0):
                        y_scale(act, g * GRP + u - 1, u - 1 + GRP, first and u <= 2)

            group(0, first=True)
            with act.Fori(1, NG) as g:
                group(g)
            y_scale(act, MT - 1, GRP - 1, False)

        def qk_project(pe, b, half, first):
            for n in range(4):
                t = half * 4 + n
                side, m = n // 2, n % 2
                if half == 1:
                    pe.wait_ge(qk_read, b * QK_USES + n + 1)
                elif not first:
                    pe.wait_ge(qf_split, (b - 1) * QF_USES + 12 + n + 1)
                if n == 0:
                    pe.wait_ge(prep_read, nth("prep", f"xT{2 * half + 1}", b))
                for i, (wl, xl) in enumerate(PASSES):
                    for k in range(KC):
                        c0 = side * D + m * P
                        mm = nc.tensor.matmul(big[n][:, :], w_hl[:, wl, k, c0:c0 + P], xT[half][:, xl * KC + k, :],
                                              start=(i == 0 and k == 0), stop=(i == 2 and k == KC - 1))
                mm.then_inc(qk_filled, 1)

        def x_transpose(pe, phase, b, half):
            pe.wait_ge(xl_split, b * 2 + half + 1)
            for j in range(2):
                dst = f16(small_ap(phase, "prep", f"xT{2 * half + j}", b, pe)).rearrange("p (t c q) -> p t c q", t=2, c=4)
                if j == 0:
                    pe.wait_ge(xn_split, b * 2 + half + 1)
                for tl in range(2):
                    for hl in range(2):
                        for k in range(KC):
                            mm = nc.tensor.transpose(dst[:, tl, hl * KC + k, :],
                                                     xhl[half][:, 2 * j + tl, hl, k * P:(k + 1) * P], ident16[:, :])
                mm.then_inc(prep_filled, 1)

        def v_project(pe, phase, b, t):
            half, tl = t // HT, t % HT
            dst = small_ap(phase, "prep", f"v{t}", b, pe)
            for i, (xl, wl) in enumerate(PASSES):
                for k in range(KC):
                    mm = nc.tensor.matmul(dst[:, 0:D + E], xT[half][:, xl * KC + k, tl * P:(tl + 1) * P],
                                          w_hl[:, wl, k, 2 * D:], start=(i == 0 and k == 0), stop=(i == 2 and k == KC - 1))
            mm.then_inc(prep_filled, 1)

        def square_sums(pe, phase, b, half):
            dst = small_ap(phase, "prep", f"nrm{half}", b, pe)
            pe.wait_ge(qk_squared, b * QK_USES + half * 4 + 4)
            for g in range(4):
                mm = nc.tensor.matmul(dst[32 * g:32 * g + 32, :], hsel[:, :], sq[:, g // 2, g % 2, :], start=True, stop=True)
            mm.then_inc(prep_filled, 1)

        def square_turn(pe, phase, b, half):
            dst = small_ap(phase, "prep", f"nrmT{half}", b, pe)
            pe.wait_ge(prep_read, nth("prep", f"nrm{half}", b))
            for t in range(HT):
                mm = nc.tensor.transpose(dst[:, t * P:(t + 1) * P], nT[:, t * P:(t + 1) * P], ident32[:, :])
            mm.then_inc(prep_filled, 1)

        def k_features(pe, b, t):
            half, tl = t // HT, t % HT
            for m in range(KC):
                n = t * KC + m
                if n < BIG_BANKS:
                    pe.wait_ge(qk_read, b * QK_USES + 4 + n + 1)
                else:
                    pe.wait_ge(feat_relu, b * FEAT_USES + n - BIG_BANKS + 1)
                if n == 0 or n == 2 * HT:
                    pe.wait_ge(qk_split, b * QK_USES + half * 4 + 4)
                for i, (kl, pl) in enumerate(PASSES):
                    mm = nc.tensor.matmul(big[n % BIG_BANKS][:, :], k_hl[half][:, m, kl, tl * P:(tl + 1) * P],
                                          p_hl[:, pl, m, :], start=(i == 0), stop=(i == 2))
                mm.then_inc(feat_filled, 1)

        def kv_sum(pe, b, t):
            pe.wait_ge(feat_relu, b * FEAT_USES + t * KC + 2)
            if t % HT == 0:
                pe.wait_ge(vp_ready, b * 2 + t // HT + 1)
            for m in range(KC):
                for s in range(2):
                    for j in range(4):
                        h = 8 * m + 2 * j + s
                        c = 2 * m + s
                        mm = nc.tensor.matmul(kvbank[32 * j:32 * j + 32, c * F:(c + 1) * F], vp[:, t, h, :],
                                              rk[t % 2][:, m, (2 * j + s) * F:(2 * j + s + 1) * F],
                                              start=(t == 0 and c == 0), stop=(t == NT - 1), skip_group_check=True)
            mm.then_inc(kv_tile_done, 1)

        def q_features(pe, b, half, p0, p1):
            for p_ in range(p0, p1):
                n = 2 * NT + half * PAIRS + p_
                m, j = p_ // 4, p_ % 4
                if half == 0 and p_ < BIG_BANKS:
                    pe.wait_ge(feat_relu, b * FEAT_USES + n - BIG_BANKS + 1)
                else:
                    pe.wait_ge(qf_split, b * QF_USES + n - 2 * NT - BIG_BANKS + 1)
                for i, (pl, ql) in enumerate(PASSES):
                    mm = nc.tensor.matmul(big[n % BIG_BANKS][:, :], p_hl[:, pl, m, j * P:(j + 1) * P],
                                          q_hl[half][:, m, ql, :], start=(i == 0), stop=(i == 2))
                mm.then_inc(feat_filled, 1)

        def attend(pe, phase, b, t):
            half, tl = t // HT, t % HT
            dst = small_ap(phase, "attn", f"ab{t}", b, pe)
            if tl == 0:
                pe.wait_ge(qf_split, b * QF_USES + (half + 1) * PAIRS)
                pe.wait_ge(kv_split, b + 1)
            for p_ in range(PAIRS):
                for i, (rl, kl) in enumerate(PASSES):
                    mm = nc.tensor.matmul(dst[:, p_ * KVW:(p_ + 1) * KVW], rq[:, p_, rl, tl * P:(tl + 1) * P],
                                          kv_hl[:, kl, p_, :], start=(i == 0), stop=(i == 2))
            mm.then_inc(attn_filled, 1)

        def o_transpose(pe, phase, b, half):
            for j in range(2):
                dst = f16(small_ap(phase, "attn", f"oT{2 * half + j}", b, pe)).rearrange("p (t c q) -> p t c q", t=2, c=4)
                if j == 0:
                    pe.wait_ge(o_split, b * 2 + half + 1)
                for tl in range(2):
                    for hl in range(2):
                        for m in range(KC):
                            mm = nc.tensor.transpose(dst[:, tl, hl * KC + m, :],
                                                     o_hl[:, 2 * j + tl, hl, m * P:(m + 1) * P], ident16[:, :])
                mm.then_inc(attn_filled, 1)

        def o_project(pe, phase, b, half):
            for j in range(2):
                dst = small_ap(phase, "attn", f"out{2 * half + j}", b, pe)
                pe.wait_ge(attn_read, nth("attn", f"oT{2 * half + j}", b))
                for tl in range(2):
                    for i, (ol, wl) in enumerate(PASSES):
                        for m in range(KC):
                            mm = nc.tensor.matmul(dst[:, tl * D:(tl + 1) * D], oT[:, 2 * j + tl, ol * KC + m, :],
                                                  wo_hl[:, wl, m, :], start=(i == 0 and m == 0), stop=(i == 2 and m == KC - 1))
                mm.then_inc(attn_filled, 1)

        def pe_turn(pe, b, phase):
            body = phase == "body"
            k_features(pe, b, 0)
            for t in range(1, NT):
                k_features(pe, b, t)
                kv_sum(pe, b, t - 1)
            dst = small_ap(phase, "attn", "rank", b, pe)
            pe.wait_ge(masks_ready, b + 1)
            m16f = m16.rearrange("p t e -> p (t e)")
            nc.tensor.matmul(dst[:, 0:(NT + 1) * E], tri[:, :], m16f, start=True, stop=False, skip_group_check=True)
            for s in range(1, NT + 1):
                mm = nc.tensor.matmul(dst[:, s * E:(NT + 1) * E], ones16[:, :], m16f[:, 0:(NT + 1 - s) * E],
                                      start=False, stop=(s == NT), skip_group_check=True)
            mm.then_inc(attn_filled, 1)
            dst = small_ap(phase, "attn", "vsum", b, pe)
            pe.wait_ge(vsum_ready, b + 1)
            nc.tensor.matmul(dst[:, 0:H * (HD + 1)], cfeat[:, :], vsum.rearrange("p h d -> p (h d)"),
                             start=True, stop=True).then_inc(attn_filled, 1)
            kv_sum(pe, b, NT - 1)
            q_features(pe, b, 0, 0, 2)
            dst = small_ap(phase, "attn", "kvT", b, pe)
            pe.wait_ge(kvt_copied, b + 1)
            for m in range(KC):
                mm = nc.tensor.transpose(dst[:, m * P:(m + 1) * P], kvt[:, m * P:(m + 1) * P], ident32[:, :])
            mm.then_inc(attn_filled, 1)
            q_features(pe, b, 0, 2, PAIRS)
            dst = small_ap(phase, "attn", "cn", b, pe)
            pe.wait_ge(kvf_ready, b + 1)
            nc.tensor.matmul(dst[:, 0:PAIRS * KVW], cfeat[:, :], kvf.rearrange("p a c -> p (a c)"),
                             start=True, stop=True).then_inc(attn_filled, 1)
            for t in range(HT):
                attend(pe, phase, b, t)
            q_features(pe, b, 1, 0, PAIRS)
            if body:
                x_transpose(pe, phase, b + 1, 0)
                qk_project(pe, b + 1, 0, False)
            o_transpose(pe, phase, b, 0)
            for t in range(HT, NT):
                attend(pe, phase, b, t)
            o_project(pe, phase, b, 0)
            if body:
                v_project(pe, phase, b + 1, 0)
                v_project(pe, phase, b + 1, 1)
                square_sums(pe, phase, b + 1, 0)
            o_transpose(pe, phase, b, 1)
            if body:
                v_project(pe, phase, b + 1, 2)
                square_turn(pe, phase, b + 1, 0)
                v_project(pe, phase, b + 1, 3)
            o_project(pe, phase, b, 1)
            if body:
                pe_second_half(pe, phase, b + 1)

        def pe_second_half(pe, phase, b):
            x_transpose(pe, phase, b, 1)
            qk_project(pe, b, 1, False)
            v_project(pe, phase, b, 4)
            v_project(pe, phase, b, 5)
            square_sums(pe, phase, b, 1)
            v_project(pe, phase, b, 6)
            square_turn(pe, phase, b, 1)
            v_project(pe, phase, b, 7)

        def rows_transpose(pe, g, u):
            dst = f16(bank[u % 2]).rearrange("p (c q) -> p c q", c=2 * KC)
            pe.wait_ge(rows_in[u % 2], (g * (GRP // 2) + u // 2 + 1) * 32)
            for a in range(2):
                for c in range(2 * KC):
                    mm = nc.tensor.transpose(dst[:, c, a * P:(a + 1) * P], xg[:, u % GRP, a, c * P:(c + 1) * P], ident16[:, :])
            mm.then_inc(mx_filled, 1)

        def hidden(pe, t, u, first):
            e = pe.value_load(tab[0:1, 0, bass.ds(t, 1)], min_val=0, max_val=E - 1)
            hold(pe, experts_in, e * 16 + 16)
            pe.wait_ge(mx_read, t + 1)
            for j in range(4):
                if not first:
                    pe.wait_ge(mh_silu, t * 4 + j - 3)
                for i2 in range(2):
                    c = 2 * j + i2
                    for i, (wl, xl) in enumerate(PASSES):
                        for k in range(KC):
                            mm = nc.tensor.matmul(
                                big[j][:, i2 * TS:(i2 + 1) * TS],
                                we[:, bass.ds(e * EXPERT + (k * 2048 + wl * 1024 + c * P), P)],
                                moe_xT[u % 2][:, xl * KC + k, :], start=(i == 0 and k == 0), stop=(i == 2 and k == KC - 1))
                mm.then_inc(mh_filled, 1)

        def expert_out(pe, t, u, first):
            e = pe.value_load(tab[0:1, 0, bass.ds(t, 1)], min_val=0, max_val=E - 1)
            pe.wait_ge(mh_split, t * 4 + 4)
            if not first:
                pe.wait_ge(my_read, t * 2 - 2)
            yb = bank[6 + u % 2]
            for a in range(2):
                for c in range(FF // P):
                    for i, (hl, wl) in enumerate(PASSES):
                        off = (2 + c // 4) * 2048 + wl * 1024 + (c % 4) * D
                        mm = nc.tensor.matmul(yb[:, a * D:(a + 1) * D], hT[u % 2][:, c, hl, a * P:(a + 1) * P],
                                              we[:, bass.ds(e * EXPERT + off, D)],
                                              start=(c == 0 and i == 0), stop=(c == FF // P - 1 and i == 2))
            mm.then_inc(my_filled, 1)

        @block.tensor
        def _(pe):
            pe.wait_ge(consts_ready, 1)
            x_transpose(pe, "first", 0, 0)
            qk_project(pe, 0, 0, True)
            v_project(pe, "first", 0, 0)
            v_project(pe, "first", 0, 1)
            square_sums(pe, "first", 0, 0)
            v_project(pe, "first", 0, 2)
            square_turn(pe, "first", 0, 0)
            v_project(pe, "first", 0, 3)
            pe_second_half(pe, "first", 0)
            pe_turn(pe, 0, "body")
            with pe.Fori(1, B - 1) as b:
                pe_turn(pe, b, "body")
            pe_turn(pe, B - 1, "tail")
            pe.wait_ge(attn_read, nth("attn", "out3", B - 1))
            pe.wait_ge(tab_ready, 1)

            def group(g, first=False, last=False):
                for u in range(GRP):
                    t = g * GRP + u
                    hidden(pe, t, u, first and u == 0)
                    if not (last and u == GRP - 1):
                        rows_transpose(pe, g, u + 1)
                    if not (first and u == 0):
                        expert_out(pe, t - 1, u - 1 + GRP, first and u <= 2)

            rows_transpose(pe, 0, 0)
            group(0, first=True)
            with pe.Fori(1, NG - 1) as g:
                group(g)
            group(NG - 1, last=True)
            expert_out(pe, MT - 1, GRP - 1, False)

        def w_low(pool, e, c):
            hold(pool, w_hi, e * 4 + c + 1)
            nc.gpsimd.tensor_tensor(w_st[c % 2][:, 1, :], w_raw[c % 2], w_st[c % 2][:, 0, :], ALU.subtract).then_inc(w_lo, 1)

        def x_low(pool, b, half):
            hold(pool, xn_split, b * 2 + half + 1)
            nc.gpsimd.tensor_tensor(xhl[half][:, :, 1, :], xn, xhl[half][:, :, 0, :], ALU.subtract).then_inc(xl_split, 1)
            nc.gpsimd.tensor_tensor(x_in[half], x_in[half], xn, ALU.add).then_inc(x_plus_xn, 1)
            hold(pool, x_plus_xn, b * 2 + half + 1)
            nc.gpsimd.tensor_tensor(x_in[half], x_in[half], bo_b[:, :].rearrange("p (a d) -> p a d", a=1).broadcast_to([P, HT, D]),
                                    ALU.add).then_inc(x_summed, 1)

        def resid_copy(pool, b, half, first=False):
            if not first:
                hold(pool, attn_read, nth("attn", f"out{2 * half + 1}", b - 1))
            hold(pool, x_summed, b * 2 + half + 1)
            nc.gpsimd.tensor_copy(resid[:, half * HT:(half + 1) * HT, :], x_in[half]).then_inc(resid_ready, 1)

        def v_total(pool, b):
            hold(pool, prep_read, nth("prep", "v7", b))
            nc.gpsimd.tensor_tensor(vtmp, v32[:, 0:4, :], v32[:, 4:8, :], ALU.add).then_inc(pool_prep, 1)
            hold(pool, pool_prep, b * 2 + 1)
            nc.gpsimd.tensor_tensor(vtmp[:, 0:2, :], vtmp[:, 0:2, :], vtmp[:, 2:4, :], ALU.add).then_inc(pool_prep, 1)
            hold(pool, pool_prep, b * 2 + 2)
            nc.gpsimd.tensor_tensor(vsum[:, :, 0:HD], vtmp[:, 0, :].rearrange("p (h d) -> p h d", h=H),
                                    vtmp[:, 1, :].rearrange("p (h d) -> p h d", h=H), ALU.add).then_inc(vsum_ready, 1)

        def scatter(pool, b):
            hold(pool, slots_ready, b + 1)
            for k in range(TOPK):
                for t in range(NT):
                    nc.gpsimd.indirect_dma_start(meta, bass.IndirectOffsetOnAxis(slot_i[:, k, t:t + 1], 0),
                                                 rec[:, k, t, :], None).then_inc(meta_stored, 16)

        def pool_turn(pool, b, phase):
            body = phase == "body"
            if body:
                x_low(pool, b + 1, 0)
            w_low(pool, b, 0)
            scatter(pool, b)
            w_low(pool, b, 1)
            w_low(pool, b, 2)
            if body:
                resid_copy(pool, b + 1, 0)
                x_low(pool, b + 1, 1)
                resid_copy(pool, b + 1, 1)
            w_low(pool, b, 3)
            if body:
                v_total(pool, b + 1)

        @block.gpsimd
        def _(pool):
            g = nc.gpsimd
            ch = Chain(pool_first, 19)
            ch.start(pool, 0)
            ch.step(g.memset(clear, 0))
            ch.step(g.memset(zero_rows, 0.0))
            ch.wait()
            g.memset(clear.rearrange("p (a c) -> p a c", c=2)[:, :, 0:1], N).then_inc(slots_cleared, 1)
            ch.step(g.memset(ident16[:, :], 0.0))
            ch.step(g.memset(ident32[:, :], 0.0))
            ch.step(g.memset(tri[:, :], 1.0))
            ch.step(g.memset(ones16[:, :], 1.0))
            ch.step(g.memset(cfeat[:, :], EPSF))
            ch.step(g.memset(hsel[:, :], 1.0))
            ch.step(g.memset(vsum[:, :, HD:HD + 1], float(NT)))
            ch.wait()
            for m in (ident16, ident32):
                ch.step(g.affine_select(out=m[:, :], in_=m[:, :], compare_op=ALU.not_equal, fill=1.0, base=0,
                                        pattern=[[-1, P]], channel_multiplier=1))
            ch.step(g.affine_select(out=tri[:, :], in_=tri[:, :], compare_op=ALU.is_gt, fill=0.0, base=0,
                                    pattern=[[1, P]], channel_multiplier=-1))
            ch.link(g.affine_select(out=hsel[:, :], in_=hsel[:, :], compare_op=ALU.is_ge, fill=0.0, base=0,
                                    pattern=[[-HD, 32]], channel_multiplier=1))
            ch.link(g.affine_select(out=hsel[:, :], in_=hsel[:, :], compare_op=ALU.is_ge, fill=0.0, base=HD - 1,
                                    pattern=[[HD, 32]], channel_multiplier=-1))
            ch.step(g.iota(iota_i[:, :], pattern=[[1, 256]], base=0, channel_multiplier=0))
            ch.step(g.iota(tok_i, pattern=[[P, NT]], base=0, channel_multiplier=1))
            ch.step(g.iota(dump_i, pattern=[[1, TOPK], [P * TOPK, NT]], base=DUMP, channel_multiplier=TOPK))
            ch.step(g.memset(vp, 0.0))
            ch.link(g.memset(kvf, 0.0))
            assert ch.n == ch.per, ch.n
            pool.wait_ge(consts_ready, 1)
            for half in range(2):
                x_low(pool, 0, half)
                resid_copy(pool, 0, half, first=True)
            v_total(pool, 0)
            pool.wait_ge(table_cleared, 16)
            pool_turn(pool, 0, "body")
            with pool.Fori(1, B - 1) as b:
                pool_turn(pool, b, "body")
            pool_turn(pool, B - 1, "tail")
            pool.wait_ge(tab_ready, 1)
            pool.wait_ge(meta_stored, 16 * TOPK * NT * B)
            pool.wait_ge(zero_stored, 16)
            for n in range(2):
                pool.wait_ge(xs_stored[n], 16 * B)
            last_row = pool.to_reg(N - 1)

            def meta_load(t, u):
                row = pool.value_load(tab[0:1, 1, bass.ds(t, 1)], min_val=0, max_val=TRASH)
                src = meta[bass.ds(row, TS), :].rearrange("(a p) c -> p a c", p=P)
                pool.dma_start(mt[:, u % GRP, :, :], src).then_inc(meta_in, 16)

            def gather(t, u):
                hold(pool, meta_in, t * 16 + 16)
                for a in range(2):
                    nc.gpsimd.indirect_dma_start(xg[:, u % GRP, a, :], None, xs,
                                                 bass.IndirectOffsetOnAxis(mt[:, u % GRP, a, 0:1], 0)).then_inc(rows_in[u % 2], 16)

            def add_out(t, u):
                hold(pool, my_read, t * 2 + 2)
                for a in range(2):
                    nc.gpsimd.indirect_dma_start(orows, bass.IndirectOffsetOnAxis(mt[:, u % GRP, a, 0:1], 0),
                                                 y_sb[u % 2][:, a, :], None, bounds_check=last_row, oob_is_err=False,
                                                 compute_op=ALU.add).then_inc(added, 16)

            def group(g, first=False, last=False):
                for u in range(GRP):
                    t = g * GRP + u
                    if not (first and u == 0):
                        hold(pool, added, t * 32)
                    else:
                        pool.wait_ge(mx_filled, 1)
                    if not (last and u >= GRP - 2):
                        gather(t + 2, u + 2)
                    if not (last and u >= GRP - 3):
                        meta_load(t + 3, u + 3)
                    if first and u == 0:
                        for n in range(2):
                            pool.wait_ge(out_stored[n], 16 * 2 * B)
                    add_out(t, u)

            meta_load(0, 0)
            pool.wait_ge(meta_in, 16)
            meta_load(1, 1)
            pool.wait_ge(meta_in, 32)
            meta_load(2, 2)
            gather(0, 0)
            gather(1, 1)
            group(0, first=True)
            with pool.Fori(1, NG - 1) as gg:
                group(gg)
            group(NG - 1, last=True)
            pool.wait_ge(added, 32 * MT)

        v = nc.vector

        def rsqrt(ch, y, a, u):
            ch.link(v.tensor_scalar(u.bitcast(I32), a.bitcast(I32), 1, None, ALU.arith_shift_right))
            ch.link(v.tensor_scalar(y.bitcast(I32), u.bitcast(I32), -1.0, MAGIC, ALU.mult, ALU.add))
            for _ in range(3):
                ch.link(v.tensor_tensor(u, a, y, ALU.mult))
                ch.link(v.scalar_tensor_tensor(u, u, -0.5, y, ALU.mult, ALU.mult))
                ch.link(v.scalar_tensor_tensor(y, u, 1.5, y, ALU.add, ALU.mult))

        chp, cha = Chain(dve_prep, 2 * (24 + 4 + 4 + 14 + 1)), Chain(dve_attn, 18 + 16 + 1 + 2 * (4 + 10))

        def layernorm(dve, b, half, first=False):
            hold(dve, x_loaded[half], (b + 1) * 16)
            for t in range(HT):
                chp.step(v.bn_stats(bn[:, t, :], x_in[half][:, t, :]))
            hold(dve, dve_prep, chp.base + chp.n)
            for t in range(HT):
                chp.step(v.bn_aggr(mv[:, t, :], bn[:, t, :]))
            chp.wait()
            chp.link(v.tensor_scalar(va, mv[:, :, 1], 1e-5, None, ALU.add))
            rsqrt(chp, vy, va, vu)
            if not (first and half == 0):
                dve.wait_ge(x_plus_xn, b * 2 + half)
            for t in range(HT):
                chp.step(v.tensor_scalar(xn[:, t, :], x_in[half][:, t, :], mv[:, t, 0:1], vy[:, t:t + 1],
                                         ALU.subtract, ALU.mult))
            chp.wait()
            if not first:
                dve.wait_ge(xs_stored[half], b * 16)
            v.tensor_copy(xhl[half][:, :, 0, :], xn).then_inc(xn_split, 1)

        def drain(dve, phase, part, name, b):
            dve.wait_ge(filled[part], nth(part, name, b))
            return small_ap(phase, part, name, b)

        def xT_copy(dve, phase, b, half):
            for j in range(2):
                src = f16(drain(dve, phase, "prep", f"xT{2 * half + j}", b)).rearrange("p (t c q) -> p c t q", t=2, c=4)
                dst = xT[half].rearrange("p c (t q) -> p c t q", q=P)[:, :, 2 * j:2 * j + 2, :]
                v.tensor_copy(dst, src).then_inc(prep_read, 1)

        def qk_halves(dve, b, half):
            for n in range(4):
                side, m = n // 2, n % 2
                dst = (q_hl, k_hl)[side][half]
                dve.wait_ge(qk_read, b * QK_USES + half * 4 + n + 1)
                chp.link(v.tensor_copy(dst[:, m, 0, :], q32[n % 2]))
                v.tensor_tensor(dst[:, m, 1, :], q32[n % 2], dst[:, m, 0, :], ALU.subtract).then_inc(qk_split, 1)

        def v_drain(dve, phase, b, t):
            src = drain(dve, phase, "prep", f"v{t}", b)
            chp.step(v.tensor_copy(lg[:, t, :], src[:, D:D + E]))
            v.scalar_tensor_tensor(v32[:, t, :], src[:, 0:D], 1.0 / W_SCALE, bv_b[:, :], ALU.mult, ALU.add).then_inc(prep_read, 1)

        def squares_drain(dve, phase, b, half):
            v.tensor_copy(nT, drain(dve, phase, "prep", f"nrm{half}", b)[:, :]).then_inc(prep_read, 1)

        def norms(dve, phase, b, half):
            src = drain(dve, phase, "prep", f"nrmT{half}", b)[:, :].rearrange("p (t g c) -> p t g c", t=HT, g=4)
            v.tensor_copy(nsq, src[:, :, :, 0:8]).then_inc(prep_read, 1)
            dve.wait_ge(prep_read, nth("prep", f"nrmT{half}", b))
            rsqrt(chp, ny, nsq, nu)
            chp.link(v.tensor_tensor(nu, nsq, ny, ALU.mult))
            chp.link(v.tensor_scalar(norm[:, half], nu, 1e-8, None, ALU.add))
            chp.link(v.reciprocal(rn, norm[:, half, :, 2:4, :]))

        def v_over_norm(dve, b, half):
            ts = slice(half * HT, (half + 1) * HT)
            dve.wait_ge(prep_read, nth("prep", f"v{half * 4 + 3}", b))
            dst = vp[:, ts].rearrange("p t h d -> p (t h) d")
            rnf = rn.rearrange("p t g e -> p (t g e)").unsqueeze(2)
            chp.step(v.tensor_copy(dst[:, :, HD:HD + 1], rnf))
            v.tensor_tensor(dst[:, :, 0:HD], v32[:, ts].rearrange("p t (h d) -> p (t h) d", d=HD),
                            rnf.broadcast_to([P, HT * H, HD]), ALU.mult).then_inc(vp_ready, 1)

        def dve_prep_first_half(dve, phase, b):
            v_drain(dve, phase, b, 0)
            v_drain(dve, phase, b, 1)
            squares_drain(dve, phase, b, 0)

        def dve_prep_second_half(dve, phase, b, first=False):
            layernorm(dve, b, 1, first)
            xT_copy(dve, phase, b, 1)
            qk_halves(dve, b, 1)
            v_drain(dve, phase, b, 4)
            v_drain(dve, phase, b, 5)
            squares_drain(dve, phase, b, 1)
            v_drain(dve, phase, b, 6)
            norms(dve, phase, b, 1)
            v_drain(dve, phase, b, 7)
            v_over_norm(dve, b, 1)

        def choose(dve, b):
            for t in range(NT):
                cha.step(v.max(mx[:, t, :], lg[:, t, :]))
            cha.wait()
            v.tensor_tensor(dl, mx[:, :, 1], mx[:, :, 0], ALU.subtract).then_inc(gate_in, 1)
            for t in range(NT):
                cha.step(v.max_index(mi[:, t, :], mx[:, t, :], lg[:, t, :]))
            cha.wait()
            cha.link(v.tensor_copy(ix, mi[:, :, 0:TOPK].rearrange("p t k -> p k t")))
            cha.link(v.tensor_tensor(oh.rearrange("p k t e -> p (k t) e"),
                                     ix.rearrange("p k t -> p (k t)").unsqueeze(2).broadcast_to([P, TOPK * NT, E]),
                                     iota_e[:, :].unsqueeze(1).broadcast_to([P, TOPK * NT, E]), ALU.is_equal))
            v.tensor_tensor(m16[:, 0:NT, :], oh[:, 0], oh[:, 1], ALU.add).then_inc(masks_ready, 1)

        def place(dve, phase, b, first):
            src = drain(dve, phase, "attn", "rank", b)
            cha.step(v.tensor_tensor(rank, src[:, 0:NT * E].rearrange("p (t e) -> p t e", e=E),
                                     carry[:, :].unsqueeze(1).broadcast_to([P, NT, E]), ALU.add))
            cha.wait()
            v.tensor_tensor(carry[:, :], src[:, NT * E:(NT + 1) * E], carry[:, :], ALU.add).then_inc(attn_read, 1)
            cha.link(v.tensor_tensor(rsel, oh, rank.unsqueeze(1).broadcast_to([P, TOPK, NT, E]), ALU.mult))
            cha.link(v.tensor_reduce(rpos, rsel, AX.X, ALU.add))
            cha.step(v.tensor_scalar(keep, rpos, float(CAP), None, ALU.is_lt))
            cha.link(v.scalar_tensor_tensor(slot, ix, float(RROWS), rpos, ALU.mult, ALU.add))
            cha.link(v.tensor_tensor(slot, slot, dump_f[:, :, :], ALU.subtract))
            cha.link(v.tensor_tensor(slot, slot, keep, ALU.mult))
            cha.link(v.tensor_tensor(slot, slot, dump_f[:, :, :], ALU.add))
            dve.wait_ge(gate_exp, b + 1)
            cha.link(v.tensor_scalar(gate[:, 1, :], eg, 1.0, None, ALU.add))
            cha.link(v.reciprocal(gate[:, 0, :], gate[:, 1, :]))
            cha.link(v.tensor_scalar(gate[:, 0, :], gate[:, 0, :], 1.0 / (H_SCALE * R_SCALE), None, ALU.mult))
            cha.link(v.tensor_tensor(gate[:, 1, :], gate[:, 0, :], eg, ALU.mult))
            if not first:
                dve.wait_ge(meta_stored, b * 16 * TOPK * NT)
            cha.step(v.tensor_copy(rec[:, :, :, 0], tok_f[:, :].unsqueeze(1).broadcast_to([P, TOPK, NT])))
            cha.step(v.tensor_copy(rec[:, :, :, 1].bitcast(F32), gate))
            cha.link(v.tensor_copy(slot_i, slot))
            cha.step(v.tensor_scalar(tok_f[:, :], tok_f[:, :], float(S), None, ALU.add))
            v.tensor_scalar(dump_f[:, :, :], dump_f[:, :, :], float(S * TOPK), None, ALU.add).then_inc(slots_ready, 1)

        def kv_build(dve, phase, b):
            src = drain(dve, phase, "attn", "kvT", b)[:, 0:256].rearrange("p (a c) -> p a c", c=32)
            csv = cs_b.rearrange("p (a s) d -> p a s d", s=2)
            rows_ = [slice(s * 64, s * 64 + 64) for s in range(2)]
            cha.step(v.tensor_tensor(kvf[rows_[0], :, 0:HD + 1], src[rows_[0], :, 0:HD + 1], csv[rows_[0], :, 0, :], ALU.add))
            v.tensor_tensor(kvf[rows_[1], :, HD + 1:], src[rows_[1], :, 0:HD + 1], csv[rows_[1], :, 1, :], ALU.add) \
                .then_inc(attn_read, 1)
            dve.wait_ge(attn_read, nth("attn", "kvT", b))
            v.tensor_copy(kv_hl[:, 0], kvf).then_inc(kvf_ready, 1)
            dve.wait_ge(kvf_ready, b + 1)
            v.tensor_tensor(kv_hl[:, 1], kvf, kv_hl[:, 0], ALU.subtract).then_inc(kv_split, 1)

        def q_low(dve, b, half, p0, p1):
            for p_ in range(p0, p1):
                n = 2 * NT + half * PAIRS + p_
                dve.wait_ge(feat_relu, b * FEAT_USES + n + 1)
                v.scalar_tensor_tensor(rq[:, p_, 1, :], big[n % BIG_BANKS][:, :], 0.0, rq[:, p_, 0, :],
                                       ALU.max, ALU.subtract).then_inc(qf_split, 1)

        def constant_part(dve, b, half):
            for t in range(HT):
                ins = v.tensor_tensor(nd[:, t], norm[:, half, t, 0:2, :].rearrange("p g e -> p (g e)").unsqueeze(2)
                                      .broadcast_to([P, H, HD + 1]), cn_b, ALU.mult)
                cha.step(ins)
            cha.wait()

        def attend_drain(dve, phase, b, t):
            src = drain(dve, phase, "attn", f"ab{t}", b)[:, 0:H * (HD + 1)].rearrange("p (h d) -> p h d", h=H)
            v.tensor_tensor(nd[:, t % HT], src, nd[:, t % HT], ALU.add).then_inc(attn_read, 1)

        def normalise(dve, b, half):
            dve.wait_ge(attn_read, nth("attn", f"ab{half * 4 + 3}", b))
            nq = norm[:, half, :, 0:2, :].rearrange("p t g e -> p t (g e)")
            cha.link(v.scalar_tensor_tensor(dn, nq, 1e-6 * P_SCALE * P_SCALE, nd[:, :, :, HD], ALU.mult, ALU.max))
            cha.link(v.reciprocal(dn, dn))
            ndv = nd.rearrange("p t h d -> p (t h) d")[:, :, 0:HD]
            cha.link(v.tensor_tensor(ndv, ndv, dn.rearrange("p t h -> p (t h)").unsqueeze(2).broadcast_to([P, HT * H, HD]),
                                     ALU.mult))
            ohv = o_hl.rearrange("p t l (h d) -> p t l h d", h=H)
            for t in range(HT):
                cha.step(v.tensor_copy(ohv[:, t, 0], nd[:, t, :, 0:HD]))
            cha.wait()
            for t in range(HT - 1):
                cha.step(v.tensor_tensor(ohv[:, t, 1], nd[:, t, :, 0:HD], ohv[:, t, 0], ALU.subtract))
            v.tensor_tensor(ohv[:, HT - 1, 1], nd[:, HT - 1, :, 0:HD], ohv[:, HT - 1, 0], ALU.subtract).then_inc(o_split, 1)

        def oT_copy(dve, phase, b, half):
            for j in range(2):
                src = f16(drain(dve, phase, "attn", f"oT{2 * half + j}", b)).rearrange("p (t c q) -> p t c q", t=2, c=4)
                v.tensor_copy(oT[:, 2 * j:2 * j + 2], src).then_inc(attn_read, 1)

        def out_drain(dve, phase, b, half, first):
            for j in range(2):
                k = 2 * half + j
                src = drain(dve, phase, "attn", f"out{k}", b)[:, :].rearrange("p (t d) -> p t d", t=2)
                if half == 1:
                    dve.wait_ge(out_stored[k % 2], b * 32 + 16)
                elif not first:
                    dve.wait_ge(out_stored[k % 2], b * 32)
                dve.wait_ge(resid_ready, b * 2 + half + 1)
                v.scalar_tensor_tensor(osb[k % 2], src, 1.0 / R_SCALE, resid[:, 2 * k:2 * k + 2, :], ALU.mult, ALU.add) \
                    .then_inc(attn_read, 1)

        def dve_turn(dve, b, phase, first=False):
            body = phase == "body"
            cha.start(dve, b)
            if body:
                chp.start(dve, b + 1)
                layernorm(dve, b + 1, 0)
            choose(dve, b)
            place(dve, phase, b, first)
            v.tensor_copy(cs_b.rearrange("p h d -> p (h d)"), drain(dve, phase, "attn", "vsum", b)[:, 0:H * (HD + 1)]) \
                .then_inc(attn_read, 1)
            dve.wait_ge(kv_tile_done, (b + 1) * NT)
            v.tensor_copy(kvt, kvbank[:, 0:256]).then_inc(kvt_copied, 1)
            q_low(dve, b, 0, 0, 2)
            kv_build(dve, phase, b)
            q_low(dve, b, 0, 2, PAIRS)
            v.tensor_copy(cn_b.rearrange("p h d -> p (h d)"), drain(dve, phase, "attn", "cn", b)[:, 0:H * (HD + 1)]) \
                .then_inc(attn_read, 1)
            dve.wait_ge(attn_read, nth("attn", "cn", b))
            constant_part(dve, b, 0)
            for t in range(HT):
                attend_drain(dve, phase, b, t)
            q_low(dve, b, 1, 0, PAIRS)
            if body:
                xT_copy(dve, phase, b + 1, 0)
            normalise(dve, b, 0)
            if body:
                qk_halves(dve, b + 1, 0)
            oT_copy(dve, phase, b, 0)
            dve.wait_ge(o_split, b * 2 + 1)
            constant_part(dve, b, 1)
            for t in range(HT, NT):
                attend_drain(dve, phase, b, t)
            out_drain(dve, phase, b, 0, first)
            if body:
                dve_prep_first_half(dve, phase, b + 1)
            normalise(dve, b, 1)
            oT_copy(dve, phase, b, 1)
            if body:
                v_drain(dve, phase, b + 1, 2)
                norms(dve, phase, b + 1, 0)
                v_drain(dve, phase, b + 1, 3)
                v_over_norm(dve, b + 1, 0)
            out_drain(dve, phase, b, 1, first)
            if body:
                dve_prep_second_half(dve, phase, b + 1)
                chp.end()
            cha.end()

        def tile_table(dve):
            K = RROWS // TS
            ch = Chain(dve_table, 0)
            ch.start(dve, 0)
            at = [0]

            def take(*shape):
                n = 1
                for k in shape:
                    n *= k
                a = tb[0:1, at[0]:at[0] + n]
                at[0] += n
                if len(shape) == 2:
                    a = a.rearrange("p (a b) -> p a b", a=shape[0])
                return a

            iota_f, cnt, over = take(256), take(E), take(E, K)
            tiles, upto, used = take(E), take(E, E), take(E)
            past, pt, ex, ue = take(MT, E), take(MT, E), take(MT), take(MT)
            dve.wait_ge(vsum_ready, B)
            dve.wait_ge(vp_ready, 2 * B)
            ch.link(v.tensor_copy(iota_f, iota_i[0:1, :]))
            ch.link(v.tensor_scalar(cnt, carry[0:1, :], float(CAP), None, ALU.min))
            ch.link(v.tensor_scalar(ue[:, 0:K], iota_f[:, 0:K], float(TS), None, ALU.mult))
            ch.link(v.tensor_tensor(over, cnt.unsqueeze(2).broadcast_to([1, E, K]),
                                    ue[:, 0:K].unsqueeze(1).broadcast_to([1, E, K]), ALU.is_gt))
            ch.link(v.tensor_reduce(tiles, over, AX.X, ALU.add))
            ch.link(v.tensor_tensor(upto, iota_f[:, 0:E].unsqueeze(1).broadcast_to([1, E, E]),
                                    iota_f[:, 0:E].unsqueeze(2).broadcast_to([1, E, E]), ALU.is_le))
            ch.link(v.tensor_tensor(upto, upto, tiles.unsqueeze(1).broadcast_to([1, E, E]), ALU.mult))
            ch.link(v.tensor_reduce(used, upto, AX.X, ALU.add))
            ch.link(v.tensor_tensor(past, iota_f[:, 0:MT].unsqueeze(2).broadcast_to([1, MT, E]),
                                    used.unsqueeze(1).broadcast_to([1, MT, E]), ALU.is_ge))
            ch.link(v.tensor_reduce(ex, past, AX.X, ALU.add))
            ch.link(v.tensor_tensor(pt, past, tiles.unsqueeze(1).broadcast_to([1, MT, E]), ALU.mult))
            ch.link(v.tensor_reduce(ue, pt, AX.X, ALU.add))
            ch.link(v.tensor_tensor(ue, iota_f[:, 0:MT], ue, ALU.subtract))
            ch.link(v.tensor_scalar(ue, ue, float(TS), None, ALU.mult))
            ch.link(v.scalar_tensor_tensor(ue, ex, float(RROWS), ue, ALU.mult, ALU.add))
            ch.link(v.tensor_scalar(tab[:, 1, :], ue, float(TRASH), None, ALU.min))
            v.tensor_scalar(tab[:, 0, :], ex, float(E - 1), None, ALU.min).then_inc(tab_ready, 1)

        def rows_copy(dve, t, u):
            dve.wait_ge(mx_filled, t + 1)
            v.tensor_copy(moe_xT[u % 2].rearrange("p c q -> p (c q)"), f16(bank[u % 2])).then_inc(mx_read, 1)

        def hidden_split(dve, t, u):
            for j in range(4):
                dve.wait_ge(mh_silu, t * 4 + j + 1)
                v.tensor_scalar(hT[u % 2][:, 2 * j:2 * j + 2, 0, :], h32[j], H_SCALE, None, ALU.mult).then_inc(mh_step, 1)
                dve.wait_ge(mh_step, t * 4 + j + 1)
                v.scalar_tensor_tensor(hT[u % 2][:, 2 * j:2 * j + 2, 1, :], h32[j], H_SCALE, hT[u % 2][:, 2 * j:2 * j + 2, 0, :],
                                       ALU.mult, ALU.subtract).then_inc(mh_split, 1)

        @block.vector
        def _(dve):
            ch = Chain(dve_first, 0)
            ch.start(dve, 0)
            v.memset(raw_p, 0.0).then_inc(proj_zeroed, 1)
            ch.step(v.memset(carry[:, :], 0.0))
            ch.step(v.memset(m16[:, NT, :], 0.0))
            dve.wait_ge(pool_first, 19)
            ch.step(v.tensor_copy(iota_e[:, :], iota_i[:, 0:E]))
            ch.step(v.tensor_copy(tok_f[:, :], tok_i))
            ch.step(v.tensor_copy(dump_f[:, :, :], dump_i))
            dve.wait_ge(weights_loaded, 16 * 9)
            dve.wait_ge(proj_loaded, 16 * H)
            scaled = ((w_hl[:, :, :, 0:3 * D], raw_w[:, :, 0:3 * D], W_SCALE), (w_hl[:, :, :, 3 * D:], raw_w[:, :, 3 * D:], R_SCALE),
                      (wo_hl[:, :, :, :], raw_o, R_SCALE), (p_hl[:, :, :, :], raw_p, P_SCALE))
            for dst, src, scale in scaled:
                ch.step(v.tensor_scalar(dst[:, 0], src, scale, None, ALU.mult))
            ch.wait()
            for dst, src, scale in scaled:
                ch.step(v.scalar_tensor_tensor(dst[:, 1], src, scale, dst[:, 0], ALU.mult, ALU.subtract))
            ch.wait()
            dve.wait_ge(table_cleared, 16)
            dve.wait_ge(zero_stored, 16)
            v.memset(mv, 0.0).then_inc(consts_ready, 1)
            dve.wait_ge(consts_ready, 1)

            chp.start(dve, 0)
            layernorm(dve, 0, 0, first=True)
            xT_copy(dve, "first", 0, 0)
            qk_halves(dve, 0, 0)
            dve_prep_first_half(dve, "first", 0)
            v_drain(dve, "first", 0, 2)
            norms(dve, "first", 0, 0)
            v_drain(dve, "first", 0, 3)
            v_over_norm(dve, 0, 0)
            dve_prep_second_half(dve, "first", 0, first=True)
            chp.end()
            dve_turn(dve, 0, "body", first=True)
            with dve.Fori(1, B - 1) as b:
                dve_turn(dve, b, "body")
            dve_turn(dve, B - 1, "tail")
            tile_table(dve)
            dve.wait_ge(attn_read, nth("attn", "out3", B - 1))
            for n in range(2):
                dve.wait_ge(out_stored[n], 16 * 2 * B)
                dve.wait_ge(w_out[n], 16 * 2 * E)

            def group(g, last=False):
                for u in range(GRP):
                    t = g * GRP + u
                    hidden_split(dve, t, u)
                    if not (last and u == GRP - 1):
                        rows_copy(dve, t + 1, u + 1)

            rows_copy(dve, 0, 0)
            with dve.Fori(0, NG - 1) as g:
                group(g)
            group(NG - 1, last=True)


def kernel(**inputs):
    import numpy as _np
    import concourse.bacc as _bacc
    from concourse import mybir as _mybir
    from concourse.bass_utils import run_bass_kernel_spmd as _run

    layout = {
        "x": inputs["L0_attn_x"], "Wq": inputs["L0_attn_Wq"], "bq": inputs["L0_attn_bq"], "Wk": inputs["L0_attn_Wk"],
        "bk": inputs["L0_attn_bk"], "Wv": inputs["L0_attn_Wv"], "bv": inputs["L0_attn_bv"], "Wo": inputs["L0_attn_Wo"],
        "bo": inputs["L0_attn_bo"], "proj_t": _np.transpose(_np.asarray(inputs["L0_attn_projection"]), (0, 2, 1)),
        "router_t": _np.transpose(_np.asarray(inputs["L0_ffn_router_w"]), (1, 0)), "w1": inputs["L0_ffn_w1"],
        "w2": inputs["L0_ffn_w2"],
    }
    nc = _bacc.Bacc("TRN2", target_bir_lowering=False, num_devices=1)
    arrays, args = {}, []
    for name, value in layout.items():
        a = _np.ascontiguousarray(value)
        arrays[f"in_{name}_dram"] = a
        args.append(nc.dram_tensor(f"in_{name}_dram", a.shape, _mybir.dt.from_np(a.dtype), kind="ExternalInput").ap())
    args.append(nc.dram_tensor("out_0_dram", (B, S, D), _mybir.dt.float32, kind="ExternalOutput").ap())
    moe_attention(nc, *args)
    r = _run(nc, [arrays], core_ids=[0])
    return r.results[0]["out_0_dram"]
```

```python
from contextlib import ExitStack

import concourse.bass as bass
from concourse import mybir

P = 128
B, S, D = 8, 1024, 256
H, HD, F = 16, 16, 64
E, TOPK, FF = 8, 2, 1024
N = B * S
CAP = int(1.25 * N * TOPK / E) + 1
NT = S // P
HT = NT // 2
HS = HT * P
KC = D // P
PAIRS = H // 2
KVW = 2 * (HD + 1)
WCOLS = 3 * D + E

TS = 256
MT = (N * TOPK) // TS + E
RROWS = -(-CAP // TS) * TS
TRASH = E * RROWS
DUMP = TRASH + TS
META_ROWS = DUMP + N * TOPK
GRP = 8
XR = 4
NG = MT // GRP
assert MT % GRP == 0 and NG > 2

W_SCALE = 16.0
R_SCALE = 256.0
H_SCALE = 64.0
P_SCALE = 1.0 / 16.0
EPSF = 0.1 * P_SCALE
MAGIC = 1597463007.0

F32, F16, I32, U32 = mybir.dt.float32, mybir.dt.float16, mybir.dt.int32, mybir.dt.uint32
ALU = mybir.AluOpType
ACT = mybir.ActivationFunctionType
AX = mybir.AxisListType
PASSES = ((0, 0), (0, 1), (1, 0))

def prep(*names):
    return [("prep", n) for n in names]


def attn(*names):
    return [("attn", n) for n in names]


BODY = (attn("rank", "vsum", "kvT") + prep("xT0", "xT1") + attn("cn", "ab0", "ab1", "ab2", "ab3") + prep("xT2", "xT3")
        + attn("oT0", "oT1", "ab4", "ab5", "ab6", "ab7") + prep("v0", "v1", "nrm0", "v2", "nrmT0", "v3")
        + attn("out0", "out1", "oT2", "oT3") + prep("v4", "v5") + attn("out2", "out3") + prep("nrm1", "v6", "nrmT1", "v7"))
PREP = [u for u in BODY if u[0] == "prep"]
TAIL = [u for u in BODY if u[0] == "attn"]
PLAN = {"first": PREP, "body": BODY, "tail": TAIL}
PER = {"prep": len(PREP), "attn": len(TAIL)}
NTH = {use: n + 1 for part in (PREP, TAIL) for n, use in enumerate(part)}
SMALL_BANKS = 3
BIG_BANKS = 4
assert len(BODY) % SMALL_BANKS == 0
ACT_READS = {"xT0", "xT1", "xT2", "xT3", "oT0", "oT1", "oT2", "oT3", "nrm0", "nrm1", "vsum", "cn"}
QK_USES, FEAT_USES, QF_USES = 2 * 4, 2 * NT + 2 * PAIRS, 2 * PAIRS


def reader(name):
    return "act" if name in ACT_READS else "dve"


def reads(use, b):
    same = [u for u in (PREP if use[0] == "prep" else TAIL) if reader(u[1]) == reader(use[1])]
    return b * len(same) + same.index(use) + 1


def small_use(phase, use, b):
    plan = PLAN[phase]
    n = plan.index(use)
    nth = n if phase == "first" else n + len(PREP)
    if n >= SMALL_BANKS:
        before = plan[n - SMALL_BANKS]
        gap = (before[0] == "prep") - (use[0] == "prep")
        return nth % SMALL_BANKS, before, b + gap
    if phase == "first":
        return nth % SMALL_BANKS, None, None
    before = (PREP if isinstance(b, int) and b == 0 else BODY)[n - SMALL_BANKS]
    return nth % SMALL_BANKS, before, b if before[0] == "prep" else b - 1


class Chain:

    def __init__(self, sem, per):
        self.sem, self.per = sem, per

    def start(self, eng, b):
        self.eng, self.base, self.n = eng, b * self.per, 0

    def step(self, ins):
        self.n += 1
        ins.then_inc(self.sem, 1)

    def wait(self):
        self.eng.wait_ge(self.sem, self.base + self.n)

    def link(self, ins):
        self.step(ins)
        self.wait()

    def end(self):
        assert self.n == self.per, (self.n, self.per)


def moe_attention(nc, x, Wq, bq, Wk, bk, Wv, bv, Wo, bo, proj_t, router_t, w1, w2, out):
    xrows = x.rearrange("b s d -> (b s) d")
    orows = out.rearrange("b s d -> (b s) d")
    xs = nc.dram_tensor("xn_split", [N + P, 2 * D], F16, kind="Internal").ap()
    meta = nc.dram_tensor("slot_table", [META_ROWS, 2], I32, kind="Internal").ap()
    wsplit = nc.dram_tensor("experts_split", [E, P, 4, 2, 1024], F16, kind="Internal").ap()

    with ExitStack() as ctx:
        def sb(name, shape, dt):
            return ctx.enter_context(nc.sbuf_tensor(name, shape, dt))

        def sem(name):
            return ctx.enter_context(nc.semaphore(name))

        bank = [ctx.enter_context(nc.psum_tensor(f"bank{i}", [P, 512], F32)) for i in range(8)]
        small = [bank[0], bank[1], bank[6]]
        big = bank[2:6]
        kvbank = bank[7]

        w_hl = sb("w_hl", [P, 2, KC, WCOLS], F16)
        wo_hl = sb("wo_hl", [P, 2, KC, D], F16)
        p_hl = sb("p_hl", [P, 2, KC, 512], F16)
        ident16 = sb("ident16", [P, P], F16)
        ident32 = sb("ident32", [P, P], F32)
        tri = sb("tri", [P, P], F16)
        ones16 = sb("ones16", [P, P], F16)
        cfeat = sb("cfeat", [P, P], F32)
        hsel = sb("hsel", [P, 32], F32)
        iota_e = sb("iota_e", [P, E], F32)
        iota_i = sb("iota_i", [P, 256], I32)
        tok_f = sb("tok_f", [P, NT], F32)
        dump_f = sb("dump_f", [P, 2, NT], F32)
        bqk = sb("bqk", [P, 2, KC], F32)
        bv_b = sb("bv_b", [P, D], F32)
        bo_b = sb("bo_b", [P, D], F32)
        carry = sb("carry", [P, E], F32)
        mt = sb("mt", [P, GRP, 2, 2], I32)
        tab = sb("tab", [1, 2, MT], I32)
        xg = sb("xg", [P, XR, 2, 2 * D], F16)
        AREA = 16384 + 166528
        EXPERT = 4 * 2 * 1024
        area = sb("area", [P, AREA // 4], F32)
        cursor = [EXPERT // 2]

        def view(shape, dt):
            n = 1
            for k in shape:
                n *= k
            words = n * (2 if dt == F16 else 4) // 4
            a = area[:, cursor[0]:cursor[0] + words]
            cursor[0] += words
            assert cursor[0] * 4 <= AREA, cursor[0] * 4
            if dt != F32:
                a = a.bitcast(dt)
            names = "abcd"[:len(shape)]
            if len(shape) > 1:
                a = a.rearrange(f"p ({' '.join(names)}) -> p {' '.join(names)}", **dict(zip(names, shape)))
            return a

        x_in = [view([HT, D], F32) for _ in range(2)]
        xn = view([HT, D], F32)
        xhl = [view([HT, 2, D], F16) for _ in range(2)]
        xT = [view([2 * KC, HS], F16) for _ in range(2)]
        q32 = [view([HS], F32) for _ in range(2)]
        q_hl = [view([KC, 2, HS], F16) for _ in range(2)]
        k_hl = [view([KC, 2, HS], F16) for _ in range(2)]
        sq = view([2, KC, HS], F32)
        v32 = view([NT, D], F32)
        vp = view([NT, H, 32], F32)
        vsum = view([H, HD + 1], F32)
        resid = view([NT, D], F32)
        rk = [view([KC, 512], F32) for _ in range(2)]
        rq = view([PAIRS, 2, HS], F16)
        kvt = view([256], F32)
        cs_b = view([H, HD + 1], F32)
        kvf = view([PAIRS, KVW], F32)
        kv_hl = view([2, PAIRS, KVW], F16)
        cn_b = view([H, HD + 1], F32)
        nT = view([HS], F32)
        nsq = view([HT, 4, 8], F32)
        ny = view([HT, 4, 8], F32)
        nu = view([HT, 4, 8], F32)
        norm = view([2, HT, 4, 8], F32)
        rn = view([HT, 2, 8], F32)
        nd = view([HT, H, HD + 1], F32)
        dn = view([HT, H], F32)
        o_hl = view([HT, 2, D], F16)
        oT = view([HT, 2 * KC, P], F16)
        osb = [view([2, D], F32) for _ in range(2)]
        w_raw = [view([1024], F32) for _ in range(2)]
        w_st = [view([2, 1024], F16) for _ in range(2)]
        bn = view([NT, 6], F32)
        mv = view([NT, 2], F32)
        va = view([NT], F32)
        vy = view([NT], F32)
        vu = view([NT], F32)
        lg = view([NT, E], F32)
        mx = view([NT, 8], F32)
        mi = view([NT, 8], U32)
        ix = view([2, NT], F32)
        oh = view([2, NT, E], F32)
        m16 = view([NT + 1, E], F16)
        rank = view([NT, E], F32)
        rsel = view([2, NT, E], F32)
        rpos = view([2, NT], F32)
        keep = view([2, NT], F32)
        slot = view([2, NT], F32)
        dl = view([NT], F32)
        eg = view([NT], F32)
        gate = view([2, NT], F32)
        slot_i = view([2, NT], I32)
        rec = view([2, NT, 2], I32)
        tb = v32.rearrange("p a b -> p (a b)")
        vtmp = view([4, D], F32)
        stage = rq.rearrange("p a b c -> p (a b c)").bitcast(F32)
        raw_w = stage[:, 0:KC * WCOLS].rearrange("p (k n) -> p k n", k=KC)
        raw_o = stage[:, KC * WCOLS:KC * (WCOLS + D)].rearrange("p (k n) -> p k n", k=KC)
        raw_p = stage[:, KC * (WCOLS + D):KC * (WCOLS + D + 512)].rearrange("p (m n) -> p m n", m=KC)
        clear = rk[0].rearrange("p a b -> p (a b)").bitcast(I32)[:, 0:2 * DUMP // P]
        zero_rows = rk[1].rearrange("p a b -> p (a b)").bitcast(F16)[:, 0:2 * D]
        tok_i = lg.bitcast(I32)[:, 0, 0:NT]
        dump_i = oh.bitcast(I32)[:, :, 0, :]

        we = area[:, 0:E * EXPERT // 2].bitcast(F16)
        cursor[0] = E * EXPERT // 2
        moe_xT = [view([2 * KC, TS], F16) for _ in range(2)]
        h32 = [view([2, TS], F32) for _ in range(4)]
        hT = [view([FF // P, 2, TS], F16) for _ in range(2)]
        y_sb = [view([2, D], F32) for _ in range(2)]

        weights_loaded = sem("weights_loaded")
        proj_zeroed = sem("proj_zeroed")
        proj_loaded = sem("proj_loaded")
        masks_made = sem("masks_made")
        consts_ready = sem("consts_ready")
        x_plus_xn = sem("x_plus_xn")
        zero_stored = sem("zero_stored")
        pool_prep = sem("pool_prep")
        pool_first = sem("pool_first")
        dve_first = sem("dve_first")
        slots_cleared = sem("slots_cleared")
        x_loaded = [sem(f"x_loaded{i}") for i in range(2)]
        xn_split = sem("xn_split")
        xl_split = sem("xl_split")
        resid_ready = sem("resid_ready")
        xn_ready = sem("xn_ready")
        xs_stored = [sem(f"xs_stored{i}") for i in range(2)]
        prep_filled, attn_filled = sem("prep_filled"), sem("attn_filled")
        prep_read, attn_read = sem("prep_read"), sem("attn_read")
        prep_taken, attn_taken = sem("prep_taken"), sem("attn_taken")
        filled = {"prep": prep_filled, "attn": attn_filled}
        read = {("prep", "dve"): prep_read, ("attn", "dve"): attn_read, ("prep", "act"): prep_taken, ("attn", "act"): attn_taken}
        qk_filled = sem("qk_filled")
        qk_read = sem("qk_read")
        qk_squared = sem("qk_squared")
        qk_split = sem("qk_split")
        vp_ready = sem("vp_ready")
        vsum_ready = sem("vsum_ready")
        feat_filled = sem("feat_filled")
        feat_relu = sem("feat_relu")
        qf_split = sem("qf_split")
        kv_tile_done = sem("kv_tile_done")
        kvt_copied = sem("kvt_copied")
        kvf_ready = sem("kvf_ready")
        kv_split = sem("kv_split")
        masks_ready = sem("masks_ready")
        gate_in, gate_exp = sem("gate_in"), sem("gate_exp")
        slots_ready = sem("slots_ready")
        table_cleared = sem("table_cleared")
        meta_stored = sem("meta_stored")
        o_ready, o_high = sem("o_ready"), sem("o_high")
        o_split = sem("o_split")
        out_stored = [sem(f"out_stored{i}") for i in range(2)]
        w_in = [sem(f"w_in{i}") for i in range(2)]
        w_scaled, w_hi, w_lo = sem("w_scaled"), sem("w_hi"), sem("w_lo")
        w_out = [sem(f"w_out{i}") for i in range(2)]
        dve_prep, dve_attn, dve_table = sem("dve_prep"), sem("dve_attn"), sem("dve_table")
        tab_ready = sem("tab_ready")
        experts_in = sem("experts_in")
        meta_in = sem("meta_in")
        rows_in = [sem(f"rows_in{i}") for i in range(2)]
        mx_filled, mx_read = sem("mx_filled"), sem("mx_read")
        mh_filled, mh_silu = sem("mh_filled"), sem("mh_silu")
        mh_split = sem("mh_split")
        mh_step = sem("mh_step")
        my_filled, my_read = sem("my_filled"), sem("my_read")
        added = sem("added")

        block = ctx.enter_context(nc.Block())

        def small_ap(phase, part, name, b, eng=None):
            i, before, bb = small_use(phase, (part, name), b)
            if eng is not None and before is not None:
                eng.wait_ge(read[before[0], reader(before[1])], reads(before, bb))
            return small[i]

        def nth(part, name, b):
            return b * PER[part] + NTH[(part, name)]

        def wait_read(eng, part, name, b, wait=None):
            (wait or (lambda e, s_, v_: e.wait_ge(s_, v_)))(eng, read[part, reader(name)], reads((part, name), b))

        def f16(a):
            return a[:, :].bitcast(F16)

        def rows(ap, first, count):
            return ap[bass.ds(first, count), :]

        def hold(eng, s, value):
            if not isinstance(value, int):
                value = eng.to_reg(value)
            eng.wait_ge(consts_ready, 1)
            eng.wait_ge(s, value)

        w1_rows = w1.rearrange("e k f -> (e k) f")
        w2_rows = w2.rearrange("e f d -> (e f) d")
        ws_rows = wsplit.rearrange("e p c h n -> (e p) c (h n)")

        def w_load(sp, e, c):
            if c < 2:
                src = w1_rows[bass.ds(e * D + c * P, P), :]
                dst = w_raw[c % 2]
            else:
                src = w2_rows[bass.ds(e * FF + (c - 2) * 4 * P, 4 * P), :].rearrange("(c p) d -> p c d", p=P)
                dst = w_raw[c % 2].rearrange("p (c d) -> p c d", c=4)
            if c >= 2:
                hold(sp, w_lo, e * 4 + c - 1)
            sp.dma_start(dst, src).then_inc(w_in[c % 2], 16)

        def w_store(sp, e, c):
            dst = ws_rows[bass.ds(e * P, P), c, :]
            hold(sp, w_lo, e * 4 + c + 1)
            sp.dma_start(dst, w_st[c % 2].rearrange("p h n -> p (h n)")).then_inc(w_out[c % 2], 16)

        def x_load(sp, b, half):
            src = xrows[bass.ds(b * S + half * HS, HS), :].rearrange("(t p) d -> p t d", p=P)
            hold(sp, resid_ready, (b - 1) * 2 + half + 1)
            sp.dma_start(x_in[half], src).then_inc(x_loaded[half], 16)

        def xs_store(sp, b, half):
            dst = xs[bass.ds(b * S + half * HS, HS), :].rearrange("(t p) n -> p t n", p=P)
            hold(sp, xl_split, b * 2 + half + 1)
            sp.dma_start(dst, xhl[half].rearrange("p t h n -> p t (h n)")).then_inc(xs_stored[half], 16)

        def out_store(sp, b, k):
            dst = orows[bass.ds(b * S + k * 2 * P, 2 * P), :].rearrange("(t p) d -> p t d", p=P)
            wait_read(sp, "attn", f"out{k}", b, hold)
            sp.dma_start(dst, osb[k % 2]).then_inc(out_stored[k % 2], 16)

        def sp_turn(sp, b, phase, x_next=True):
            body = phase == "body"
            if body:
                xs_store(sp, b + 1, 0)
            w_store(sp, b, 0)
            w_load(sp, b, 2)
            if body:
                xs_store(sp, b + 1, 1)
            w_store(sp, b, 1)
            w_load(sp, b, 3)
            w_store(sp, b, 2)
            if body:
                w_load(sp, b + 1, 0)
            out_store(sp, b, 0)
            out_store(sp, b, 1)
            if body and x_next:
                x_load(sp, b + 2, 0)
            w_store(sp, b, 3)
            if body:
                w_load(sp, b + 1, 1)
            out_store(sp, b, 2)
            out_store(sp, b, 3)
            if body and x_next:
                x_load(sp, b + 2, 1)

        @block.sync
        def _(sp):
            for half in range(2):
                sp.dma_start(x_in[half], xrows[half * HS:(half + 1) * HS, :].rearrange("(t p) d -> p t d", p=P)) \
                    .then_inc(x_loaded[half], 16)
            for n, w in enumerate((Wq, Wk, Wv)):
                sp.dma_start(raw_w[:, :, n * D:(n + 1) * D], w.rearrange("(k p) n -> p k n", p=P)).then_inc(weights_loaded, 16)
            sp.dma_start(raw_w[:, :, 3 * D:], router_t.rearrange("(k p) n -> p k n", p=P)).then_inc(weights_loaded, 16)
            sp.dma_start(raw_o, Wo.rearrange("(k p) n -> p k n", p=P)).then_inc(weights_loaded, 16)
            for dst, v_ in ((bv_b, bv), (bo_b, bo)):
                sp.dma_start(dst[:, :], v_.rearrange("(a n) -> a n", a=1).broadcast_to([P, D])).then_inc(weights_loaded, 16)
            for n, v_ in enumerate((bq, bk)):
                sp.dma_start(bqk[:, n, :], v_.rearrange("(k p) -> p k", p=P),
                             allow_slow_non_contiguous=True).then_inc(weights_loaded, 16)
            sp.wait_ge(proj_zeroed, 1)
            for h in range(H):
                m, l = h // 8, h % 8
                sp.dma_start(raw_p[l * HD:(l + 1) * HD, m, l * F:(l + 1) * F], proj_t[h]).then_inc(proj_loaded, 16)
            sp.wait_ge(slots_cleared, 1)
            sp.dma_start(meta[0:DUMP, :].rearrange("(p a) c -> p (a c)", p=P), clear[:, 0:2 * DUMP // P]).then_inc(table_cleared, 16)
            sp.dma_start(xs[N:N + P, :], zero_rows).then_inc(zero_stored, 16)
            sp.wait_ge(consts_ready, 1)
            for half in range(2):
                xs_store(sp, 0, half)
                x_load(sp, 1, half)
                w_load(sp, 0, half)
            sp_turn(sp, 0, "body")
            with sp.Fori(1, B - 2) as b:
                sp_turn(sp, b, "body")
            sp_turn(sp, B - 2, "body", x_next=False)
            for n in range(2):
                sp.wait_ge(w_out[n], 16 * 2 * (E - 1))
            for e in range(E):
                if e == 1:
                    sp_turn(sp, B - 1, "tail")
                    for n in range(2):
                        sp.wait_ge(w_out[n], 16 * 2 * E)
                    wait_read(sp, "attn", "out3", B - 1)
                    for n in range(2):
                        sp.wait_ge(out_stored[n], 16 * 2 * B)
                    sp.wait_ge(meta_stored, 16 * TOPK * NT * B)
                    sp.wait_ge(tab_ready, 1)
                if e > 0:
                    sp.wait_ge(experts_in, 16 * e)
                sp.dma_start(we[:, e * EXPERT:(e + 1) * EXPERT],
                             wsplit[e].rearrange("p c h n -> p (c h n)")).then_inc(experts_in, 16)
            sp.wait_ge(experts_in, 16 * E)

        def w_high(act, e, c, first=False):
            hold(act, w_in[c % 2], (e * 2 + c // 2 + 1) * 16)
            if not (first and c < 2):
                hold(act, w_out[c % 2], (e * 2 + c // 2) * 16)
            nc.scalar.activation(w_raw[c % 2], w_raw[c % 2], ACT.Copy, scale=R_SCALE).then_inc(w_scaled, 1)
            hold(act, w_scaled, e * 4 + c + 1)
            nc.scalar.activation(w_st[c % 2][:, 0, :], w_raw[c % 2], ACT.Copy).then_inc(w_hi, 1)

        def qk_read_half(act, b, half, n0=0, n1=4):
            for n in range(n0, n1):
                t = half * 4 + n
                side, m = n // 2, n % 2
                act.wait_ge(qk_filled, b * QK_USES + t + 1)
                if t >= 2:
                    act.wait_ge(qk_split, b * QK_USES + t - 1)
                elif not isinstance(b, int) or b > 0:
                    act.wait_ge(qk_split, (b - 1) * QK_USES + t + 7)
                nc.scalar.activation(q32[n % 2], big[n % BIG_BANKS][:, :], ACT.Identity, bias=bqk[:, side, m:m + 1],
                                     scale=1.0 / W_SCALE).then_inc(qk_read, 1)
                act.wait_ge(qk_read, b * QK_USES + t + 1)
                nc.scalar.activation(sq[:, side, m, :], q32[n % 2], ACT.Square).then_inc(qk_squared, 1)

        def k_relu(act, b, t):
            for m in range(KC):
                n = t * KC + m
                act.wait_ge(feat_filled, b * FEAT_USES + n + 1)
                if m == 0 and t >= 2:
                    act.wait_ge(kv_tile_done, b * NT + t - 1)
                nc.scalar.activation(rk[t % 2][:, m, :], big[n % BIG_BANKS][:, :], ACT.Relu).then_inc(feat_relu, 1)

        def q_relu(act, b, half):
            for p_ in range(PAIRS):
                n = 2 * NT + half * PAIRS + p_
                act.wait_ge(feat_filled, b * FEAT_USES + n + 1)
                nc.scalar.activation(rq[:, p_, 0, :], big[n % BIG_BANKS][:, :], ACT.Relu).then_inc(feat_relu, 1)

        def take(act, phase, part, name, b):
            act.wait_ge(filled[part], nth(part, name, b))
            return small_ap(phase, part, name, b)

        def xn_high(act, b, half, first=False):
            if not first:
                hold(act, xs_stored[half], b * 16)
            act.wait_ge(xn_ready, b * 2 + half + 1)
            nc.scalar.copy(xhl[half][:, :, 0, :], xn).then_inc(xn_split, 1)

        def xT_copy(act, phase, b, half):
            for j in range(2):
                src = f16(take(act, phase, "prep", f"xT{2 * half + j}", b)).rearrange("p (t c q) -> p c t q", t=2, c=4)
                dst = xT[half].rearrange("p c (t q) -> p c t q", q=P)[:, :, 2 * j:2 * j + 2, :]
                nc.scalar.copy(dst, src).then_inc(prep_taken, 1)

        def squares_copy(act, phase, b, half):
            nc.scalar.copy(nT, take(act, phase, "prep", f"nrm{half}", b)[:, :]).then_inc(prep_taken, 1)

        def o_hi(act, b, half):
            act.wait_ge(o_ready, b * 2 + half + 1)
            nc.scalar.copy(o_hl.rearrange("p t l (h d) -> p l t h d", h=H)[:, 0], nd[:, :, :, 0:HD]).then_inc(o_high, 1)

        def oT_copy(act, phase, b, half):
            for j in range(2):
                src = f16(take(act, phase, "attn", f"oT{2 * half + j}", b)).rearrange("p (t c q) -> p t c q", t=2, c=4)
                nc.scalar.copy(oT[:, 2 * j:2 * j + 2], src).then_inc(attn_taken, 1)

        def act_turn(act, b, phase, first=False):
            body = phase == "body"
            for t in range(2):
                k_relu(act, b, t)
            w_high(act, b, 0, first)
            for t in range(2, 4):
                k_relu(act, b, t)
            act.wait_ge(gate_in, b + 1)
            nc.scalar.activation(eg, dl, ACT.Exp, scale=1.0 / R_SCALE).then_inc(gate_exp, 1)
            for t in range(4, 6):
                k_relu(act, b, t)
            w_high(act, b, 1, first)
            for t in range(6, NT):
                k_relu(act, b, t)
            if body:
                xn_high(act, b + 1, 0)
            nc.scalar.copy(cs_b.rearrange("p h d -> p (h d)"), take(act, phase, "attn", "vsum", b)[:, 0:H * (HD + 1)]) \
                .then_inc(attn_taken, 1)
            q_relu(act, b, 0)
            if body:
                xT_copy(act, phase, b + 1, 0)
            nc.scalar.copy(cn_b.rearrange("p h d -> p (h d)"), take(act, phase, "attn", "cn", b)[:, 0:H * (HD + 1)]) \
                .then_inc(attn_taken, 1)
            if body:
                xn_high(act, b + 1, 1)
            w_high(act, b, 2)
            q_relu(act, b, 1)
            if body:
                xT_copy(act, phase, b + 1, 1)
                qk_read_half(act, b + 1, 0, 0, 2)
            o_hi(act, b, 0)
            if body:
                qk_read_half(act, b + 1, 0, 2, 4)
            oT_copy(act, phase, b, 0)
            if body:
                squares_copy(act, phase, b + 1, 0)
            w_high(act, b, 3)
            o_hi(act, b, 1)
            if body:
                qk_read_half(act, b + 1, 1, 0, 2)
            oT_copy(act, phase, b, 1)
            if body:
                qk_read_half(act, b + 1, 1, 2, 4)
                squares_copy(act, phase, b + 1, 1)

        def silu(act, t, u, first):
            for j in range(4):
                act.wait_ge(mh_filled, t * 4 + j + 1)
                if not first:
                    act.wait_ge(mh_split, t * 4 + j - 3)
                nc.scalar.activation(h32[j].rearrange("p a b -> p (a b)"), big[j][:, :], ACT.Silu,
                                     scale=1.0 / R_SCALE).then_inc(mh_silu, 1)

        def y_scale(act, t, u, first):
            act.wait_ge(my_filled, t + 1)
            if not first:
                act.wait_ge(added, (t - 1) * 32)
            yb = bank[6 + u % 2]
            for a in range(2):
                nc.scalar.activation(y_sb[u % 2][:, a, :], yb[:, a * D:(a + 1) * D], ACT.Copy,
                                     scale=mt[:, u % GRP, a, 1:2].bitcast(F32)).then_inc(my_read, 1)

        @block.scalar
        def _(act):
            act.wait_ge(consts_ready, 1)
            for half in range(2):
                xn_high(act, 0, half, first=True)
                xT_copy(act, "first", 0, half)
            qk_read_half(act, 0, 0)
            squares_copy(act, "first", 0, 0)
            qk_read_half(act, 0, 1)
            squares_copy(act, "first", 0, 1)
            act_turn(act, 0, "body", first=True)
            with act.Fori(1, B - 1) as b:
                act_turn(act, b, "body")
            act_turn(act, B - 1, "tail")
            wait_read(act, "attn", "out3", B - 1)
            for n in range(2):
                act.wait_ge(out_stored[n], 16 * 2 * B)
                act.wait_ge(w_out[n], 16 * 2 * E)

            def group(g, first=False):
                for u in range(GRP):
                    silu(act, g * GRP + u, u, first and u == 0)
                    if not (first and u == 0):
                        y_scale(act, g * GRP + u - 1, u - 1 + GRP, first and u <= 2)

            group(0, first=True)
            with act.Fori(1, NG) as g:
                group(g)
            y_scale(act, MT - 1, GRP - 1, False)

        def qk_project(pe, b, half, first):
            for n in range(4):
                t = half * 4 + n
                side, m = n // 2, n % 2
                if half == 1:
                    pe.wait_ge(qk_read, b * QK_USES + n + 1)
                elif not first:
                    pe.wait_ge(qf_split, (b - 1) * QF_USES + 12 + n + 1)
                if n == 0:
                    wait_read(pe, "prep", f"xT{2 * half + 1}", b)
                for i, (wl, xl) in enumerate(PASSES):
                    for k in range(KC):
                        c0 = side * D + m * P
                        mm = nc.tensor.matmul(big[n][:, :], w_hl[:, wl, k, c0:c0 + P], xT[half][:, xl * KC + k, :],
                                              start=(i == 0 and k == 0), stop=(i == 2 and k == KC - 1))
                mm.then_inc(qk_filled, 1)

        def x_transpose(pe, phase, b, half):
            pe.wait_ge(xl_split, b * 2 + half + 1)
            for j in range(2):
                dst = f16(small_ap(phase, "prep", f"xT{2 * half + j}", b, pe)).rearrange("p (t c q) -> p t c q", t=2, c=4)
                if j == 0:
                    pe.wait_ge(xn_split, b * 2 + half + 1)
                for tl in range(2):
                    for hl in range(2):
                        for k in range(KC):
                            mm = nc.tensor.transpose(dst[:, tl, hl * KC + k, :],
                                                     xhl[half][:, 2 * j + tl, hl, k * P:(k + 1) * P], ident16[:, :])
                mm.then_inc(prep_filled, 1)

        def v_project(pe, phase, b, t):
            half, tl = t // HT, t % HT
            dst = small_ap(phase, "prep", f"v{t}", b, pe)
            for i, (xl, wl) in enumerate(PASSES):
                for k in range(KC):
                    mm = nc.tensor.matmul(dst[:, 0:D + E], xT[half][:, xl * KC + k, tl * P:(tl + 1) * P],
                                          w_hl[:, wl, k, 2 * D:], start=(i == 0 and k == 0), stop=(i == 2 and k == KC - 1))
            mm.then_inc(prep_filled, 1)

        def square_sums(pe, phase, b, half):
            dst = small_ap(phase, "prep", f"nrm{half}", b, pe)
            pe.wait_ge(qk_squared, b * QK_USES + half * 4 + 4)
            for g in range(4):
                mm = nc.tensor.matmul(dst[32 * g:32 * g + 32, :], hsel[:, :], sq[:, g // 2, g % 2, :], start=True, stop=True)
            mm.then_inc(prep_filled, 1)

        def square_turn(pe, phase, b, half):
            dst = small_ap(phase, "prep", f"nrmT{half}", b, pe)
            wait_read(pe, "prep", f"nrm{half}", b)
            for t in range(HT):
                mm = nc.tensor.transpose(dst[:, t * P:(t + 1) * P], nT[:, t * P:(t + 1) * P], ident32[:, :])
            mm.then_inc(prep_filled, 1)

        def k_features(pe, b, t):
            half, tl = t // HT, t % HT
            for m in range(KC):
                n = t * KC + m
                if n < BIG_BANKS:
                    pe.wait_ge(qk_read, b * QK_USES + 4 + n + 1)
                else:
                    pe.wait_ge(feat_relu, b * FEAT_USES + n - BIG_BANKS + 1)
                if n == 0 or n == 2 * HT:
                    pe.wait_ge(qk_split, b * QK_USES + half * 4 + 4)
                for i, (kl, pl) in enumerate(PASSES):
                    mm = nc.tensor.matmul(big[n % BIG_BANKS][:, :], k_hl[half][:, m, kl, tl * P:(tl + 1) * P],
                                          p_hl[:, pl, m, :], start=(i == 0), stop=(i == 2))
                mm.then_inc(feat_filled, 1)

        def kv_sum(pe, b, t):
            pe.wait_ge(feat_relu, b * FEAT_USES + t * KC + 2)
            if t % HT == 0:
                pe.wait_ge(vp_ready, b * 2 + t // HT + 1)
            for m in range(KC):
                for s in range(2):
                    for j in range(4):
                        h = 8 * m + 2 * j + s
                        c = 2 * m + s
                        mm = nc.tensor.matmul(kvbank[32 * j:32 * j + 32, c * F:(c + 1) * F], vp[:, t, h, :],
                                              rk[t % 2][:, m, (2 * j + s) * F:(2 * j + s + 1) * F],
                                              start=(t == 0 and c == 0), stop=(t == NT - 1), skip_group_check=True)
            mm.then_inc(kv_tile_done, 1)

        def q_features(pe, b, half, p0, p1):
            for p_ in range(p0, p1):
                n = 2 * NT + half * PAIRS + p_
                m, j = p_ // 4, p_ % 4
                if half == 0 and p_ < BIG_BANKS:
                    pe.wait_ge(feat_relu, b * FEAT_USES + n - BIG_BANKS + 1)
                else:
                    pe.wait_ge(qf_split, b * QF_USES + n - 2 * NT - BIG_BANKS + 1)
                for i, (pl, ql) in enumerate(PASSES):
                    mm = nc.tensor.matmul(big[n % BIG_BANKS][:, :], p_hl[:, pl, m, j * P:(j + 1) * P],
                                          q_hl[half][:, m, ql, :], start=(i == 0), stop=(i == 2))
                mm.then_inc(feat_filled, 1)

        def attend(pe, phase, b, t):
            half, tl = t // HT, t % HT
            dst = small_ap(phase, "attn", f"ab{t}", b, pe)
            if tl == 0:
                pe.wait_ge(qf_split, b * QF_USES + (half + 1) * PAIRS)
                pe.wait_ge(kv_split, b + 1)
            for p_ in range(PAIRS):
                for i, (rl, kl) in enumerate(PASSES):
                    mm = nc.tensor.matmul(dst[:, p_ * KVW:(p_ + 1) * KVW], rq[:, p_, rl, tl * P:(tl + 1) * P],
                                          kv_hl[:, kl, p_, :], start=(i == 0), stop=(i == 2))
            mm.then_inc(attn_filled, 1)

        def o_transpose(pe, phase, b, half):
            for j in range(2):
                dst = f16(small_ap(phase, "attn", f"oT{2 * half + j}", b, pe)).rearrange("p (t c q) -> p t c q", t=2, c=4)
                if j == 0:
                    pe.wait_ge(o_split, b * 2 + half + 1)
                for tl in range(2):
                    for hl in range(2):
                        for m in range(KC):
                            mm = nc.tensor.transpose(dst[:, tl, hl * KC + m, :],
                                                     o_hl[:, 2 * j + tl, hl, m * P:(m + 1) * P], ident16[:, :])
                mm.then_inc(attn_filled, 1)

        def o_project(pe, phase, b, half):
            for j in range(2):
                dst = small_ap(phase, "attn", f"out{2 * half + j}", b, pe)
                wait_read(pe, "attn", f"oT{2 * half + j}", b)
                for tl in range(2):
                    for i, (ol, wl) in enumerate(PASSES):
                        for m in range(KC):
                            mm = nc.tensor.matmul(dst[:, tl * D:(tl + 1) * D], oT[:, 2 * j + tl, ol * KC + m, :],
                                                  wo_hl[:, wl, m, :], start=(i == 0 and m == 0), stop=(i == 2 and m == KC - 1))
                mm.then_inc(attn_filled, 1)

        def pe_turn(pe, b, phase):
            body = phase == "body"
            k_features(pe, b, 0)
            for t in range(1, NT):
                k_features(pe, b, t)
                kv_sum(pe, b, t - 1)
            dst = small_ap(phase, "attn", "rank", b, pe)
            pe.wait_ge(masks_ready, b + 1)
            m16f = m16.rearrange("p t e -> p (t e)")
            nc.tensor.matmul(dst[:, 0:(NT + 1) * E], tri[:, :], m16f, start=True, stop=False, skip_group_check=True)
            for s in range(1, NT + 1):
                mm = nc.tensor.matmul(dst[:, s * E:(NT + 1) * E], ones16[:, :], m16f[:, 0:(NT + 1 - s) * E],
                                      start=False, stop=(s == NT), skip_group_check=True)
            mm.then_inc(attn_filled, 1)
            dst = small_ap(phase, "attn", "vsum", b, pe)
            pe.wait_ge(vsum_ready, b + 1)
            nc.tensor.matmul(dst[:, 0:H * (HD + 1)], cfeat[:, :], vsum.rearrange("p h d -> p (h d)"),
                             start=True, stop=True).then_inc(attn_filled, 1)
            kv_sum(pe, b, NT - 1)
            q_features(pe, b, 0, 0, 2)
            dst = small_ap(phase, "attn", "kvT", b, pe)
            pe.wait_ge(kvt_copied, b + 1)
            for m in range(KC):
                mm = nc.tensor.transpose(dst[:, m * P:(m + 1) * P], kvt[:, m * P:(m + 1) * P], ident32[:, :])
            mm.then_inc(attn_filled, 1)
            q_features(pe, b, 0, 2, PAIRS)
            if body:
                x_transpose(pe, phase, b + 1, 0)
            dst = small_ap(phase, "attn", "cn", b, pe)
            pe.wait_ge(kvf_ready, b + 1)
            nc.tensor.matmul(dst[:, 0:PAIRS * KVW], cfeat[:, :], kvf.rearrange("p a c -> p (a c)"),
                             start=True, stop=True).then_inc(attn_filled, 1)
            for t in range(HT):
                attend(pe, phase, b, t)
            q_features(pe, b, 1, 0, PAIRS)
            if body:
                x_transpose(pe, phase, b + 1, 1)
                qk_project(pe, b + 1, 0, False)
            o_transpose(pe, phase, b, 0)
            for t in range(HT, NT):
                attend(pe, phase, b, t)
            if body:
                v_and_squares(pe, phase, b + 1, 0)
            o_project(pe, phase, b, 0)
            if body:
                qk_project(pe, b + 1, 1, False)
            o_transpose(pe, phase, b, 1)
            if body:
                v_and_squares(pe, phase, b + 1, 1, attended=b)
            else:
                o_project(pe, phase, b, 1)

        def v_and_squares(pe, phase, b, half, attended=None):
            v_project(pe, phase, b, half * HT)
            v_project(pe, phase, b, half * HT + 1)
            if attended is not None:
                o_project(pe, phase, attended, 1)
            square_sums(pe, phase, b, half)
            v_project(pe, phase, b, half * HT + 2)
            square_turn(pe, phase, b, half)
            v_project(pe, phase, b, half * HT + 3)

        def rows_transpose(pe, g, u):
            dst = f16(bank[u % 2]).rearrange("p (c q) -> p c q", c=2 * KC)
            pe.wait_ge(rows_in[u % 2], (g * (GRP // 2) + u // 2 + 1) * 32)
            for a in range(2):
                for c in range(2 * KC):
                    mm = nc.tensor.transpose(dst[:, c, a * P:(a + 1) * P], xg[:, u % XR, a, c * P:(c + 1) * P], ident16[:, :])
            mm.then_inc(mx_filled, 1)

        def hidden(pe, t, u, first):
            e = pe.value_load(tab[0:1, 0, bass.ds(t, 1)], min_val=0, max_val=E - 1)
            hold(pe, experts_in, e * 16 + 16)
            pe.wait_ge(mx_read, t + 1)
            for j in range(4):
                if not first:
                    pe.wait_ge(mh_silu, t * 4 + j - 3)
                for i2 in range(2):
                    c = 2 * j + i2
                    for i, (wl, xl) in enumerate(PASSES):
                        for k in range(KC):
                            mm = nc.tensor.matmul(
                                big[j][:, i2 * TS:(i2 + 1) * TS],
                                we[:, bass.ds(e * EXPERT + (k * 2048 + wl * 1024 + c * P), P)],
                                moe_xT[u % 2][:, xl * KC + k, :], start=(i == 0 and k == 0), stop=(i == 2 and k == KC - 1))
                mm.then_inc(mh_filled, 1)

        def expert_out(pe, t, u, first):
            e = pe.value_load(tab[0:1, 0, bass.ds(t, 1)], min_val=0, max_val=E - 1)
            pe.wait_ge(mh_split, t * 4 + 4)
            if not first:
                pe.wait_ge(my_read, t * 2 - 2)
            yb = bank[6 + u % 2]
            for a in range(2):
                for c in range(FF // P):
                    for i, (hl, wl) in enumerate(PASSES):
                        off = (2 + c // 4) * 2048 + wl * 1024 + (c % 4) * D
                        mm = nc.tensor.matmul(yb[:, a * D:(a + 1) * D], hT[u % 2][:, c, hl, a * P:(a + 1) * P],
                                              we[:, bass.ds(e * EXPERT + off, D)],
                                              start=(c == 0 and i == 0), stop=(c == FF // P - 1 and i == 2))
            mm.then_inc(my_filled, 1)

        @block.tensor
        def _(pe):
            pe.wait_ge(consts_ready, 1)
            x_transpose(pe, "first", 0, 0)
            x_transpose(pe, "first", 0, 1)
            for half in range(2):
                qk_project(pe, 0, half, True)
                v_and_squares(pe, "first", 0, half)
            pe_turn(pe, 0, "body")
            with pe.Fori(1, B - 1) as b:
                pe_turn(pe, b, "body")
            pe_turn(pe, B - 1, "tail")
            wait_read(pe, "attn", "out3", B - 1)
            pe.wait_ge(tab_ready, 1)

            def group(g, first=False, last=False):
                for u in range(GRP):
                    t = g * GRP + u
                    hidden(pe, t, u, first and u == 0)
                    if not (last and u == GRP - 1):
                        rows_transpose(pe, g, u + 1)
                    if not (first and u == 0):
                        expert_out(pe, t - 1, u - 1 + GRP, first and u <= 2)

            rows_transpose(pe, 0, 0)
            group(0, first=True)
            with pe.Fori(1, NG - 1) as g:
                group(g)
            group(NG - 1, last=True)
            expert_out(pe, MT - 1, GRP - 1, False)

        def w_low(pool, e, c):
            hold(pool, w_hi, e * 4 + c + 1)
            nc.gpsimd.tensor_tensor(w_st[c % 2][:, 1, :], w_raw[c % 2], w_st[c % 2][:, 0, :], ALU.subtract).then_inc(w_lo, 1)

        def x_low(pool, b, half):
            hold(pool, xn_split, b * 2 + half + 1)
            nc.gpsimd.tensor_tensor(xhl[half][:, :, 1, :], xn, xhl[half][:, :, 0, :], ALU.subtract).then_inc(xl_split, 1)
            nc.gpsimd.tensor_tensor(x_in[half], x_in[half], xn, ALU.add).then_inc(x_plus_xn, 1)

        def resid_sum(pool, b, half, first=False):
            if not first:
                wait_read(pool, "attn", f"out{2 * half + 1}", b - 1, hold)
            hold(pool, x_plus_xn, b * 2 + half + 1)
            nc.gpsimd.tensor_tensor(resid[:, half * HT:(half + 1) * HT, :], x_in[half],
                                    bo_b[:, :].rearrange("p (a d) -> p a d", a=1).broadcast_to([P, HT, D]),
                                    ALU.add).then_inc(resid_ready, 1)

        def v_total(pool, b):
            wait_read(pool, "prep", "v7", b, hold)
            nc.gpsimd.tensor_tensor(vtmp, v32[:, 0:4, :], v32[:, 4:8, :], ALU.add).then_inc(pool_prep, 1)
            hold(pool, pool_prep, b * 2 + 1)
            nc.gpsimd.tensor_tensor(vtmp[:, 0:2, :], vtmp[:, 0:2, :], vtmp[:, 2:4, :], ALU.add).then_inc(pool_prep, 1)
            hold(pool, pool_prep, b * 2 + 2)
            nc.gpsimd.tensor_tensor(vsum[:, :, 0:HD], vtmp[:, 0, :].rearrange("p (h d) -> p h d", h=H),
                                    vtmp[:, 1, :].rearrange("p (h d) -> p h d", h=H), ALU.add).then_inc(vsum_ready, 1)

        def scatter(pool, b):
            hold(pool, slots_ready, b + 1)
            for k in range(TOPK):
                for t in range(NT):
                    nc.gpsimd.indirect_dma_start(meta, bass.IndirectOffsetOnAxis(slot_i[:, k, t:t + 1], 0),
                                                 rec[:, k, t, :], None).then_inc(meta_stored, 16)

        def pool_turn(pool, b, phase):
            body = phase == "body"
            w_low(pool, b, 0)
            if body:
                x_low(pool, b + 1, 0)
            w_low(pool, b, 1)
            if body:
                x_low(pool, b + 1, 1)
            scatter(pool, b)
            w_low(pool, b, 2)
            if body:
                resid_sum(pool, b + 1, 0)
            w_low(pool, b, 3)
            if body:
                resid_sum(pool, b + 1, 1)
                v_total(pool, b + 1)

        @block.gpsimd
        def _(pool):
            g = nc.gpsimd
            ch = Chain(pool_first, 19)
            ch.start(pool, 0)
            ch.step(g.memset(clear, 0))
            ch.step(g.memset(zero_rows, 0.0))
            ch.wait()
            g.memset(clear.rearrange("p (a c) -> p a c", c=2)[:, :, 0:1], N).then_inc(slots_cleared, 1)
            ch.step(g.memset(ident16[:, :], 0.0))
            ch.step(g.memset(ident32[:, :], 0.0))
            ch.step(g.memset(tri[:, :], 1.0))
            ch.step(g.memset(ones16[:, :], 1.0))
            ch.step(g.memset(cfeat[:, :], EPSF))
            ch.step(g.memset(hsel[:, :], 1.0))
            ch.step(g.memset(vsum[:, :, HD:HD + 1], float(NT)))
            ch.wait()
            for m in (ident16, ident32):
                ch.step(g.affine_select(out=m[:, :], in_=m[:, :], compare_op=ALU.not_equal, fill=1.0, base=0,
                                        pattern=[[-1, P]], channel_multiplier=1))
            ch.step(g.affine_select(out=tri[:, :], in_=tri[:, :], compare_op=ALU.is_gt, fill=0.0, base=0,
                                    pattern=[[1, P]], channel_multiplier=-1))
            ch.link(g.affine_select(out=hsel[:, :], in_=hsel[:, :], compare_op=ALU.is_ge, fill=0.0, base=0,
                                    pattern=[[-HD, 32]], channel_multiplier=1))
            ch.link(g.affine_select(out=hsel[:, :], in_=hsel[:, :], compare_op=ALU.is_ge, fill=0.0, base=HD - 1,
                                    pattern=[[HD, 32]], channel_multiplier=-1))
            ch.step(g.iota(iota_i[:, :], pattern=[[1, 256]], base=0, channel_multiplier=0))
            ch.step(g.iota(tok_i, pattern=[[P, NT]], base=0, channel_multiplier=1))
            ch.step(g.iota(dump_i, pattern=[[1, TOPK], [P * TOPK, NT]], base=DUMP, channel_multiplier=TOPK))
            ch.step(g.memset(vp, 0.0))
            ch.link(g.memset(kvf, 0.0))
            assert ch.n == ch.per, ch.n
            pool.wait_ge(consts_ready, 1)
            for half in range(2):
                x_low(pool, 0, half)
                resid_sum(pool, 0, half, first=True)
            v_total(pool, 0)
            pool.wait_ge(table_cleared, 16)
            pool_turn(pool, 0, "body")
            with pool.Fori(1, B - 1) as b:
                pool_turn(pool, b, "body")
            pool_turn(pool, B - 1, "tail")
            pool.wait_ge(tab_ready, 1)
            pool.wait_ge(meta_stored, 16 * TOPK * NT * B)
            pool.wait_ge(zero_stored, 16)
            for n in range(2):
                pool.wait_ge(xs_stored[n], 16 * B)
            last_row = pool.to_reg(N - 1)

            def meta_load(t, u):
                row = pool.value_load(tab[0:1, 1, bass.ds(t, 1)], min_val=0, max_val=TRASH)
                src = meta[bass.ds(row, TS), :].rearrange("(a p) c -> p a c", p=P)
                pool.dma_start(mt[:, u % GRP, :, :], src).then_inc(meta_in, 16)

            def gather(t, u):
                if not isinstance(t, int) or t >= 4:
                    hold(pool, meta_in, t * 16 + 16)
                for a in range(2):
                    nc.gpsimd.indirect_dma_start(xg[:, u % XR, a, :], None, xs,
                                                 bass.IndirectOffsetOnAxis(mt[:, u % GRP, a, 0:1], 0)).then_inc(rows_in[u % 2], 16)

            def add_out(t, u):
                hold(pool, my_read, t * 2 + 2)
                for a in range(2):
                    nc.gpsimd.indirect_dma_start(orows, bass.IndirectOffsetOnAxis(mt[:, u % GRP, a, 0:1], 0),
                                                 y_sb[u % 2][:, a, :], None, bounds_check=last_row, oob_is_err=False,
                                                 compute_op=ALU.add).then_inc(added, 16)

            def group(g, first=False, last=False):
                for u in range(GRP):
                    t = g * GRP + u
                    if not (last and u >= GRP - 3):
                        hold(pool, mx_filled, t + 2)
                        gather(t + 3, u + 3)
                    if not (first and u == 0):
                        hold(pool, added, t * 32)
                    if not (last and u >= GRP - 4):
                        meta_load(t + 4, u + 4)
                    if first and u == 0:
                        for n in range(2):
                            pool.wait_ge(out_stored[n], 16 * 2 * B)
                    add_out(t, u)

            for t in range(4):
                meta_load(t, t)
            pool.wait_ge(meta_in, 16 * 4)
            gather(0, 0)
            gather(1, 1)
            pool.wait_ge(mx_filled, 1)
            gather(2, 2)
            group(0, first=True)
            with pool.Fori(1, NG - 1) as gg:
                group(gg)
            group(NG - 1, last=True)
            pool.wait_ge(added, 32 * MT)

        v = nc.vector

        def rsqrt(ch, y, a, u):
            ch.link(v.tensor_scalar(u.bitcast(I32), a.bitcast(I32), 1, None, ALU.arith_shift_right))
            ch.link(v.tensor_scalar(y.bitcast(I32), u.bitcast(I32), -1.0, MAGIC, ALU.mult, ALU.add))
            for _ in range(3):
                ch.link(v.tensor_tensor(u, a, y, ALU.mult))
                ch.link(v.scalar_tensor_tensor(u, u, -0.5, y, ALU.mult, ALU.mult))
                ch.link(v.scalar_tensor_tensor(y, u, 1.5, y, ALU.add, ALU.mult))

        chp, cha = Chain(dve_prep, 28 + 2 * (3 + 4 + 4 + 14 + 1)), Chain(dve_attn, 18 + 16 + 1 + 2 * (4 + 2))

        def row_stats(dve, b):
            for half in range(2):
                hold(dve, x_loaded[half], (b + 1) * 16)
            for t in range(NT):
                chp.step(v.bn_stats(bn[:, t, :], x_in[t // HT][:, t % HT, :]))
            hold(dve, dve_prep, chp.base + chp.n)
            for t in range(NT):
                chp.step(v.bn_aggr(mv[:, t, :], bn[:, t, :]))
            chp.wait()
            chp.link(v.tensor_scalar(va, mv[:, :, 1], 1e-5, None, ALU.add))
            rsqrt(chp, vy, va, vu)

        def normalise_rows(dve, b, half, first=False):
            if not (first and half == 0):
                dve.wait_ge(x_plus_xn, b * 2 + half)
            for t in range(HT):
                n = half * HT + t
                ins = v.tensor_scalar(xn[:, t, :], x_in[half][:, t, :], mv[:, n, 0:1], vy[:, n:n + 1],
                                      ALU.subtract, ALU.mult)
                if t < HT - 1:
                    chp.step(ins)
            ins.then_inc(xn_ready, 1)

        def drain(dve, phase, part, name, b):
            dve.wait_ge(filled[part], nth(part, name, b))
            return small_ap(phase, part, name, b)

        def qk_halves(dve, b, half, n0=0, n1=4):
            for n in range(n0, n1):
                side, m = n // 2, n % 2
                dst = (q_hl, k_hl)[side][half]
                dve.wait_ge(qk_read, b * QK_USES + half * 4 + n + 1)
                chp.link(v.tensor_copy(dst[:, m, 0, :], q32[n % 2]))
                v.tensor_tensor(dst[:, m, 1, :], q32[n % 2], dst[:, m, 0, :], ALU.subtract).then_inc(qk_split, 1)

        def v_drain(dve, phase, b, t):
            src = drain(dve, phase, "prep", f"v{t}", b)
            chp.step(v.tensor_copy(lg[:, t, :], src[:, D:D + E]))
            v.scalar_tensor_tensor(v32[:, t, :], src[:, 0:D], 1.0 / W_SCALE, bv_b[:, :], ALU.mult, ALU.add).then_inc(prep_read, 1)

        def norms(dve, phase, b, half):
            src = drain(dve, phase, "prep", f"nrmT{half}", b)[:, :].rearrange("p (t g c) -> p t g c", t=HT, g=4)
            v.tensor_copy(nsq, src[:, :, :, 0:8]).then_inc(prep_read, 1)
            wait_read(dve, "prep", f"nrmT{half}", b)
            rsqrt(chp, ny, nsq, nu)
            chp.link(v.tensor_tensor(nu, nsq, ny, ALU.mult))
            chp.link(v.tensor_scalar(norm[:, half], nu, 1e-8, None, ALU.add))
            chp.link(v.reciprocal(rn, norm[:, half, :, 2:4, :]))

        def v_over_norm(dve, b, half):
            ts = slice(half * HT, (half + 1) * HT)
            wait_read(dve, "prep", f"v{half * 4 + 3}", b)
            dst = vp[:, ts].rearrange("p t h d -> p (t h) d")
            rnf = rn.rearrange("p t g e -> p (t g e)").unsqueeze(2)
            chp.step(v.tensor_copy(dst[:, :, HD:HD + 1], rnf))
            v.tensor_tensor(dst[:, :, 0:HD], v32[:, ts].rearrange("p t (h d) -> p (t h) d", d=HD),
                            rnf.broadcast_to([P, HT * H, HD]), ALU.mult).then_inc(vp_ready, 1)

        def choose(dve, b):
            for t in range(NT):
                cha.step(v.max(mx[:, t, :], lg[:, t, :]))
            cha.wait()
            v.tensor_tensor(dl, mx[:, :, 1], mx[:, :, 0], ALU.subtract).then_inc(gate_in, 1)
            for t in range(NT):
                cha.step(v.max_index(mi[:, t, :], mx[:, t, :], lg[:, t, :]))
            cha.wait()
            cha.link(v.tensor_copy(ix, mi[:, :, 0:TOPK].rearrange("p t k -> p k t")))
            cha.link(v.tensor_tensor(oh.rearrange("p k t e -> p (k t) e"),
                                     ix.rearrange("p k t -> p (k t)").unsqueeze(2).broadcast_to([P, TOPK * NT, E]),
                                     iota_e[:, :].unsqueeze(1).broadcast_to([P, TOPK * NT, E]), ALU.is_equal))
            v.tensor_tensor(m16[:, 0:NT, :], oh[:, 0], oh[:, 1], ALU.add).then_inc(masks_ready, 1)

        def place(dve, phase, b, first):
            src = drain(dve, phase, "attn", "rank", b)
            cha.step(v.tensor_tensor(rank, src[:, 0:NT * E].rearrange("p (t e) -> p t e", e=E),
                                     carry[:, :].unsqueeze(1).broadcast_to([P, NT, E]), ALU.add))
            cha.wait()
            v.tensor_tensor(carry[:, :], src[:, NT * E:(NT + 1) * E], carry[:, :], ALU.add).then_inc(attn_read, 1)
            cha.link(v.tensor_tensor(rsel, oh, rank.unsqueeze(1).broadcast_to([P, TOPK, NT, E]), ALU.mult))
            cha.link(v.tensor_reduce(rpos, rsel, AX.X, ALU.add))
            cha.step(v.tensor_scalar(keep, rpos, float(CAP), None, ALU.is_lt))
            cha.link(v.scalar_tensor_tensor(slot, ix, float(RROWS), rpos, ALU.mult, ALU.add))
            cha.link(v.tensor_tensor(slot, slot, dump_f[:, :, :], ALU.subtract))
            cha.link(v.tensor_tensor(slot, slot, keep, ALU.mult))
            cha.link(v.tensor_tensor(slot, slot, dump_f[:, :, :], ALU.add))
            dve.wait_ge(gate_exp, b + 1)
            cha.link(v.tensor_scalar(gate[:, 1, :], eg, 1.0, None, ALU.add))
            cha.link(v.reciprocal(gate[:, 0, :], gate[:, 1, :]))
            cha.link(v.tensor_scalar(gate[:, 0, :], gate[:, 0, :], 1.0 / (H_SCALE * R_SCALE), None, ALU.mult))
            cha.link(v.tensor_tensor(gate[:, 1, :], gate[:, 0, :], eg, ALU.mult))
            if not first:
                dve.wait_ge(meta_stored, b * 16 * TOPK * NT)
            cha.step(v.tensor_copy(rec[:, :, :, 0], tok_f[:, :].unsqueeze(1).broadcast_to([P, TOPK, NT])))
            cha.step(v.tensor_copy(rec[:, :, :, 1].bitcast(F32), gate))
            cha.link(v.tensor_copy(slot_i, slot))
            cha.step(v.tensor_scalar(tok_f[:, :], tok_f[:, :], float(S), None, ALU.add))
            v.tensor_scalar(dump_f[:, :, :], dump_f[:, :, :], float(S * TOPK), None, ALU.add).then_inc(slots_ready, 1)

        def kv_build(dve, phase, b):
            src = drain(dve, phase, "attn", "kvT", b)[:, 0:256].rearrange("p (a c) -> p a c", c=32)
            wait_read(dve, "attn", "vsum", b)
            csv = cs_b.rearrange("p (a s) d -> p a s d", s=2)
            rows_ = [slice(s * 64, s * 64 + 64) for s in range(2)]
            cha.step(v.tensor_tensor(kvf[rows_[0], :, 0:HD + 1], src[rows_[0], :, 0:HD + 1], csv[rows_[0], :, 0, :], ALU.add))
            v.tensor_tensor(kvf[rows_[1], :, HD + 1:], src[rows_[1], :, 0:HD + 1], csv[rows_[1], :, 1, :], ALU.add) \
                .then_inc(attn_read, 1)
            wait_read(dve, "attn", "kvT", b)
            v.tensor_copy(kv_hl[:, 0], kvf).then_inc(kvf_ready, 1)
            dve.wait_ge(kvf_ready, b + 1)
            v.tensor_tensor(kv_hl[:, 1], kvf, kv_hl[:, 0], ALU.subtract).then_inc(kv_split, 1)

        def q_low(dve, b, half, p0, p1):
            for p_ in range(p0, p1):
                n = 2 * NT + half * PAIRS + p_
                dve.wait_ge(feat_relu, b * FEAT_USES + n + 1)
                v.scalar_tensor_tensor(rq[:, p_, 1, :], big[n % BIG_BANKS][:, :], 0.0, rq[:, p_, 0, :],
                                       ALU.max, ALU.subtract).then_inc(qf_split, 1)

        def constant_part(dve, b, half):
            if half == 0:
                wait_read(dve, "attn", "cn", b)
            else:
                dve.wait_ge(o_split, b * 2 + 1)
            for t in range(HT):
                ins = v.tensor_tensor(nd[:, t], norm[:, half, t, 0:2, :].rearrange("p g e -> p (g e)").unsqueeze(2)
                                      .broadcast_to([P, H, HD + 1]), cn_b, ALU.mult)
                cha.step(ins)
            cha.wait()

        def attend_drain(dve, phase, b, t):
            src = drain(dve, phase, "attn", f"ab{t}", b)[:, 0:H * (HD + 1)].rearrange("p (h d) -> p h d", h=H)
            v.tensor_tensor(nd[:, t % HT], src, nd[:, t % HT], ALU.add).then_inc(attn_read, 1)

        def normalise(dve, b, half):
            wait_read(dve, "attn", f"ab{half * 4 + 3}", b)
            nq = norm[:, half, :, 0:2, :].rearrange("p t g e -> p t (g e)")
            cha.link(v.scalar_tensor_tensor(dn, nq, 1e-6 * P_SCALE * P_SCALE, nd[:, :, :, HD], ALU.mult, ALU.max))
            cha.link(v.reciprocal(dn, dn))
            ndv = nd.rearrange("p t h d -> p (t h) d")[:, :, 0:HD]
            v.tensor_tensor(ndv, ndv, dn.rearrange("p t h -> p (t h)").unsqueeze(2).broadcast_to([P, HT * H, HD]),
                            ALU.mult).then_inc(o_ready, 1)

        def o_low(dve, b, half):
            dve.wait_ge(o_high, b * 2 + half + 1)
            ohv = o_hl.rearrange("p t l (h d) -> p l t h d", h=H)
            v.tensor_tensor(ohv[:, 1], nd[:, :, :, 0:HD], ohv[:, 0], ALU.subtract).then_inc(o_split, 1)

        def out_drain(dve, phase, b, half, first):
            for j in range(2):
                k = 2 * half + j
                src = drain(dve, phase, "attn", f"out{k}", b)[:, :].rearrange("p (t d) -> p t d", t=2)
                if half == 1:
                    dve.wait_ge(out_stored[k % 2], b * 32 + 16)
                elif not first:
                    dve.wait_ge(out_stored[k % 2], b * 32)
                dve.wait_ge(resid_ready, b * 2 + half + 1)
                v.scalar_tensor_tensor(osb[k % 2], src, 1.0 / R_SCALE, resid[:, 2 * k:2 * k + 2, :], ALU.mult, ALU.add) \
                    .then_inc(attn_read, 1)

        def v_and_norms(dve, phase, b, half, attended=None, first=False):
            v_drain(dve, phase, b, half * HT)
            v_drain(dve, phase, b, half * HT + 1)
            if attended is not None and half == 0:
                normalise(dve, attended, 1)
            elif attended is not None:
                out_drain(dve, phase, attended, 1, first)
            v_drain(dve, phase, b, half * HT + 2)
            norms(dve, phase, b, half)
            v_drain(dve, phase, b, half * HT + 3)

        def dve_turn(dve, b, phase, first=False):
            body = phase == "body"
            cha.start(dve, b)
            choose(dve, b)
            if body:
                chp.start(dve, b + 1)
                row_stats(dve, b + 1)
                normalise_rows(dve, b + 1, 0)
            place(dve, phase, b, first)
            if not body:
                tile_table(dve)
            dve.wait_ge(kv_tile_done, (b + 1) * NT)
            v.tensor_copy(kvt, kvbank[:, 0:256]).then_inc(kvt_copied, 1)
            q_low(dve, b, 0, 0, 2)
            kv_build(dve, phase, b)
            q_low(dve, b, 0, 2, PAIRS)
            if body:
                normalise_rows(dve, b + 1, 1)
            constant_part(dve, b, 0)
            for t in range(HT):
                attend_drain(dve, phase, b, t)
            q_low(dve, b, 1, 0, PAIRS)
            normalise(dve, b, 0)
            if body:
                qk_halves(dve, b + 1, 0, 0, 2)
            o_low(dve, b, 0)
            if body:
                qk_halves(dve, b + 1, 0, 2, 4)
            constant_part(dve, b, 1)
            for t in range(HT, NT):
                attend_drain(dve, phase, b, t)
            if body:
                v_and_norms(dve, phase, b + 1, 0, attended=b)
            else:
                normalise(dve, b, 1)
            o_low(dve, b, 1)
            out_drain(dve, phase, b, 0, first)
            if body:
                v_over_norm(dve, b + 1, 0)
                qk_halves(dve, b + 1, 1)
                v_and_norms(dve, phase, b + 1, 1, attended=b, first=first)
                v_over_norm(dve, b + 1, 1)
                chp.end()
            else:
                out_drain(dve, phase, b, 1, first)
            cha.end()

        def tile_table(dve):
            K = RROWS // TS
            ch = Chain(dve_table, 0)
            ch.start(dve, 0)
            at = [0]

            def take(*shape):
                n = 1
                for k in shape:
                    n *= k
                a = tb[0:1, at[0]:at[0] + n]
                at[0] += n
                if len(shape) == 2:
                    a = a.rearrange("p (a b) -> p a b", a=shape[0])
                return a

            iota_f, cnt, over = take(256), take(E), take(E, K)
            tiles, upto, used = take(E), take(E, E), take(E)
            past, pt, ex, ue = take(MT, E), take(MT, E), take(MT), take(MT)
            dve.wait_ge(vsum_ready, B)
            dve.wait_ge(vp_ready, 2 * B)
            ch.link(v.tensor_copy(iota_f, iota_i[0:1, :]))
            ch.link(v.tensor_scalar(cnt, carry[0:1, :], float(CAP), None, ALU.min))
            ch.link(v.tensor_scalar(ue[:, 0:K], iota_f[:, 0:K], float(TS), None, ALU.mult))
            ch.link(v.tensor_tensor(over, cnt.unsqueeze(2).broadcast_to([1, E, K]),
                                    ue[:, 0:K].unsqueeze(1).broadcast_to([1, E, K]), ALU.is_gt))
            ch.link(v.tensor_reduce(tiles, over, AX.X, ALU.add))
            ch.link(v.tensor_tensor(upto, iota_f[:, 0:E].unsqueeze(1).broadcast_to([1, E, E]),
                                    iota_f[:, 0:E].unsqueeze(2).broadcast_to([1, E, E]), ALU.is_le))
            ch.link(v.tensor_tensor(upto, upto, tiles.unsqueeze(1).broadcast_to([1, E, E]), ALU.mult))
            ch.link(v.tensor_reduce(used, upto, AX.X, ALU.add))
            ch.link(v.tensor_tensor(past, iota_f[:, 0:MT].unsqueeze(2).broadcast_to([1, MT, E]),
                                    used.unsqueeze(1).broadcast_to([1, MT, E]), ALU.is_ge))
            ch.link(v.tensor_reduce(ex, past, AX.X, ALU.add))
            ch.link(v.tensor_tensor(pt, past, tiles.unsqueeze(1).broadcast_to([1, MT, E]), ALU.mult))
            ch.link(v.tensor_reduce(ue, pt, AX.X, ALU.add))
            ch.link(v.tensor_tensor(ue, iota_f[:, 0:MT], ue, ALU.subtract))
            ch.link(v.tensor_scalar(ue, ue, float(TS), None, ALU.mult))
            ch.link(v.scalar_tensor_tensor(ue, ex, float(RROWS), ue, ALU.mult, ALU.add))
            ch.link(v.tensor_scalar(tab[:, 1, :], ue, float(TRASH), None, ALU.min))
            v.tensor_scalar(tab[:, 0, :], ex, float(E - 1), None, ALU.min).then_inc(tab_ready, 1)

        def rows_copy(dve, t, u):
            dve.wait_ge(mx_filled, t + 1)
            v.tensor_copy(moe_xT[u % 2].rearrange("p c q -> p (c q)"), f16(bank[u % 2])).then_inc(mx_read, 1)

        def hidden_split(dve, t, u):
            for j in range(4):
                dve.wait_ge(mh_silu, t * 4 + j + 1)
                v.tensor_scalar(hT[u % 2][:, 2 * j:2 * j + 2, 0, :], h32[j], H_SCALE, None, ALU.mult).then_inc(mh_step, 1)
                dve.wait_ge(mh_step, t * 4 + j + 1)
                v.scalar_tensor_tensor(hT[u % 2][:, 2 * j:2 * j + 2, 1, :], h32[j], H_SCALE, hT[u % 2][:, 2 * j:2 * j + 2, 0, :],
                                       ALU.mult, ALU.subtract).then_inc(mh_split, 1)

        @block.vector
        def _(dve):
            ch = Chain(dve_first, 0)
            ch.start(dve, 0)
            v.memset(raw_p, 0.0).then_inc(proj_zeroed, 1)
            ch.step(v.memset(carry[:, :], 0.0))
            ch.step(v.memset(m16[:, NT, :], 0.0))
            dve.wait_ge(pool_first, 19)
            ch.step(v.tensor_copy(iota_e[:, :], iota_i[:, 0:E]))
            ch.step(v.tensor_copy(tok_f[:, :], tok_i))
            ch.step(v.tensor_copy(dump_f[:, :, :], dump_i))
            dve.wait_ge(weights_loaded, 16 * 9)
            dve.wait_ge(proj_loaded, 16 * H)
            scaled = ((w_hl[:, :, :, 0:3 * D], raw_w[:, :, 0:3 * D], W_SCALE), (w_hl[:, :, :, 3 * D:], raw_w[:, :, 3 * D:], R_SCALE),
                      (wo_hl[:, :, :, :], raw_o, R_SCALE), (p_hl[:, :, :, :], raw_p, P_SCALE))
            for dst, src, scale in scaled:
                ch.step(v.tensor_scalar(dst[:, 0], src, scale, None, ALU.mult))
            ch.wait()
            for dst, src, scale in scaled:
                ch.step(v.scalar_tensor_tensor(dst[:, 1], src, scale, dst[:, 0], ALU.mult, ALU.subtract))
            ch.wait()
            dve.wait_ge(table_cleared, 16)
            dve.wait_ge(zero_stored, 16)
            v.memset(mv, 0.0).then_inc(consts_ready, 1)
            dve.wait_ge(consts_ready, 1)

            chp.start(dve, 0)
            row_stats(dve, 0)
            for half in range(2):
                normalise_rows(dve, 0, half, first=True)
            for half in range(2):
                qk_halves(dve, 0, half)
                v_and_norms(dve, "first", 0, half)
                v_over_norm(dve, 0, half)
            chp.end()
            dve_turn(dve, 0, "body", first=True)
            with dve.Fori(1, B - 1) as b:
                dve_turn(dve, b, "body")
            dve_turn(dve, B - 1, "tail")
            wait_read(dve, "attn", "out3", B - 1)
            for n in range(2):
                dve.wait_ge(out_stored[n], 16 * 2 * B)
                dve.wait_ge(w_out[n], 16 * 2 * E)

            def group(g, last=False):
                for u in range(GRP):
                    t = g * GRP + u
                    hidden_split(dve, t, u)
                    if not (last and u == GRP - 1):
                        rows_copy(dve, t + 1, u + 1)

            rows_copy(dve, 0, 0)
            with dve.Fori(0, NG - 1) as g:
                group(g)
            group(NG - 1, last=True)


def kernel(**inputs):
    import numpy as _np
    import concourse.bacc as _bacc
    from concourse import mybir as _mybir
    from concourse.bass_utils import run_bass_kernel_spmd as _run

    layout = {
        "x": inputs["L0_attn_x"], "Wq": inputs["L0_attn_Wq"], "bq": inputs["L0_attn_bq"], "Wk": inputs["L0_attn_Wk"],
        "bk": inputs["L0_attn_bk"], "Wv": inputs["L0_attn_Wv"], "bv": inputs["L0_attn_bv"], "Wo": inputs["L0_attn_Wo"],
        "bo": inputs["L0_attn_bo"], "proj_t": _np.transpose(_np.asarray(inputs["L0_attn_projection"]), (0, 2, 1)),
        "router_t": _np.transpose(_np.asarray(inputs["L0_ffn_router_w"]), (1, 0)), "w1": inputs["L0_ffn_w1"],
        "w2": inputs["L0_ffn_w2"],
    }
    nc = _bacc.Bacc("TRN2", target_bir_lowering=False, num_devices=1)
    arrays, args = {}, []
    for name, value in layout.items():
        a = _np.ascontiguousarray(value)
        arrays[f"in_{name}_dram"] = a
        args.append(nc.dram_tensor(f"in_{name}_dram", a.shape, _mybir.dt.from_np(a.dtype), kind="ExternalInput").ap())
    args.append(nc.dram_tensor("out_0_dram", (B, S, D), _mybir.dt.float32, kind="ExternalOutput").ap())
    moe_attention(nc, *args)
    r = _run(nc, [arrays], core_ids=[0])
    return r.results[0]["out_0_dram"]
```

```python
from contextlib import ExitStack

import concourse.bass as bass
from concourse import mybir

P = 128
B, S, D = 8, 1024, 256
H, HD, F = 16, 16, 64
E, TOPK, FF = 8, 2, 1024
N = B * S
CAP = int(1.25 * N * TOPK / E) + 1
NT = S // P
HT = NT // 2
HS = HT * P
KC = D // P
PAIRS = H // 2
KVW = 2 * (HD + 1)
WCOLS = 3 * D + E

TS = 256
MT = (N * TOPK + E * (TS - 1)) // TS
RROWS = -(-CAP // TS) * TS
TRASH = E * RROWS
DUMP = TRASH + TS
META_ROWS = DUMP + N * TOPK
GRP = 8
XR = 4
NG = -(-MT // GRP)
LASTG = MT - (NG - 1) * GRP
assert LASTG >= 5 and NG > 2

W_SCALE = 16.0
R_SCALE = 256.0
H_SCALE = 64.0
P_SCALE = 1.0 / 16.0
EPSF = 0.1 * P_SCALE
MAGIC = 1597463007.0

F32, F16, I32, U32 = mybir.dt.float32, mybir.dt.float16, mybir.dt.int32, mybir.dt.uint32
ALU = mybir.AluOpType
ACT = mybir.ActivationFunctionType
AX = mybir.AxisListType
PASSES = ((0, 0), (0, 1), (1, 0))

def prep(*names):
    return [("prep", n) for n in names]


def attn(*names):
    return [("attn", n) for n in names]


BODY = (attn("rank", "vsum", "kvT") + prep("xT0", "xT1") + attn("cn", "ab0", "ab1", "ab2", "ab3") + prep("xT2", "xT3")
        + attn("oT0", "oT1", "ab4", "ab5", "ab6", "ab7") + prep("v0", "v1", "nrm0", "v2", "nrmT0", "v3")
        + attn("out0", "out1", "oT2", "oT3") + prep("v4", "v5") + attn("out2", "out3") + prep("v6", "nrm1", "v7", "nrmT1"))
PREP = [u for u in BODY if u[0] == "prep"]
TAIL = [u for u in BODY if u[0] == "attn"]
PLAN = {"first": PREP, "body": BODY, "tail": TAIL}
PER = {"prep": len(PREP), "attn": len(TAIL)}
NTH = {use: n + 1 for part in (PREP, TAIL) for n, use in enumerate(part)}
RANK_AT = {"body": 5, "tail": 2}
SMALL_BANKS = 3
BIG_BANKS = 4
assert len(BODY) % SMALL_BANKS == 0
ACT_READS = {"xT0", "xT1", "xT2", "xT3", "oT0", "oT1", "oT2", "oT3", "nrm0", "nrm1", "vsum", "cn"} | {f"v{t}" for t in range(NT)}
QK_USES, FEAT_USES, QF_USES = 2 * 4, 2 * NT + 2 * PAIRS, 2 * PAIRS


def reader(name):
    return "act" if name in ACT_READS else "dve"


def reads(use, b):
    same = [u for u in (PREP if use[0] == "prep" else TAIL) if reader(u[1]) == reader(use[1])]
    return b * len(same) + same.index(use) + 1


def small_use(phase, use, b):
    plan = PLAN[phase]
    n = plan.index(use)
    nth = n if phase == "first" else n + len(PREP)
    if n >= SMALL_BANKS:
        before = plan[n - SMALL_BANKS]
        gap = (before[0] == "prep") - (use[0] == "prep")
        return nth % SMALL_BANKS, before, b + gap
    if phase == "first":
        return nth % SMALL_BANKS, None, None
    before = (PREP if isinstance(b, int) and b == 0 else BODY)[n - SMALL_BANKS]
    return nth % SMALL_BANKS, before, b if before[0] == "prep" else b - 1


class Chain:

    def __init__(self, sem, per):
        self.sem, self.per = sem, per

    def start(self, eng, b):
        self.eng, self.base, self.n = eng, b * self.per, 0

    def step(self, ins):
        self.n += 1
        ins.then_inc(self.sem, 1)

    def wait(self):
        self.eng.wait_ge(self.sem, self.base + self.n)

    def link(self, ins):
        self.step(ins)
        self.wait()

    def end(self):
        assert self.n == self.per, (self.n, self.per)


def moe_attention(nc, x, Wq, bq, Wk, bk, Wv, bv, Wo, bo, proj_t, router_t, w1, w2, out):
    xrows = x.rearrange("b s d -> (b s) d")
    orows = out.rearrange("b s d -> (b s) d")
    xs = nc.dram_tensor("xn_split", [N + P, 2 * D], F16, kind="Internal").ap()
    meta = nc.dram_tensor("slot_table", [META_ROWS, 2], I32, kind="Internal").ap()
    wsplit = nc.dram_tensor("experts_split", [E, P, 4, 2, 1024], F16, kind="Internal").ap()

    with ExitStack() as ctx:
        def sb(name, shape, dt):
            return ctx.enter_context(nc.sbuf_tensor(name, shape, dt))

        def sem(name):
            return ctx.enter_context(nc.semaphore(name))

        bank = [ctx.enter_context(nc.psum_tensor(f"bank{i}", [P, 512], F32)) for i in range(8)]
        small = [bank[0], bank[1], bank[6]]
        big = bank[2:6]
        kvbank = bank[7]

        w_hl = sb("w_hl", [P, 2, KC, WCOLS], F16)
        wo_hl = sb("wo_hl", [P, 2, KC, D], F16)
        p_hl = sb("p_hl", [P, 2, KC, 512], F16)
        ident16 = sb("ident16", [P, P], F16)
        ident32 = sb("ident32", [P, P], F32)
        tri = sb("tri", [P, P], F16)
        ones16 = sb("ones16", [P, P], F16)
        cfeat = sb("cfeat", [P, P], F32)
        hsel = sb("hsel", [P, 32], F32)
        iota_e = sb("iota_e", [P, E], F32)
        iota_i = sb("iota_i", [P, 256], I32)
        tok_f = sb("tok_f", [P, NT], F32)
        dump_f = sb("dump_f", [P, 2, NT], F32)
        bqk = sb("bqk", [P, 2, KC], F32)
        bv_hl = sb("bv_hl", [1, 2, D], F16)
        bv_two = sb("bv_two", [2, D], F16)
        bo_b = sb("bo_b", [P, D], F32)
        carry = sb("carry", [P, E], F32)
        mt = sb("mt", [P, GRP, 2, 2], I32)
        tab = sb("tab", [1, 2, MT], I32)
        xg = sb("xg", [P, XR, 2, 2 * D], F16)
        AREA = 16384 + 166528 + 2048
        EXPERT = 4 * 2 * 1024
        area = sb("area", [P, AREA // 4], F32)
        cursor = [EXPERT // 2]

        def view(shape, dt):
            n = 1
            for k in shape:
                n *= k
            words = n * (2 if dt == F16 else 4) // 4
            a = area[:, cursor[0]:cursor[0] + words]
            cursor[0] += words
            assert cursor[0] * 4 <= AREA, cursor[0] * 4
            if dt != F32:
                a = a.bitcast(dt)
            names = "abcd"[:len(shape)]
            if len(shape) > 1:
                a = a.rearrange(f"p ({' '.join(names)}) -> p {' '.join(names)}", **dict(zip(names, shape)))
            return a

        x_in = [view([HT, D], F32) for _ in range(2)]
        xn = view([HT, D], F32)
        xhl = [view([HT, 2, D], F16) for _ in range(2)]
        xT = [view([2 * KC, HS], F16) for _ in range(2)]
        q32 = [view([HS], F32) for _ in range(3)]
        q_hl = [view([KC, 2, HS], F16) for _ in range(2)]
        k_hl = [view([KC, 2, HS], F16) for _ in range(2)]
        sq = view([2, KC, HS], F32)
        v32 = view([NT, D + E], F32)
        vp = view([NT, H, 32], F32)
        vsum = view([H, HD + 1], F32)
        resid = view([NT, D], F32)
        rk = [view([KC, 512], F32) for _ in range(2)]
        rq = view([PAIRS, 2, HS], F16)
        kvt = view([256], F32)
        cs_b = view([H, HD + 1], F32)
        kvf = view([PAIRS, KVW], F32)
        kv_hl = view([2, PAIRS, KVW], F16)
        cn_b = view([H, HD + 1], F32)
        nT = view([HS], F32)
        nsq = view([HT, 4, 8], F32)
        ny = view([HT, 4, 8], F32)
        nu = view([HT, 4, 8], F32)
        norm = view([2, HT, 4, 8], F32)
        rn = view([HT, 2, 8], F32)
        nd = view([HT, H, HD + 1], F32)
        dn = view([HT, H], F32)
        o_hl = view([HT, 2, D], F16)
        oT = view([HT, 2 * KC, P], F16)
        osb = [view([2, D], F32) for _ in range(2)]
        w_raw = [view([1024], F32) for _ in range(2)]
        w_st = [view([2, 1024], F16) for _ in range(2)]
        bn = view([NT, 6], F32)
        mv = view([NT, 2], F32)
        va = view([NT], F32)
        vy = view([NT], F32)
        vu = view([NT], F32)
        mx = view([NT, 8], F32)
        mi = view([NT, 8], U32)
        ix = view([2, NT], F32)
        oh = view([2, NT, E], F32)
        m16 = view([NT + 1, E], F16)
        rank = view([NT, E], F32)
        rsel = view([2, NT, E], F32)
        rpos = view([2, NT], F32)
        keep = view([2, NT], F32)
        slot = view([2, NT], F32)
        dl = view([NT], F32)
        eg = view([NT], F32)
        gate = view([2, NT], F32)
        slot_i = view([2, NT], I32)
        rec = view([2, NT, 2], I32)
        tb = v32.rearrange("p a b -> p (a b)")
        vtmp = view([4, D], F32)
        stage = rq.rearrange("p a b c -> p (a b c)").bitcast(F32)
        raw_w = stage[:, 0:KC * WCOLS].rearrange("p (k n) -> p k n", k=KC)
        raw_o = stage[:, KC * WCOLS:KC * (WCOLS + D)].rearrange("p (k n) -> p k n", k=KC)
        raw_p = stage[:, KC * (WCOLS + D):KC * (WCOLS + D + 512)].rearrange("p (m n) -> p m n", m=KC)
        bv_row = stage[0:1, KC * (WCOLS + D + 512):KC * (WCOLS + D + 512) + D]
        clear = rk[0].rearrange("p a b -> p (a b)").bitcast(I32)[:, 0:2 * DUMP // P]
        zero_rows = rk[1].rearrange("p a b -> p (a b)").bitcast(F16)[:, 0:2 * D]
        tok_i = v32.bitcast(I32)[:, 0, 0:NT]
        dump_i = oh.bitcast(I32)[:, :, 0, :]

        we = area[:, 0:E * EXPERT // 2].bitcast(F16)
        cursor[0] = E * EXPERT // 2
        moe_xT = [view([2 * KC, TS], F16) for _ in range(2)]
        h32 = [view([2, TS], F32) for _ in range(4)]
        hT = [view([FF // P, 2, TS], F16) for _ in range(2)]
        y_sb = [view([2, D], F32) for _ in range(2)]

        weights_loaded = sem("weights_loaded")
        bias_split, bias_placed = sem("bias_split"), sem("bias_placed")
        proj_zeroed = sem("proj_zeroed")
        proj_loaded = sem("proj_loaded")
        consts_ready = sem("consts_ready")
        w_ready = sem("w_ready")
        x_plus_xn = sem("x_plus_xn")
        zero_stored = sem("zero_stored")
        norm_guess = sem("norm_guess")
        pool_norm = sem("pool_norm")
        norm_ready = sem("norm_ready")
        pool_prep = sem("pool_prep")
        pool_first = sem("pool_first")
        dve_first = sem("dve_first")
        slots_cleared = sem("slots_cleared")
        x_loaded = [sem(f"x_loaded{i}") for i in range(2)]
        xn_split = sem("xn_split")
        xl_split = sem("xl_split")
        resid_ready = sem("resid_ready")
        xn_ready = sem("xn_ready")
        xs_stored = [sem(f"xs_stored{i}") for i in range(2)]
        prep_filled, attn_filled = sem("prep_filled"), sem("attn_filled")
        prep_read, attn_read = sem("prep_read"), sem("attn_read")
        prep_taken, attn_taken = sem("prep_taken"), sem("attn_taken")
        filled = {"prep": prep_filled, "attn": attn_filled}
        read = {("prep", "dve"): prep_read, ("attn", "dve"): attn_read, ("prep", "act"): prep_taken, ("attn", "act"): attn_taken}
        qk_filled = sem("qk_filled")
        qk_read = sem("qk_read")
        qk_squared = sem("qk_squared")
        qk_split = sem("qk_split")
        vp_ready = sem("vp_ready")
        vsum_ready = sem("vsum_ready")
        feat_filled = sem("feat_filled")
        feat_relu = sem("feat_relu")
        qf_split = sem("qf_split")
        kv_tile_done = sem("kv_tile_done")
        kvt_copied = sem("kvt_copied")
        kvf_ready = sem("kvf_ready")
        kv_split = sem("kv_split")
        masks_ready = sem("masks_ready")
        gate_in, gate_exp = sem("gate_in"), sem("gate_exp")
        slots_ready = sem("slots_ready")
        table_cleared = sem("table_cleared")
        meta_stored = sem("meta_stored")
        o_ready, o_high = sem("o_ready"), sem("o_high")
        o_split = sem("o_split")
        out_stored = [sem(f"out_stored{i}") for i in range(2)]
        w_in = [sem(f"w_in{i}") for i in range(2)]
        w_scaled, w_hi, w_lo = sem("w_scaled"), sem("w_hi"), sem("w_lo")
        w_out = [sem(f"w_out{i}") for i in range(2)]
        dve_prep, dve_attn, dve_table = sem("dve_prep"), sem("dve_attn"), sem("dve_table")
        tab_ready = sem("tab_ready")
        experts_in = sem("experts_in")
        meta_in = sem("meta_in")
        rows_in = [sem(f"rows_in{i}") for i in range(2)]
        mx_filled, mx_read = sem("mx_filled"), sem("mx_read")
        mh_filled, mh_silu = sem("mh_filled"), sem("mh_silu")
        mh_split = sem("mh_split")
        mh_step = sem("mh_step")
        my_filled, my_read = sem("my_filled"), sem("my_read")
        added = sem("added")

        block = ctx.enter_context(nc.Block())

        def small_ap(phase, part, name, b, eng=None):
            i, before, bb = small_use(phase, (part, name), b)
            if eng is not None and before is not None:
                eng.wait_ge(read[before[0], reader(before[1])], reads(before, bb))
            return small[i]

        def nth(part, name, b):
            return b * PER[part] + NTH[(part, name)]

        def wait_read(eng, part, name, b, wait=None):
            (wait or (lambda e, s_, v_: e.wait_ge(s_, v_)))(eng, read[part, reader(name)], reads((part, name), b))

        def f16(a):
            return a[:, :].bitcast(F16)

        def rows(ap, first, count):
            return ap[bass.ds(first, count), :]

        def hold(eng, s, value):
            if isinstance(value, int):
                eng.wait_ge(s, value)
                return
            value = eng.to_reg(value)
            eng.wait_ge(consts_ready, 1)
            eng.wait_ge(s, value)

        w1_rows = w1.rearrange("e k f -> (e k) f")
        w2_rows = w2.rearrange("e f d -> (e f) d")
        ws_rows = wsplit.rearrange("e p c h n -> (e p) c (h n)")

        def w_load(sp, e, c):
            if c < 2:
                src = w1_rows[bass.ds(e * D + c * P, P), :]
                dst = w_raw[c % 2]
            else:
                src = w2_rows[bass.ds(e * FF + (c - 2) * 4 * P, 4 * P), :].rearrange("(c p) d -> p c d", p=P)
                dst = w_raw[c % 2].rearrange("p (c d) -> p c d", c=4)
            if c >= 2:
                hold(sp, w_lo, e * 4 + c - 1)
            sp.dma_start(dst, src).then_inc(w_in[c % 2], 16)

        def w_store(sp, e, c):
            dst = ws_rows[bass.ds(e * P, P), c, :]
            hold(sp, w_lo, e * 4 + c + 1)
            sp.dma_start(dst, w_st[c % 2].rearrange("p h n -> p (h n)")).then_inc(w_out[c % 2], 16)

        def x_load(sp, b, half):
            src = xrows[bass.ds(b * S + half * HS, HS), :].rearrange("(t p) d -> p t d", p=P)
            hold(sp, resid_ready, (b - 1) * 2 + half + 1)
            sp.dma_start(x_in[half], src).then_inc(x_loaded[half], 16)

        def xs_store(sp, b, half):
            dst = xs[bass.ds(b * S + half * HS, HS), :].rearrange("(t p) n -> p t n", p=P)
            hold(sp, xl_split, b * 2 + half + 1)
            sp.dma_start(dst, xhl[half].rearrange("p t h n -> p t (h n)")).then_inc(xs_stored[half], 16)

        def out_store(sp, b, k):
            dst = orows[bass.ds(b * S + k * 2 * P, 2 * P), :].rearrange("(t p) d -> p t d", p=P)
            wait_read(sp, "attn", f"out{k}", b, hold)
            sp.dma_start(dst, osb[k % 2]).then_inc(out_stored[k % 2], 16)

        def sp_turn(sp, b, phase, x_next=True):
            body = phase == "body"
            if body:
                xs_store(sp, b + 1, 0)
            w_store(sp, b, 0)
            w_load(sp, b, 2)
            if body:
                xs_store(sp, b + 1, 1)
            w_store(sp, b, 1)
            w_load(sp, b, 3)
            out_store(sp, b, 0)
            out_store(sp, b, 1)
            w_store(sp, b, 2)
            if body:
                w_load(sp, b + 1, 0)
            if body and x_next:
                x_load(sp, b + 2, 0)
            out_store(sp, b, 2)
            out_store(sp, b, 3)
            if body and x_next:
                x_load(sp, b + 2, 1)
            w_store(sp, b, 3)
            if body:
                w_load(sp, b + 1, 1)

        @block.sync
        def _(sp):
            for half in range(2):
                sp.dma_start(x_in[half], xrows[half * HS:(half + 1) * HS, :].rearrange("(t p) d -> p t d", p=P)) \
                    .then_inc(x_loaded[half], 16)
            for n, w in enumerate((Wq, Wk, Wv)):
                sp.dma_start(raw_w[:, :, n * D:(n + 1) * D], w.rearrange("(k p) n -> p k n", p=P)).then_inc(weights_loaded, 16)
            sp.dma_start(raw_w[:, :, 3 * D:], router_t.rearrange("(k p) n -> p k n", p=P)).then_inc(weights_loaded, 16)
            sp.dma_start(raw_o, Wo.rearrange("(k p) n -> p k n", p=P)).then_inc(weights_loaded, 16)
            sp.dma_start(bv_row, bv.rearrange("(a n) -> a n", a=1)).then_inc(weights_loaded, 16)
            sp.dma_start(bo_b[:, :], bo.rearrange("(a n) -> a n", a=1).broadcast_to([P, D])).then_inc(weights_loaded, 16)
            for n, v_ in enumerate((bq, bk)):
                sp.dma_start(bqk[:, n, :], v_.rearrange("(k p) -> p k", p=P),
                             allow_slow_non_contiguous=True).then_inc(weights_loaded, 16)
            sp.wait_ge(proj_zeroed, 1)
            per_head = proj_t.rearrange("(m l) d f -> l d m f", m=KC)
            for l in range(H // KC):
                sp.dma_start(raw_p[l * HD:(l + 1) * HD, :, l * F:(l + 1) * F], per_head[l]).then_inc(proj_loaded, 16)
            sp.wait_ge(slots_cleared, 1)
            sp.dma_start(meta[0:DUMP, :].rearrange("(p a) c -> p (a c)", p=P), clear[:, 0:2 * DUMP // P]).then_inc(table_cleared, 16)
            sp.dma_start(xs[N:N + P, :], zero_rows).then_inc(zero_stored, 16)
            sp.wait_ge(bias_split, 1)
            for hl in range(2):
                sp.dma_start(bv_two[hl:hl + 1, :], bv_hl[:, hl, :]).then_inc(bias_placed, 16)
            sp.wait_ge(consts_ready, 1)
            for half in range(2):
                xs_store(sp, 0, half)
                x_load(sp, 1, half)
                w_load(sp, 0, half)
            sp_turn(sp, 0, "body")
            with sp.Fori(1, B - 2) as b:
                sp_turn(sp, b, "body")
            sp_turn(sp, B - 2, "body", x_next=False)
            for n in range(2):
                sp.wait_ge(w_out[n], 16 * 2 * (E - 1))
            for e in range(E):
                if e == 1:
                    sp_turn(sp, B - 1, "tail")
                    for n in range(2):
                        sp.wait_ge(w_out[n], 16 * 2 * E)
                    wait_read(sp, "attn", "out3", B - 1)
                    for n in range(2):
                        sp.wait_ge(out_stored[n], 16 * 2 * B)
                    sp.wait_ge(meta_stored, 16 * TOPK * NT * B)
                    sp.wait_ge(tab_ready, 1)
                if e > 0:
                    sp.wait_ge(experts_in, 16 * e)
                sp.dma_start(we[:, e * EXPERT:(e + 1) * EXPERT],
                             wsplit[e].rearrange("p c h n -> p (c h n)")).then_inc(experts_in, 16)
            sp.wait_ge(experts_in, 16 * E)

        def w_high(act, e, c, first=False):
            hold(act, w_in[c % 2], (e * 2 + c // 2 + 1) * 16)
            if not (first and c < 2):
                hold(act, w_out[c % 2], (e * 2 + c // 2) * 16)
            nc.scalar.activation(w_raw[c % 2], w_raw[c % 2], ACT.Copy, scale=R_SCALE).then_inc(w_scaled, 1)
            hold(act, w_scaled, e * 4 + c + 1)
            nc.scalar.activation(w_st[c % 2][:, 0, :], w_raw[c % 2], ACT.Copy).then_inc(w_hi, 1)

        def qk_read_half(act, b, half, n0=0, n1=4):
            for n in range(n0, n1):
                t = half * 4 + n
                side, m = n // 2, n % 2
                act.wait_ge(qk_filled, b * QK_USES + t + 1)
                held = half * 4 + (0, -2, -1, 1)[n]
                if held > 0:
                    act.wait_ge(qk_split, b * QK_USES + held)
                elif not isinstance(b, int) or b > 0:
                    act.wait_ge(qk_split, (b - 1) * QK_USES + QK_USES + held)
                nc.scalar.activation(q32[n % 3], big[n % BIG_BANKS][:, :], ACT.Identity, bias=bqk[:, side, m:m + 1],
                                     scale=1.0 / W_SCALE).then_inc(qk_read, 1)
                act.wait_ge(qk_read, b * QK_USES + t + 1)
                nc.scalar.activation(sq[:, side, m, :], q32[n % 3], ACT.Square).then_inc(qk_squared, 1)

        def k_relu(act, b, t):
            for m in range(KC):
                n = t * KC + m
                act.wait_ge(feat_filled, b * FEAT_USES + n + 1)
                if m == 0 and t >= 2:
                    act.wait_ge(kv_tile_done, b * NT + t - 1)
                nc.scalar.activation(rk[t % 2][:, m, :], big[n % BIG_BANKS][:, :], ACT.Relu).then_inc(feat_relu, 1)

        def q_relu(act, b, half):
            for p_ in range(PAIRS):
                n = 2 * NT + half * PAIRS + p_
                act.wait_ge(feat_filled, b * FEAT_USES + n + 1)
                nc.scalar.activation(rq[:, p_, 0, :], big[n % BIG_BANKS][:, :], ACT.Relu).then_inc(feat_relu, 1)

        def take(act, phase, part, name, b):
            act.wait_ge(filled[part], nth(part, name, b))
            return small_ap(phase, part, name, b)

        def xn_high(act, b, half, first=False):
            if not first:
                hold(act, xs_stored[half], b * 16)
            act.wait_ge(xn_ready, b * 2 + half + 1)
            nc.scalar.copy(xhl[half][:, :, 0, :], xn).then_inc(xn_split, 1)

        def xT_copy(act, phase, b, half):
            for j in range(2):
                src = f16(take(act, phase, "prep", f"xT{2 * half + j}", b)).rearrange("p (t c q) -> p c t q", t=2, c=4)
                dst = xT[half].rearrange("p c (t q) -> p c t q", q=P)[:, :, 2 * j:2 * j + 2, :]
                nc.scalar.copy(dst, src).then_inc(prep_taken, 1)

        def v_copy(act, phase, b, t):
            nc.scalar.copy(v32[:, t, :], take(act, phase, "prep", f"v{t}", b)[:, 0:D + E]).then_inc(prep_taken, 1)

        def squares_copy(act, phase, b, half):
            nc.scalar.copy(nT, take(act, phase, "prep", f"nrm{half}", b)[:, :]).then_inc(prep_taken, 1)

        def last_copies(act, phase, b):
            v_copy(act, phase, b, HT + 2)
            squares_copy(act, phase, b, 1)
            v_copy(act, phase, b, HT + 3)

        def o_hi(act, b, half):
            act.wait_ge(o_ready, b * 2 + half + 1)
            nc.scalar.copy(o_hl.rearrange("p t l (h d) -> p l t h d", h=H)[:, 0], nd[:, :, :, 0:HD]).then_inc(o_high, 1)

        def oT_copy(act, phase, b, half):
            for j in range(2):
                src = f16(take(act, phase, "attn", f"oT{2 * half + j}", b)).rearrange("p (t c q) -> p t c q", t=2, c=4)
                nc.scalar.copy(oT[:, 2 * j:2 * j + 2], src).then_inc(attn_taken, 1)

        def act_turn(act, b, phase, first=False):
            body = phase == "body"
            for t in range(2):
                k_relu(act, b, t)
            w_high(act, b, 0, first)
            for t in range(2, 4):
                k_relu(act, b, t)
            act.wait_ge(gate_in, b + 1)
            nc.scalar.activation(eg, dl, ACT.Exp, scale=1.0 / R_SCALE).then_inc(gate_exp, 1)
            for t in range(4, 6):
                k_relu(act, b, t)
            w_high(act, b, 1, first)
            for t in range(6, NT):
                k_relu(act, b, t)
            if body:
                xn_high(act, b + 1, 0)
            nc.scalar.copy(cs_b.rearrange("p h d -> p (h d)"), take(act, phase, "attn", "vsum", b)[:, 0:H * (HD + 1)]) \
                .then_inc(attn_taken, 1)
            q_relu(act, b, 0)
            if body:
                xT_copy(act, phase, b + 1, 0)
            nc.scalar.copy(cn_b.rearrange("p h d -> p (h d)"), take(act, phase, "attn", "cn", b)[:, 0:H * (HD + 1)]) \
                .then_inc(attn_taken, 1)
            if body:
                xn_high(act, b + 1, 1)
            w_high(act, b, 2)
            if not body:
                w_high(act, b, 3)
            act.wait_ge(attn_filled, nth("attn", f"ab{HT - 1}", b))
            q_relu(act, b, 1)
            if body:
                xT_copy(act, phase, b + 1, 1)
                qk_read_half(act, b + 1, 0, 0, 1)
            o_hi(act, b, 0)
            if body:
                qk_read_half(act, b + 1, 0, 1, 2)
            oT_copy(act, phase, b, 0)
            if body:
                qk_read_half(act, b + 1, 0, 2, 4)
                v_copy(act, phase, b + 1, 0)
                v_copy(act, phase, b + 1, 1)
                squares_copy(act, phase, b + 1, 0)
            if body:
                v_copy(act, phase, b + 1, 2)
            o_hi(act, b, 1)
            if body:
                v_copy(act, phase, b + 1, 3)
            if body:
                w_high(act, b, 3)
                qk_read_half(act, b + 1, 1, 0, 2)
            oT_copy(act, phase, b, 1)
            if body:
                v_copy(act, phase, b + 1, HT)
                v_copy(act, phase, b + 1, HT + 1)
                qk_read_half(act, b + 1, 1, 2, 4)
                last_copies(act, phase, b + 1)

        def silu(act, t, u, first):
            for j in range(4):
                act.wait_ge(mh_filled, t * 4 + j + 1)
                if not first:
                    act.wait_ge(mh_split, t * 4 + j - 3)
                nc.scalar.activation(h32[j].rearrange("p a b -> p (a b)"), big[j][:, :], ACT.Silu,
                                     scale=1.0 / R_SCALE).then_inc(mh_silu, 1)

        def y_scale(act, t, u, first):
            act.wait_ge(my_filled, t + 1)
            if not first:
                act.wait_ge(added, (t - 1) * 32)
            yb = bank[6 + u % 2]
            for a in range(2):
                nc.scalar.activation(y_sb[u % 2][:, a, :], yb[:, a * D:(a + 1) * D], ACT.Copy,
                                     scale=mt[:, u % GRP, a, 1:2].bitcast(F32)).then_inc(my_read, 1)

        @block.scalar
        def _(act):
            for half in range(2):
                xn_high(act, 0, half, first=True)
                if half == 0:
                    xT_copy(act, "first", 0, 0)
            act.wait_ge(w_ready, 1)
            qk_read_half(act, 0, 0, 0, 2)
            xT_copy(act, "first", 0, 1)
            qk_read_half(act, 0, 0, 2, 4)
            v_copy(act, "first", 0, 0)
            v_copy(act, "first", 0, 1)
            squares_copy(act, "first", 0, 0)
            v_copy(act, "first", 0, 2)
            v_copy(act, "first", 0, 3)
            qk_read_half(act, 0, 1)
            v_copy(act, "first", 0, HT)
            v_copy(act, "first", 0, HT + 1)
            last_copies(act, "first", 0)
            act_turn(act, 0, "body", first=True)
            with act.Fori(1, B - 1) as b:
                act_turn(act, b, "body")
            act_turn(act, B - 1, "tail")
            wait_read(act, "attn", "out3", B - 1)
            for n in range(2):
                act.wait_ge(out_stored[n], 16 * 2 * B)
                act.wait_ge(w_out[n], 16 * 2 * E)

            def group(g, first=False, last=False):
                for u in range(LASTG if last else GRP):
                    silu(act, g * GRP + u, u, first and u == 0)
                    if not (first and u == 0):
                        y_scale(act, g * GRP + u - 1, u - 1 + GRP, first and u <= 2)

            group(0, first=True)
            with act.Fori(1, NG - 1) as g:
                group(g)
            group(NG - 1, last=True)
            y_scale(act, MT - 1, LASTG - 1, False)

        def qk_project(pe, b, half, first):
            for n in range(4):
                t = half * 4 + n
                side, m = n // 2, n % 2
                if half == 1:
                    pe.wait_ge(qk_read, b * QK_USES + n + 1)
                elif not first:
                    pe.wait_ge(qf_split, (b - 1) * QF_USES + 12 + n + 1)
                if n == 0:
                    wait_read(pe, "prep", f"xT{2 * half + 1}", b)
                for i, (wl, xl) in enumerate(PASSES):
                    for k in range(KC):
                        c0 = side * D + m * P
                        mm = nc.tensor.matmul(big[n][:, :], w_hl[:, wl, k, c0:c0 + P], xT[half][:, xl * KC + k, :],
                                              start=(i == 0 and k == 0), stop=(i == 2 and k == KC - 1))
                mm.then_inc(qk_filled, 1)

        def x_transpose(pe, phase, b, half):
            pe.wait_ge(xl_split, b * 2 + half + 1)
            for j in range(2):
                dst = f16(small_ap(phase, "prep", f"xT{2 * half + j}", b, pe)).rearrange("p (t c q) -> p t c q", t=2, c=4)
                if j == 0:
                    pe.wait_ge(xn_split, b * 2 + half + 1)
                for tl in range(2):
                    for hl in range(2):
                        for k in range(KC):
                            mm = nc.tensor.transpose(dst[:, tl, hl * KC + k, :],
                                                     xhl[half][:, 2 * j + tl, hl, k * P:(k + 1) * P], ident16[:, :])
                mm.then_inc(prep_filled, 1)

        def v_project(pe, phase, b, t):
            half, tl = t // HT, t % HT
            dst = small_ap(phase, "prep", f"v{t}", b, pe)
            for i, (xl, wl) in enumerate(PASSES):
                for k in range(KC):
                    mm = nc.tensor.matmul(dst[:, 0:D + E], xT[half][:, xl * KC + k, tl * P:(tl + 1) * P],
                                          w_hl[:, wl, k, 2 * D:], start=(i == 0 and k == 0), stop=(i == 2 and k == KC - 1))
                    if i == 0 and k == 0:
                        nc.tensor.matmul(dst[:, 0:D], ones16[0:2, :], bv_two[:, :], start=False, stop=False)
            mm.then_inc(prep_filled, 1)

        def square_sums(pe, phase, b, half):
            dst = small_ap(phase, "prep", f"nrm{half}", b, pe)
            pe.wait_ge(qk_squared, b * QK_USES + half * 4 + 4)
            for g in range(4):
                mm = nc.tensor.matmul(dst[32 * g:32 * g + 32, :], hsel[:, :], sq[:, g // 2, g % 2, :], start=True, stop=True)
            mm.then_inc(prep_filled, 1)

        def square_turn(pe, phase, b, half):
            dst = small_ap(phase, "prep", f"nrmT{half}", b, pe)
            wait_read(pe, "prep", f"nrm{half}", b)
            for t in range(HT):
                mm = nc.tensor.transpose(dst[:, t * P:(t + 1) * P], nT[:, t * P:(t + 1) * P], ident32[:, :])
            mm.then_inc(prep_filled, 1)

        def k_features(pe, b, t):
            half, tl = t // HT, t % HT
            for m in range(KC):
                n = t * KC + m
                if n < BIG_BANKS:
                    pe.wait_ge(qk_read, b * QK_USES + 4 + n + 1)
                else:
                    pe.wait_ge(feat_relu, b * FEAT_USES + n - BIG_BANKS + 1)
                if n == 0 or n == 2 * HT:
                    pe.wait_ge(qk_split, b * QK_USES + half * 4 + 4)
                for i, (kl, pl) in enumerate(PASSES):
                    mm = nc.tensor.matmul(big[n % BIG_BANKS][:, :], k_hl[half][:, m, kl, tl * P:(tl + 1) * P],
                                          p_hl[:, pl, m, :], start=(i == 0), stop=(i == 2))
                mm.then_inc(feat_filled, 1)

        def kv_sum(pe, b, t):
            pe.wait_ge(feat_relu, b * FEAT_USES + t * KC + 2)
            if t % HT == 0:
                pe.wait_ge(vp_ready, b * 2 + t // HT + 1)
            for m in range(KC):
                for s in range(2):
                    for j in range(4):
                        h = 8 * m + 2 * j + s
                        c = 2 * m + s
                        mm = nc.tensor.matmul(kvbank[32 * j:32 * j + 32, c * F:(c + 1) * F], vp[:, t, h, :],
                                              rk[t % 2][:, m, (2 * j + s) * F:(2 * j + s + 1) * F],
                                              start=(t == 0 and c == 0), stop=(t == NT - 1), skip_group_check=True)
            mm.then_inc(kv_tile_done, 1)

        def q_features(pe, b, half, p0, p1):
            for p_ in range(p0, p1):
                n = 2 * NT + half * PAIRS + p_
                m, j = p_ // 4, p_ % 4
                if half == 0 and p_ < BIG_BANKS:
                    pe.wait_ge(feat_relu, b * FEAT_USES + n - BIG_BANKS + 1)
                else:
                    pe.wait_ge(qf_split, b * QF_USES + n - 2 * NT - BIG_BANKS + 1)
                for i, (pl, ql) in enumerate(PASSES):
                    mm = nc.tensor.matmul(big[n % BIG_BANKS][:, :], p_hl[:, pl, m, j * P:(j + 1) * P],
                                          q_hl[half][:, m, ql, :], start=(i == 0), stop=(i == 2))
                mm.then_inc(feat_filled, 1)

        def attend(pe, phase, b, t):
            half, tl = t // HT, t % HT
            dst = small_ap(phase, "attn", f"ab{t}", b, pe)
            if tl == 0:
                pe.wait_ge(qf_split, b * QF_USES + (half + 1) * PAIRS)
                pe.wait_ge(kv_split, b + 1)
            for p_ in range(PAIRS):
                for i, (rl, kl) in enumerate(PASSES):
                    mm = nc.tensor.matmul(dst[:, p_ * KVW:(p_ + 1) * KVW], rq[:, p_, rl, tl * P:(tl + 1) * P],
                                          kv_hl[:, kl, p_, :], start=(i == 0), stop=(i == 2))
            mm.then_inc(attn_filled, 1)

        def o_transpose(pe, phase, b, half):
            for j in range(2):
                dst = f16(small_ap(phase, "attn", f"oT{2 * half + j}", b, pe)).rearrange("p (t c q) -> p t c q", t=2, c=4)
                if j == 0:
                    pe.wait_ge(o_split, b * 2 + half + 1)
                for tl in range(2):
                    for hl in range(2):
                        for m in range(KC):
                            mm = nc.tensor.transpose(dst[:, tl, hl * KC + m, :],
                                                     o_hl[:, 2 * j + tl, hl, m * P:(m + 1) * P], ident16[:, :])
                mm.then_inc(attn_filled, 1)

        def o_project(pe, phase, b, half):
            for j in range(2):
                dst = small_ap(phase, "attn", f"out{2 * half + j}", b, pe)
                wait_read(pe, "attn", f"oT{2 * half + j}", b)
                for tl in range(2):
                    for i, (ol, wl) in enumerate(PASSES):
                        for m in range(KC):
                            mm = nc.tensor.matmul(dst[:, tl * D:(tl + 1) * D], oT[:, 2 * j + tl, ol * KC + m, :],
                                                  wo_hl[:, wl, m, :], start=(i == 0 and m == 0), stop=(i == 2 and m == KC - 1))
                mm.then_inc(attn_filled, 1)

        def count_ranks(pe, phase, b):
            dst = small_ap(phase, "attn", "rank", b, pe)
            pe.wait_ge(masks_ready, b + 1)
            m16f = m16.rearrange("p t e -> p (t e)")
            nc.tensor.matmul(dst[:, 0:(NT + 1) * E], tri[:, :], m16f, start=True, stop=False, skip_group_check=True)
            for s in range(1, NT + 1):
                mm = nc.tensor.matmul(dst[:, s * E:(NT + 1) * E], ones16[:, :], m16f[:, 0:(NT + 1 - s) * E],
                                      start=False, stop=(s == NT), skip_group_check=True)
            mm.then_inc(attn_filled, 1)

        def pe_turn(pe, b, phase):
            body = phase == "body"
            k_features(pe, b, 0)
            for t in range(1, NT):
                k_features(pe, b, t)
                kv_sum(pe, b, t - 1)
                if t == RANK_AT[phase]:
                    count_ranks(pe, phase, b)
            dst = small_ap(phase, "attn", "vsum", b, pe)
            pe.wait_ge(vsum_ready, b + 1)
            nc.tensor.matmul(dst[:, 0:H * (HD + 1)], cfeat[:, :], vsum.rearrange("p h d -> p (h d)"),
                             start=True, stop=True).then_inc(attn_filled, 1)
            kv_sum(pe, b, NT - 1)
            q_features(pe, b, 0, 0, 2)
            dst = small_ap(phase, "attn", "kvT", b, pe)
            pe.wait_ge(kvt_copied, b + 1)
            for m in range(KC):
                mm = nc.tensor.transpose(dst[:, m * P:(m + 1) * P], kvt[:, m * P:(m + 1) * P], ident32[:, :])
            mm.then_inc(attn_filled, 1)
            q_features(pe, b, 0, 2, PAIRS)
            if body:
                x_transpose(pe, phase, b + 1, 0)
            dst = small_ap(phase, "attn", "cn", b, pe)
            pe.wait_ge(kvf_ready, b + 1)
            nc.tensor.matmul(dst[:, 0:PAIRS * KVW], cfeat[:, :], kvf.rearrange("p a c -> p (a c)"),
                             start=True, stop=True).then_inc(attn_filled, 1)
            for t in range(HT - 1):
                attend(pe, phase, b, t)
            q_features(pe, b, 1, 0, 3)
            attend(pe, phase, b, HT - 1)
            q_features(pe, b, 1, 3, PAIRS)
            if body:
                x_transpose(pe, phase, b + 1, 1)
                qk_project(pe, b + 1, 0, False)
            o_transpose(pe, phase, b, 0)
            for t in range(HT, NT):
                attend(pe, phase, b, t)
            if body:
                v_and_squares(pe, phase, b + 1, 0)
            o_project(pe, phase, b, 0)
            if body:
                qk_project(pe, b + 1, 1, False)
            o_transpose(pe, phase, b, 1)
            if body:
                v_and_squares(pe, phase, b + 1, 1, attended=b)
            else:
                o_project(pe, phase, b, 1)

        def v_and_squares(pe, phase, b, half, attended=None):
            v_project(pe, phase, b, half * HT)
            v_project(pe, phase, b, half * HT + 1)
            if attended is not None:
                o_project(pe, phase, attended, 1)
            if half == 0:
                square_sums(pe, phase, b, half)
                v_project(pe, phase, b, 2)
                square_turn(pe, phase, b, half)
                v_project(pe, phase, b, 3)
            else:
                v_project(pe, phase, b, HT + 2)
                square_sums(pe, phase, b, half)
                v_project(pe, phase, b, HT + 3)
                square_turn(pe, phase, b, half)

        def rows_transpose(pe, g, u):
            dst = f16(bank[u % 2]).rearrange("p (c q) -> p c q", c=2 * KC)
            pe.wait_ge(rows_in[u % 2], (g * (GRP // 2) + u // 2 + 1) * 32)
            for a in range(2):
                for c in range(2 * KC):
                    mm = nc.tensor.transpose(dst[:, c, a * P:(a + 1) * P], xg[:, u % XR, a, c * P:(c + 1) * P], ident16[:, :])
            mm.then_inc(mx_filled, 1)

        def hidden(pe, t, u, first):
            e = pe.value_load(tab[0:1, 0, bass.ds(t, 1)], min_val=0, max_val=E - 1)
            hold(pe, experts_in, e * 16 + 16)
            pe.wait_ge(mx_read, t + 1)
            for j in range(4):
                if not first:
                    pe.wait_ge(mh_silu, t * 4 + j - 3)
                for i2 in range(2):
                    c = 2 * j + i2
                    for i, (wl, xl) in enumerate(PASSES):
                        for k in range(KC):
                            mm = nc.tensor.matmul(
                                big[j][:, i2 * TS:(i2 + 1) * TS],
                                we[:, bass.ds(e * EXPERT + (k * 2048 + wl * 1024 + c * P), P)],
                                moe_xT[u % 2][:, xl * KC + k, :], start=(i == 0 and k == 0), stop=(i == 2 and k == KC - 1))
                mm.then_inc(mh_filled, 1)

        def expert_out(pe, t, u, first):
            e = pe.value_load(tab[0:1, 0, bass.ds(t, 1)], min_val=0, max_val=E - 1)
            pe.wait_ge(mh_split, t * 4 + 4)
            if not first:
                pe.wait_ge(my_read, t * 2 - 2)
            yb = bank[6 + u % 2]
            for a in range(2):
                for c in range(FF // P):
                    for i, (hl, wl) in enumerate(PASSES):
                        off = (2 + c // 4) * 2048 + wl * 1024 + (c % 4) * D
                        mm = nc.tensor.matmul(yb[:, a * D:(a + 1) * D], hT[u % 2][:, c, hl, a * P:(a + 1) * P],
                                              we[:, bass.ds(e * EXPERT + off, D)],
                                              start=(c == 0 and i == 0), stop=(c == FF // P - 1 and i == 2))
            mm.then_inc(my_filled, 1)

        @block.tensor
        def _(pe):
            pe.wait_ge(pool_first, 19)
            x_transpose(pe, "first", 0, 0)
            pe.wait_ge(w_ready, 1)
            qk_project(pe, 0, 0, True)
            x_transpose(pe, "first", 0, 1)
            pe.wait_ge(bias_placed, 32)
            v_and_squares(pe, "first", 0, 0)
            qk_project(pe, 0, 1, True)
            v_and_squares(pe, "first", 0, 1)
            pe.wait_ge(consts_ready, 1)
            pe_turn(pe, 0, "body")
            with pe.Fori(1, B - 1) as b:
                pe_turn(pe, b, "body")
            pe_turn(pe, B - 1, "tail")
            wait_read(pe, "attn", "out3", B - 1)
            pe.wait_ge(tab_ready, 1)

            def group(g, first=False, last=False):
                for u in range(LASTG if last else GRP):
                    t = g * GRP + u
                    hidden(pe, t, u, first and u == 0)
                    if not (last and u == LASTG - 1):
                        rows_transpose(pe, g, u + 1)
                    if not (first and u == 0):
                        expert_out(pe, t - 1, u - 1 + GRP, first and u <= 2)

            rows_transpose(pe, 0, 0)
            group(0, first=True)
            with pe.Fori(1, NG - 1) as g:
                group(g)
            group(NG - 1, last=True)
            expert_out(pe, MT - 1, LASTG - 1, False)

        def w_low(pool, e, c):
            hold(pool, w_hi, e * 4 + c + 1)
            nc.gpsimd.tensor_tensor(w_st[c % 2][:, 1, :], w_raw[c % 2], w_st[c % 2][:, 0, :], ALU.subtract).then_inc(w_lo, 1)

        def x_low(pool, b, half):
            hold(pool, xn_split, b * 2 + half + 1)
            nc.gpsimd.tensor_tensor(xhl[half][:, :, 1, :], xn, xhl[half][:, :, 0, :], ALU.subtract).then_inc(xl_split, 1)
            nc.gpsimd.tensor_tensor(x_in[half], x_in[half], xn, ALU.add).then_inc(x_plus_xn, 1)

        def resid_sum(pool, b, half, first=False):
            if not first:
                wait_read(pool, "attn", f"out{2 * half + 1}", b - 1, hold)
            hold(pool, x_plus_xn, b * 2 + half + 1)
            nc.gpsimd.tensor_tensor(resid[:, half * HT:(half + 1) * HT, :], x_in[half],
                                    bo_b[:, :].rearrange("p (a d) -> p a d", a=1).broadcast_to([P, HT, D]),
                                    ALU.add).then_inc(resid_ready, 1)

        def v_total(pool, b):
            wait_read(pool, "prep", "v7", b, hold)
            nc.gpsimd.tensor_tensor(vtmp, v32[:, 0:4, 0:D], v32[:, 4:8, 0:D], ALU.add).then_inc(pool_prep, 1)
            hold(pool, pool_prep, b * 2 + 1)
            nc.gpsimd.tensor_tensor(vtmp[:, 0:2, :], vtmp[:, 0:2, :], vtmp[:, 2:4, :], ALU.add).then_inc(pool_prep, 1)
            hold(pool, pool_prep, b * 2 + 2)
            nc.gpsimd.tensor_tensor(vsum[:, :, 0:HD], vtmp[:, 0, :].rearrange("p (h d) -> p h d", h=H),
                                    vtmp[:, 1, :].rearrange("p (h d) -> p h d", h=H), ALU.add).then_inc(vsum_ready, 1)

        def norm_refine(pool, b, half):
            g = nc.gpsimd
            steps = [(b * 2 + half) * 13]

            def link(ins, apart=False):
                ins.then_inc(pool_norm, 1)
                steps[0] += 1
                if apart:
                    hold(pool, pool_norm, steps[0])
                else:
                    pool.wait_ge(pool_norm, steps[0])

            hold(pool, norm_guess, b * 2 + half + 1)
            for _ in range(3):
                link(g.tensor_tensor(nu, nsq, ny, ALU.mult))
                link(g.tensor_tensor(nu, nu, ny, ALU.mult), apart=True)
                link(g.tensor_scalar(nu, nu, -0.5, 1.5, ALU.mult, ALU.add))
                link(g.tensor_tensor(ny, ny, nu, ALU.mult))
            link(g.tensor_tensor(nu, nsq, ny, ALU.mult), apart=True)
            g.tensor_scalar(norm[:, half], nu, 1e-8, None, ALU.add).then_inc(norm_ready, 1)

        def scatter(pool, b):
            hold(pool, slots_ready, b + 1)
            for k in range(TOPK):
                for t in range(NT):
                    nc.gpsimd.indirect_dma_start(meta, bass.IndirectOffsetOnAxis(slot_i[:, k, t:t + 1], 0),
                                                 rec[:, k, t, :], None).then_inc(meta_stored, 16)

        def pool_turn(pool, b, phase):
            body = phase == "body"
            w_low(pool, b, 0)
            if body:
                x_low(pool, b + 1, 0)
            w_low(pool, b, 1)
            if body:
                x_low(pool, b + 1, 1)
            scatter(pool, b)
            if body:
                norm_refine(pool, b + 1, 0)
            w_low(pool, b, 2)
            if body:
                resid_sum(pool, b + 1, 0)
            if body:
                resid_sum(pool, b + 1, 1)
            w_low(pool, b, 3)
            if body:
                norm_refine(pool, b + 1, 1)
                v_total(pool, b + 1)

        @block.gpsimd
        def _(pool):
            g = nc.gpsimd
            ch = Chain(pool_first, 19)
            ch.start(pool, 0)
            ch.step(g.memset(clear, 0))
            ch.step(g.memset(zero_rows, 0.0))
            ch.wait()
            g.memset(clear.rearrange("p (a c) -> p a c", c=2)[:, :, 0:1], N).then_inc(slots_cleared, 1)
            ch.step(g.memset(ident16[:, :], 0.0))
            ch.step(g.memset(ident32[:, :], 0.0))
            ch.step(g.memset(tri[:, :], 1.0))
            ch.step(g.memset(ones16[:, :], 1.0))
            ch.step(g.memset(cfeat[:, :], EPSF))
            ch.step(g.memset(hsel[:, :], 1.0))
            ch.step(g.memset(vsum[:, :, HD:HD + 1], float(NT)))
            ch.wait()
            for m in (ident16, ident32):
                ch.step(g.affine_select(out=m[:, :], in_=m[:, :], compare_op=ALU.not_equal, fill=1.0, base=0,
                                        pattern=[[-1, P]], channel_multiplier=1))
            ch.step(g.affine_select(out=tri[:, :], in_=tri[:, :], compare_op=ALU.is_gt, fill=0.0, base=0,
                                    pattern=[[1, P]], channel_multiplier=-1))
            ch.link(g.affine_select(out=hsel[:, :], in_=hsel[:, :], compare_op=ALU.is_ge, fill=0.0, base=0,
                                    pattern=[[-HD, 32]], channel_multiplier=1))
            ch.link(g.affine_select(out=hsel[:, :], in_=hsel[:, :], compare_op=ALU.is_ge, fill=0.0, base=HD - 1,
                                    pattern=[[HD, 32]], channel_multiplier=-1))
            ch.step(g.iota(iota_i[:, :], pattern=[[1, 256]], base=0, channel_multiplier=0))
            ch.step(g.iota(tok_i, pattern=[[P, NT]], base=0, channel_multiplier=1))
            ch.step(g.iota(dump_i, pattern=[[1, TOPK], [P * TOPK, NT]], base=DUMP, channel_multiplier=TOPK))
            ch.step(g.memset(vp, 0.0))
            ch.link(g.memset(kvf, 0.0))
            assert ch.n == ch.per, ch.n
            for half in range(2):
                x_low(pool, 0, half)
            pool.wait_ge(w_ready, 1)
            for half in range(2):
                resid_sum(pool, 0, half, first=True)
            for half in range(2):
                norm_refine(pool, 0, half)
            v_total(pool, 0)
            pool.wait_ge(table_cleared, 16)
            pool_turn(pool, 0, "body")
            with pool.Fori(1, B - 1) as b:
                pool_turn(pool, b, "body")
            pool_turn(pool, B - 1, "tail")
            pool.wait_ge(tab_ready, 1)
            pool.wait_ge(meta_stored, 16 * TOPK * NT * B)
            pool.wait_ge(zero_stored, 16)
            for n in range(2):
                pool.wait_ge(xs_stored[n], 16 * B)
            last_row = pool.to_reg(N - 1)

            def meta_load(t, u):
                row = pool.value_load(tab[0:1, 1, bass.ds(t, 1)], min_val=0, max_val=TRASH)
                src = meta[bass.ds(row, TS), :].rearrange("(a p) c -> p a c", p=P)
                pool.dma_start(mt[:, u % GRP, :, :], src).then_inc(meta_in, 16)

            def gather(t, u):
                if not isinstance(t, int) or t >= 4:
                    hold(pool, meta_in, t * 16 + 16)
                for a in range(2):
                    nc.gpsimd.indirect_dma_start(xg[:, u % XR, a, :], None, xs,
                                                 bass.IndirectOffsetOnAxis(mt[:, u % GRP, a, 0:1], 0)).then_inc(rows_in[u % 2], 16)

            def add_out(t, u):
                hold(pool, my_read, t * 2 + 2)
                for a in range(2):
                    nc.gpsimd.indirect_dma_start(orows, bass.IndirectOffsetOnAxis(mt[:, u % GRP, a, 0:1], 0),
                                                 y_sb[u % 2][:, a, :], None, bounds_check=last_row, oob_is_err=False,
                                                 compute_op=ALU.add).then_inc(added, 16)

            def group(g, first=False, last=False):
                for u in range(LASTG if last else GRP):
                    t = g * GRP + u
                    if not (last and u >= LASTG - 3):
                        hold(pool, mx_filled, t + 2)
                        gather(t + 3, u + 3)
                    if not (first and u == 0):
                        hold(pool, added, t * 32)
                    if not (last and u >= LASTG - 4):
                        meta_load(t + 4, u + 4)
                    if first and u == 0:
                        for n in range(2):
                            pool.wait_ge(out_stored[n], 16 * 2 * B)
                    add_out(t, u)

            for t in range(4):
                meta_load(t, t)
            pool.wait_ge(meta_in, 16 * 4)
            gather(0, 0)
            gather(1, 1)
            pool.wait_ge(mx_filled, 1)
            gather(2, 2)
            group(0, first=True)
            with pool.Fori(1, NG - 1) as gg:
                group(gg)
            group(NG - 1, last=True)
            pool.wait_ge(added, 32 * MT)

        v = nc.vector

        def rsqrt_guess(ch, y, a, u, ready=None):
            ch.link(v.tensor_scalar(u.bitcast(I32), a.bitcast(I32), 1, None, ALU.arith_shift_right))
            ins = v.tensor_scalar(y.bitcast(I32), u.bitcast(I32), -1.0, MAGIC, ALU.mult, ALU.add)
            if ready is None:
                ch.link(ins)
            else:
                ins.then_inc(ready, 1)

        def rsqrt(ch, y, a, u):
            rsqrt_guess(ch, y, a, u)
            for _ in range(3):
                ch.link(v.tensor_tensor(u, a, y, ALU.mult))
                ch.link(v.scalar_tensor_tensor(u, u, -0.5, y, ALU.mult, ALU.mult))
                ch.link(v.scalar_tensor_tensor(y, u, 1.5, y, ALU.add, ALU.mult))

        chp, cha = Chain(dve_prep, 28 + 2 * (3 + 4 + 1) + 2), Chain(dve_attn, 18 + 2 + 16 + 1 + 2 * (4 + 2))

        def row_sums(dve, b):
            for half in range(2):
                hold(dve, x_loaded[half], (b + 1) * 16)
            for t in range(NT):
                chp.step(v.bn_stats(bn[:, t, :], x_in[t // HT][:, t % HT, :]))
            hold(dve, dve_prep, chp.base + chp.n)
            for t in range(NT):
                chp.step(v.bn_aggr(mv[:, t, :], bn[:, t, :]))

        def row_factors(dve):
            chp.wait()
            chp.link(v.tensor_scalar(va, mv[:, :, 1], 1e-5, None, ALU.add))
            rsqrt(chp, vy, va, vu)

        def normalise_rows(dve, b, half, first=False):
            if not (first and half == 0):
                dve.wait_ge(x_plus_xn, b * 2 + half)
            for t in range(HT):
                n = half * HT + t
                ins = v.tensor_scalar(xn[:, t, :], x_in[half][:, t, :], mv[:, n, 0:1], vy[:, n:n + 1],
                                      ALU.subtract, ALU.mult)
                if t < HT - 1:
                    chp.step(ins)
            ins.then_inc(xn_ready, 1)

        def drain(dve, phase, part, name, b):
            dve.wait_ge(filled[part], nth(part, name, b))
            return small_ap(phase, part, name, b)

        def qk_halves(dve, b, half, n0=0, n1=4):
            for n in range(n0, n1):
                side, m = n // 2, n % 2
                dst = (q_hl, k_hl)[side][half]
                dve.wait_ge(qk_read, b * QK_USES + half * 4 + n + 1)
                chp.link(v.tensor_copy(dst[:, m, 0, :], q32[n % 3]))
                v.tensor_tensor(dst[:, m, 1, :], q32[n % 3], dst[:, m, 0, :], ALU.subtract).then_inc(qk_split, 1)

        def norms(dve, phase, b, half):
            src = drain(dve, phase, "prep", f"nrmT{half}", b)[:, :].rearrange("p (t g c) -> p t g c", t=HT, g=4)
            v.tensor_copy(nsq, src[:, :, :, 0:8]).then_inc(prep_read, 1)
            wait_read(dve, "prep", f"nrmT{half}", b)
            rsqrt_guess(chp, ny, nsq, nu, ready=norm_guess)

        def v_over_norm(dve, b, half, ch):
            ts = slice(half * HT, (half + 1) * HT)
            wait_read(dve, "prep", f"v{half * 4 + 3}", b)
            dst = vp[:, ts]
            rnf = rn.rearrange("p t g e -> p t (g e)").unsqueeze(3)
            dve.wait_ge(norm_ready, b * 2 + half + 1)
            ch.link(v.reciprocal(rn, norm[:, half, :, 2:4, :]))
            ch.step(v.tensor_copy(dst[:, :, :, HD:HD + 1], rnf))
            v.tensor_tensor(dst[:, :, :, 0:HD], v32[:, ts, 0:D].rearrange("p t (h d) -> p t h d", d=HD),
                            rnf.broadcast_to([P, HT, H, HD]), ALU.mult).then_inc(vp_ready, 1)

        def choose(dve, b):
            wait_read(dve, "prep", "v7", b, hold)
            lg = v32[:, :, D:]
            for t in range(NT):
                cha.step(v.max(mx[:, t, :], lg[:, t, :]))
            cha.wait()
            v.tensor_tensor(dl, mx[:, :, 1], mx[:, :, 0], ALU.subtract).then_inc(gate_in, 1)
            for t in range(NT):
                cha.step(v.max_index(mi[:, t, :], mx[:, t, :], lg[:, t, :]))
            cha.wait()
            cha.link(v.tensor_copy(ix, mi[:, :, 0:TOPK].rearrange("p t k -> p k t")))
            cha.link(v.tensor_tensor(oh.rearrange("p k t e -> p (k t) e"),
                                     ix.rearrange("p k t -> p (k t)").unsqueeze(2).broadcast_to([P, TOPK * NT, E]),
                                     iota_e[:, :].unsqueeze(1).broadcast_to([P, TOPK * NT, E]), ALU.is_equal))
            v.tensor_tensor(m16[:, 0:NT, :], oh[:, 0], oh[:, 1], ALU.add).then_inc(masks_ready, 1)

        def place(dve, phase, b, first):
            src = drain(dve, phase, "attn", "rank", b)
            cha.step(v.tensor_tensor(rank, src[:, 0:NT * E].rearrange("p (t e) -> p t e", e=E),
                                     carry[:, :].unsqueeze(1).broadcast_to([P, NT, E]), ALU.add))
            cha.wait()
            v.tensor_tensor(carry[:, :], src[:, NT * E:(NT + 1) * E], carry[:, :], ALU.add).then_inc(attn_read, 1)
            cha.link(v.tensor_tensor(rsel, oh, rank.unsqueeze(1).broadcast_to([P, TOPK, NT, E]), ALU.mult))
            cha.link(v.tensor_reduce(rpos, rsel, AX.X, ALU.add))
            cha.step(v.tensor_scalar(keep, rpos, float(CAP), None, ALU.is_lt))
            cha.link(v.scalar_tensor_tensor(slot, ix, float(RROWS), rpos, ALU.mult, ALU.add))
            cha.link(v.tensor_tensor(slot, slot, dump_f[:, :, :], ALU.subtract))
            cha.link(v.tensor_tensor(slot, slot, keep, ALU.mult))
            cha.link(v.tensor_tensor(slot, slot, dump_f[:, :, :], ALU.add))
            dve.wait_ge(gate_exp, b + 1)
            cha.link(v.tensor_scalar(gate[:, 1, :], eg, 1.0, None, ALU.add))
            cha.link(v.reciprocal(gate[:, 0, :], gate[:, 1, :]))
            cha.link(v.tensor_scalar(gate[:, 0, :], gate[:, 0, :], 1.0 / (H_SCALE * R_SCALE), None, ALU.mult))
            cha.link(v.tensor_tensor(gate[:, 1, :], gate[:, 0, :], eg, ALU.mult))
            if not first:
                dve.wait_ge(meta_stored, b * 16 * TOPK * NT)
            cha.step(v.tensor_copy(rec[:, :, :, 0], tok_f[:, :].unsqueeze(1).broadcast_to([P, TOPK, NT])))
            cha.step(v.tensor_copy(rec[:, :, :, 1].bitcast(F32), gate))
            cha.link(v.tensor_copy(slot_i, slot))
            cha.step(v.tensor_scalar(tok_f[:, :], tok_f[:, :], float(S), None, ALU.add))
            v.tensor_scalar(dump_f[:, :, :], dump_f[:, :, :], float(S * TOPK), None, ALU.add).then_inc(slots_ready, 1)

        def kv_build(dve, phase, b):
            src = drain(dve, phase, "attn", "kvT", b)[:, 0:256].rearrange("p (a c) -> p a c", c=32)
            wait_read(dve, "attn", "vsum", b)
            csv = cs_b.rearrange("p (a s) d -> p a s d", s=2)
            rows_ = [slice(s * 64, s * 64 + 64) for s in range(2)]
            cha.step(v.tensor_tensor(kvf[rows_[0], :, 0:HD + 1], src[rows_[0], :, 0:HD + 1], csv[rows_[0], :, 0, :], ALU.add))
            v.tensor_tensor(kvf[rows_[1], :, HD + 1:], src[rows_[1], :, 0:HD + 1], csv[rows_[1], :, 1, :], ALU.add) \
                .then_inc(attn_read, 1)
            wait_read(dve, "attn", "kvT", b)
            v.tensor_copy(kv_hl[:, 0], kvf).then_inc(kvf_ready, 1)
            dve.wait_ge(kvf_ready, b + 1)
            v.tensor_tensor(kv_hl[:, 1], kvf, kv_hl[:, 0], ALU.subtract).then_inc(kv_split, 1)

        def q_low(dve, b, half, p0, p1):
            for p_ in range(p0, p1):
                n = 2 * NT + half * PAIRS + p_
                dve.wait_ge(feat_relu, b * FEAT_USES + n + 1)
                v.scalar_tensor_tensor(rq[:, p_, 1, :], big[n % BIG_BANKS][:, :], 0.0, rq[:, p_, 0, :],
                                       ALU.max, ALU.subtract).then_inc(qf_split, 1)

        def constant_part(dve, b, half):
            if half == 0:
                wait_read(dve, "attn", "cn", b)
            else:
                dve.wait_ge(o_split, b * 2 + 1)
            for t in range(HT):
                ins = v.tensor_tensor(nd[:, t], norm[:, half, t, 0:2, :].rearrange("p g e -> p (g e)").unsqueeze(2)
                                      .broadcast_to([P, H, HD + 1]), cn_b, ALU.mult)
                cha.step(ins)
            cha.wait()

        def attend_drain(dve, phase, b, t):
            src = drain(dve, phase, "attn", f"ab{t}", b)[:, 0:H * (HD + 1)].rearrange("p (h d) -> p h d", h=H)
            v.tensor_tensor(nd[:, t % HT], src, nd[:, t % HT], ALU.add).then_inc(attn_read, 1)

        def normalise(dve, b, half):
            wait_read(dve, "attn", f"ab{half * 4 + 3}", b)
            nq = norm[:, half, :, 0:2, :].rearrange("p t g e -> p t (g e)")
            cha.link(v.scalar_tensor_tensor(dn, nq, 1e-6 * P_SCALE * P_SCALE, nd[:, :, :, HD], ALU.mult, ALU.max))
            cha.link(v.reciprocal(dn, dn))
            ndv = nd.rearrange("p t h d -> p (t h) d")[:, :, 0:HD]
            v.tensor_tensor(ndv, ndv, dn.rearrange("p t h -> p (t h)").unsqueeze(2).broadcast_to([P, HT * H, HD]),
                            ALU.mult).then_inc(o_ready, 1)

        def o_low(dve, b, half):
            dve.wait_ge(o_high, b * 2 + half + 1)
            ohv = o_hl.rearrange("p t l (h d) -> p l t h d", h=H)
            v.tensor_tensor(ohv[:, 1], nd[:, :, :, 0:HD], ohv[:, 0], ALU.subtract).then_inc(o_split, 1)

        def out_drain(dve, phase, b, half, first):
            for j in range(2):
                k = 2 * half + j
                src = drain(dve, phase, "attn", f"out{k}", b)[:, :].rearrange("p (t d) -> p t d", t=2)
                if half == 1:
                    dve.wait_ge(out_stored[k % 2], b * 32 + 16)
                elif not first:
                    dve.wait_ge(out_stored[k % 2], b * 32)
                dve.wait_ge(resid_ready, b * 2 + half + 1)
                v.scalar_tensor_tensor(osb[k % 2], src, 1.0 / (R_SCALE * W_SCALE), resid[:, 2 * k:2 * k + 2, :], ALU.mult, ALU.add) \
                    .then_inc(attn_read, 1)

        def dve_turn(dve, b, phase, first=False):
            body = phase == "body"
            cha.start(dve, b)
            choose(dve, b)
            if body:
                chp.start(dve, b + 1)
                row_sums(dve, b + 1)
            if not body:
                place(dve, phase, b, first)
            v_over_norm(dve, b, 1, cha)
            if body:
                row_factors(dve)
                normalise_rows(dve, b + 1, 0)
            if body:
                place(dve, phase, b, first)
            else:
                tile_table(dve)
            dve.wait_ge(kv_tile_done, (b + 1) * NT)
            v.tensor_copy(kvt, kvbank[:, 0:256]).then_inc(kvt_copied, 1)
            q_low(dve, b, 0, 0, 2)
            kv_build(dve, phase, b)
            q_low(dve, b, 0, 2, PAIRS)
            if body:
                normalise_rows(dve, b + 1, 1)
            constant_part(dve, b, 0)
            for t in range(HT):
                attend_drain(dve, phase, b, t)
            q_low(dve, b, 1, 0, PAIRS)
            normalise(dve, b, 0)
            if body:
                qk_halves(dve, b + 1, 0, 0, 1)
            o_low(dve, b, 0)
            constant_part(dve, b, 1)
            for t in range(HT, NT):
                attend_drain(dve, phase, b, t)
            if body:
                qk_halves(dve, b + 1, 0, 1, 4)
            normalise(dve, b, 1)
            if body:
                norms(dve, phase, b + 1, 0)
            o_low(dve, b, 1)
            out_drain(dve, phase, b, 0, first)
            if body:
                qk_halves(dve, b + 1, 1, 0, 2)
                v_over_norm(dve, b + 1, 0, chp)
                qk_halves(dve, b + 1, 1, 2, 3)
            out_drain(dve, phase, b, 1, first)
            if body:
                qk_halves(dve, b + 1, 1, 3, 4)
                norms(dve, phase, b + 1, 1)
                chp.end()
            cha.end()

        def tile_table(dve):
            K = RROWS // TS
            ch = Chain(dve_table, 0)
            ch.start(dve, 0)
            at = [0]

            def take(*shape):
                n = 1
                for k in shape:
                    n *= k
                a = tb[0:1, at[0]:at[0] + n]
                at[0] += n
                if len(shape) == 2:
                    a = a.rearrange("p (a b) -> p a b", a=shape[0])
                return a

            iota_f, cnt, over = take(256), take(E), take(E, K)
            tiles, upto, used = take(E), take(E, E), take(E)
            past, pt, ex, ue = take(MT, E), take(MT, E), take(MT), take(MT)
            dve.wait_ge(vsum_ready, B)
            dve.wait_ge(vp_ready, 2 * B)
            ch.link(v.tensor_copy(iota_f, iota_i[0:1, :]))
            ch.link(v.tensor_scalar(cnt, carry[0:1, :], float(CAP), None, ALU.min))
            ch.link(v.tensor_scalar(ue[:, 0:K], iota_f[:, 0:K], float(TS), None, ALU.mult))
            ch.link(v.tensor_tensor(over, cnt.unsqueeze(2).broadcast_to([1, E, K]),
                                    ue[:, 0:K].unsqueeze(1).broadcast_to([1, E, K]), ALU.is_gt))
            ch.link(v.tensor_reduce(tiles, over, AX.X, ALU.add))
            ch.link(v.tensor_tensor(upto, iota_f[:, 0:E].unsqueeze(1).broadcast_to([1, E, E]),
                                    iota_f[:, 0:E].unsqueeze(2).broadcast_to([1, E, E]), ALU.is_le))
            ch.link(v.tensor_tensor(upto, upto, tiles.unsqueeze(1).broadcast_to([1, E, E]), ALU.mult))
            ch.link(v.tensor_reduce(used, upto, AX.X, ALU.add))
            ch.link(v.tensor_tensor(past, iota_f[:, 0:MT].unsqueeze(2).broadcast_to([1, MT, E]),
                                    used.unsqueeze(1).broadcast_to([1, MT, E]), ALU.is_ge))
            ch.link(v.tensor_reduce(ex, past, AX.X, ALU.add))
            ch.link(v.tensor_tensor(pt, past, tiles.unsqueeze(1).broadcast_to([1, MT, E]), ALU.mult))
            ch.link(v.tensor_reduce(ue, pt, AX.X, ALU.add))
            ch.link(v.tensor_tensor(ue, iota_f[:, 0:MT], ue, ALU.subtract))
            ch.link(v.tensor_scalar(ue, ue, float(TS), None, ALU.mult))
            ch.link(v.scalar_tensor_tensor(ue, ex, float(RROWS), ue, ALU.mult, ALU.add))
            ch.link(v.tensor_scalar(tab[:, 1, :], ue, float(TRASH), None, ALU.min))
            v.tensor_scalar(tab[:, 0, :], ex, float(E - 1), None, ALU.min).then_inc(tab_ready, 1)

        def rows_copy(dve, t, u):
            dve.wait_ge(mx_filled, t + 1)
            v.tensor_copy(moe_xT[u % 2].rearrange("p c q -> p (c q)"), f16(bank[u % 2])).then_inc(mx_read, 1)

        def hidden_split(dve, t, u):
            for j in range(4):
                dve.wait_ge(mh_silu, t * 4 + j + 1)
                v.tensor_scalar(hT[u % 2][:, 2 * j:2 * j + 2, 0, :], h32[j], H_SCALE, None, ALU.mult).then_inc(mh_step, 1)
                dve.wait_ge(mh_step, t * 4 + j + 1)
                v.scalar_tensor_tensor(hT[u % 2][:, 2 * j:2 * j + 2, 1, :], h32[j], H_SCALE, hT[u % 2][:, 2 * j:2 * j + 2, 0, :],
                                       ALU.mult, ALU.subtract).then_inc(mh_split, 1)

        @block.vector
        def _(dve):
            ch = Chain(dve_first, 0)
            ch.start(dve, 0)
            v.memset(raw_p, 0.0).then_inc(proj_zeroed, 1)
            ch.step(v.memset(carry[:, :], 0.0))
            ch.step(v.memset(m16[:, NT, :], 0.0))
            chp.start(dve, 0)
            row_sums(dve, 0)
            row_factors(dve)
            normalise_rows(dve, 0, 0, first=True)
            dve.wait_ge(weights_loaded, 16 * 9)
            ch.link(v.tensor_scalar(bv_hl[:, 0, :], bv_row, W_SCALE, None, ALU.mult))
            v.scalar_tensor_tensor(bv_hl[:, 1, :], bv_row, W_SCALE, bv_hl[:, 0, :], ALU.mult, ALU.subtract).then_inc(bias_split, 1)
            columns = (slice(0, 3 * D), W_SCALE), (slice(3 * D, WCOLS), R_SCALE)
            for c, scale in columns:
                ch.link(v.tensor_scalar(w_hl[:, 0, :, c], raw_w[:, :, c], scale, None, ALU.mult))
            for n, (c, scale) in enumerate(columns):
                ins = v.scalar_tensor_tensor(w_hl[:, 1, :, c], raw_w[:, :, c], scale, w_hl[:, 0, :, c], ALU.mult, ALU.subtract)
                if n == 0:
                    ch.step(ins)
            ins.then_inc(w_ready, 1)
            dve.wait_ge(pool_first, 19)
            ch.step(v.tensor_copy(iota_e[:, :], iota_i[:, 0:E]))
            ch.step(v.tensor_copy(tok_f[:, :], tok_i))
            ch.step(v.tensor_copy(dump_f[:, :, :], dump_i))
            normalise_rows(dve, 0, 1, first=True)
            dve.wait_ge(proj_loaded, 16 * H // KC)
            scaled = ((p_hl[:, :, :, :], raw_p, P_SCALE), (wo_hl[:, :, :, :], raw_o, R_SCALE))
            for dst, src, scale in scaled:
                ch.step(v.tensor_scalar(dst[:, 0], src, scale, None, ALU.mult))
            ch.wait()
            dve.wait_ge(table_cleared, 16)
            dve.wait_ge(zero_stored, 16)
            for n, (dst, src, scale) in enumerate(scaled):
                ins = v.scalar_tensor_tensor(dst[:, 1], src, scale, dst[:, 0], ALU.mult, ALU.subtract)
                if n == 0:
                    ch.step(ins)
            ins.then_inc(consts_ready, 1)

            for half in range(2):
                qk_halves(dve, 0, half)
                if half == 1:
                    v_over_norm(dve, 0, 0, chp)
                norms(dve, "first", 0, half)
            chp.end()
            dve_turn(dve, 0, "body", first=True)
            with dve.Fori(1, B - 1) as b:
                dve_turn(dve, b, "body")
            dve_turn(dve, B - 1, "tail")
            wait_read(dve, "attn", "out3", B - 1)

            def group(g, last=False):
                for u in range(LASTG if last else GRP):
                    t = g * GRP + u
                    hidden_split(dve, t, u)
                    if not (last and u == LASTG - 1):
                        rows_copy(dve, t + 1, u + 1)

            rows_copy(dve, 0, 0)
            for n in range(2):
                dve.wait_ge(out_stored[n], 16 * 2 * B)
                dve.wait_ge(w_out[n], 16 * 2 * E)
            with dve.Fori(0, NG - 1) as g:
                group(g)
            group(NG - 1, last=True)


def kernel(**inputs):
    import numpy as _np
    import concourse.bacc as _bacc
    from concourse import mybir as _mybir
    from concourse.bass_utils import run_bass_kernel_spmd as _run

    layout = {
        "x": inputs["L0_attn_x"], "Wq": inputs["L0_attn_Wq"], "bq": inputs["L0_attn_bq"], "Wk": inputs["L0_attn_Wk"],
        "bk": inputs["L0_attn_bk"], "Wv": inputs["L0_attn_Wv"], "bv": inputs["L0_attn_bv"], "Wo": inputs["L0_attn_Wo"],
        "bo": inputs["L0_attn_bo"], "proj_t": _np.transpose(_np.asarray(inputs["L0_attn_projection"]), (0, 2, 1)),
        "router_t": _np.transpose(_np.asarray(inputs["L0_ffn_router_w"]), (1, 0)), "w1": inputs["L0_ffn_w1"],
        "w2": inputs["L0_ffn_w2"],
    }
    nc = _bacc.Bacc("TRN2", target_bir_lowering=False, num_devices=1)
    arrays, args = {}, []
    for name, value in layout.items():
        a = _np.ascontiguousarray(value)
        arrays[f"in_{name}_dram"] = a
        args.append(nc.dram_tensor(f"in_{name}_dram", a.shape, _mybir.dt.from_np(a.dtype), kind="ExternalInput").ap())
    args.append(nc.dram_tensor("out_0_dram", (B, S, D), _mybir.dt.float32, kind="ExternalOutput").ap())
    moe_attention(nc, *args)
    r = _run(nc, [arrays], core_ids=[0])
    return r.results[0]["out_0_dram"]
```
